# Optimizing a Trainium2 kernel written in Bass

```python
import numpy as np
import jax
import jax.numpy as jnp

def _softmax(x, axis=-1):
    return jax.nn.softmax(x, axis=axis)

def _gelu(x):
    return jax.nn.gelu(x, approximate=True)

def _silu(x):
    return jax.nn.silu(x)

def _sigmoid(x):
    return jax.nn.sigmoid(x)

def _layernorm(x, axis=-1, eps=1e-05):
    m = jnp.mean(x, axis=axis, keepdims=True)
    v = jnp.var(x, axis=axis, keepdims=True)
    return (x - m) / jnp.sqrt(v + eps)

def _scatter_add(tgt, idx, src, axis=0):
    return tgt.at[idx].add(src)

def _segment_sum(src, seg, n):
    return jax.ops.segment_sum(src, seg, n)
kernel_name = 'mk_vit_tower_d2_tok_img1024_r4_0c822b'

def setup_inputs(seed: int=0):
    np.random.seed(seed)
    _w = jnp.asarray

    def _rec_inputs():
        import jax
        import jax.numpy as jnp
        _rk = jax.random.key(seed)
        x = -0.00016672 + 0.999947 * jax.random.normal(jax.random.fold_in(_rk, 1), (32, 3, 96, 96), jnp.float32)
        return x
    x = _rec_inputs()

    def _L0_tok_setup():
        import jax, jax.numpy as jnp
        import numpy as np
        PATCH = 16
        EPS = 1e-05

        def _patchify(x, p):
            B, C, H, W = x.shape
            hp, wp = (H // p, W // p)
            x = x.reshape(B, C, hp, p, wp, p)
            x = x.transpose(0, 2, 4, 1, 3, 5)
            return x.reshape(B, hp * wp, C * p * p)
        key = jax.random.key(seed)
        ks = jax.random.split(key, 6)
        B, C, H = (64, 3, 96)
        E = 256
        P = PATCH
        N = (H // P) ** 2
        D = C * P * P
        x = jax.random.normal(ks[0], (B, C, H, H), dtype=jnp.float32)
        W = jax.random.normal(ks[1], (D, E), dtype=jnp.float32) * (1.0 / np.sqrt(D))
        b = jnp.zeros((E,), dtype=jnp.float32)
        cls_token = jax.random.normal(ks[2], (1, 1, E), dtype=jnp.float32) * 0.02
        pos_embedding = jax.random.normal(ks[3], (1, N + 1, E), dtype=jnp.float32) * 0.02
        gamma = jnp.ones((E,), dtype=jnp.float32)
        beta = jnp.zeros((E,), dtype=jnp.float32)
        return {'x': x, 'W': W, 'b': b, 'cls_token': cls_token, 'pos_embedding': pos_embedding, 'gamma': gamma, 'beta': beta}
    _L0_tok_all = _L0_tok_setup()
    _L0_tok_in = {k: v for k, v in _L0_tok_all.items() if k in ('W', 'b', 'cls_token', 'pos_embedding', 'gamma', 'beta')}
    del _L0_tok_all

    def _L0_attn_setup():
        import jax, jax.numpy as jnp
        import numpy as np
        B, T, C, HS = (4, 512, 256, 16)
        H = C // HS
        LAYER_ID, N_LAYER = (2, 24)
        D_MIX, D_DECAY = (32, 64)
        LN_EPS = 1e-05

        def _wkv6(r, k, v, w, u):
            wd = jnp.exp(-jnp.exp(w))
            rT, kT, vT, wT = (a.transpose(1, 0, 2, 3) for a in (r, k, v, wd))

            def step(S, ins):
                r_t, k_t, v_t, w_t = ins
                kv = jnp.einsum('bhi,bhj->bhij', k_t, v_t)
                y_t = jnp.einsum('bhi,bhij->bhj', r_t, S + u[None, :, :, None] * kv)
                return (w_t[..., None] * S + kv, y_t)
            S0 = jnp.zeros((r.shape[0], H, HS, HS), r.dtype)
            _, ys = jax.lax.scan(step, S0, (rT, kT, vT, wT))
            return ys.transpose(1, 0, 2, 3)
        key = jax.random.key(seed)
        ks = jax.random.split(key, 8)
        r01 = LAYER_ID / (N_LAYER - 1)
        r10 = 1.0 - LAYER_ID / N_LAYER
        ddd = np.arange(C, dtype=np.float64) / C
        tm = lambda p: (1.0 - ddd ** p).reshape(1, 1, C).astype(np.float32)
        time_maa_x = tm(r10)
        time_maa_w = tm(r10)
        time_maa_k = tm(r10)
        time_maa_v = (1.0 - (ddd ** r10 + 0.3 * r01)).reshape(1, 1, C).astype(np.float32)
        time_maa_r = tm(0.5 * r10)
        n = np.arange(C, dtype=np.float64)
        decay = (-6.0 + 5.0 * (n / (C - 1)) ** (0.7 + 1.3 * r01)).reshape(1, 1, C).astype(np.float32)
        zig = ((n + 1) % 3 - 1) * 0.1
        faaaa = (r01 * (1.0 - n / (C - 1)) + zig).reshape(H, HS).astype(np.float32)
        u01 = lambda k, s: jax.random.uniform(k, s, jnp.float32, -0.01, 0.01)
        return {'x': jax.random.normal(ks[0], (B, T, C), jnp.float32), 'time_maa_x': jnp.asarray(time_maa_x), 'time_maa_w': jnp.asarray(time_maa_w), 'time_maa_k': jnp.asarray(time_maa_k), 'time_maa_v': jnp.asarray(time_maa_v), 'time_maa_r': jnp.asarray(time_maa_r), 'time_maa_w1': u01(ks[1], (C, D_MIX * 4)), 'time_maa_w2': u01(ks[2], (4, D_MIX, C)), 'time_decay': jnp.asarray(decay), 'time_decay_w1': u01(ks[3], (C, D_DECAY)), 'time_decay_w2': u01(ks[4], (D_DECAY, C)), 'time_faaaa': jnp.asarray(faaaa), 'W_r': jax.random.normal(ks[5], (C, C), jnp.float32) * 0.02, 'W_k': jax.random.normal(ks[6], (C, C), jnp.float32) * 0.02, 'W_v': jax.random.normal(ks[7], (C, C), jnp.float32) * 0.02, 'W_o': jax.random.normal(jax.random.fold_in(key, 99), (C, C), jnp.float32) * 0.02, 'ln_g': jnp.ones((C,), jnp.float32), 'ln_b': jnp.zeros((C,), jnp.float32)}
    _L0_attn_all = _L0_attn_setup()
    _L0_attn_in = {k: v for k, v in _L0_attn_all.items() if k in ('time_maa_x', 'time_maa_w', 'time_maa_k', 'time_maa_v', 'time_maa_r', 'time_maa_w1', 'time_maa_w2', 'time_decay', 'time_decay_w1', 'time_decay_w2', 'time_faaaa', 'W_r', 'W_k', 'W_v', 'W_o', 'ln_g', 'ln_b')}
    del _L0_attn_all

    def _L0_ffn_setup():
        import jax, jax.numpy as jnp
        import numpy as np
        B, S, D, F_DIM, E, TOPK = (2, 256, 256, 1024, 8, 2)
        key = jax.random.key(seed)
        k0, k1, k2, k3 = jax.random.split(key, 4)
        hidden_states = jax.random.normal(k0, (B, S, D), dtype=jnp.float32)
        router_w = jax.random.normal(k1, (E, D), dtype=jnp.float32) * 0.02
        w1 = jax.random.normal(k2, (E, F_DIM, D), dtype=jnp.float32) * 0.02
        w2 = jax.random.normal(k3, (E, D, F_DIM), dtype=jnp.float32) * 0.02
        expert_scale = jnp.ones((E,), dtype=jnp.float32)
        return {'hidden_states': hidden_states, 'router_w': router_w, 'w1': w1, 'w2': w2, 'expert_scale': expert_scale}
    _L0_ffn_all = _L0_ffn_setup()
    _L0_ffn_in = {k: v for k, v in _L0_ffn_all.items() if k in ('router_w', 'w1', 'w2', 'expert_scale')}
    del _L0_ffn_all

    def _L1_attn_setup():
        import jax, jax.numpy as jnp
        import numpy as np
        import math
        H = 8
        D = 32
        DEPTH = 1
        LAMBDA_INIT = 0.8 - 0.6 * math.exp(-0.3 * DEPTH)
        EPS = 1e-08
        key = jax.random.key(seed)
        ks = jax.random.split(key, 9)
        B, T, IN_DIM, OUT_DIM = (2, 512, 256, 256)
        E = 2 * H * D
        inp = {'x': jax.random.normal(ks[0], (B, T, IN_DIM), dtype=jnp.float32), 'Wq': jax.random.normal(ks[1], (IN_DIM, E), dtype=jnp.float32) * IN_DIM ** (-0.5), 'Wkv': jax.random.normal(ks[2], (IN_DIM, 2 * E), dtype=jnp.float32) * IN_DIM ** (-0.5), 'Wout': jax.random.normal(ks[3], (E, OUT_DIM), dtype=jnp.float32) * E ** (-0.5), 'lambda_q1': 0.1 * jax.random.normal(ks[4], (D,), dtype=jnp.float32), 'lambda_k1': 0.1 * jax.random.normal(ks[5], (D,), dtype=jnp.float32), 'lambda_q2': 0.1 * jax.random.normal(ks[6], (D,), dtype=jnp.float32), 'lambda_k2': 0.1 * jax.random.normal(ks[7], (D,), dtype=jnp.float32), 'gamma': jnp.ones((2 * D,), dtype=jnp.float32)}
        return inp
    _L1_attn_all = _L1_attn_setup()
    _L1_attn_in = {k: v for k, v in _L1_attn_all.items() if k in ('Wq', 'Wkv', 'Wout', 'lambda_q1', 'lambda_k1', 'lambda_q2', 'lambda_k2', 'gamma')}
    del _L1_attn_all

    def _L1_ffn_setup():
        import jax, jax.numpy as jnp
        import numpy as np
        H = 256
        E = 32
        I = 128
        TOP_K = 6
        IS = 256
        NORM_MIN = 1e-12
        B, S = (2, 256)
        key = jax.random.key(seed)
        ks = jax.random.split(key, 8)
        sc = 0.02
        return {'hidden_states': jax.random.normal(ks[0], (B, S, H), jnp.float32), 'router_weight': jax.random.normal(ks[1], (E, H), jnp.float32) * sc, 'e_score_bias': jnp.zeros((E,), jnp.float32), 'gate_up_proj': jax.random.normal(ks[2], (E, 2 * I, H), jnp.float32) * sc, 'down_proj': jax.random.normal(ks[3], (E, H, I), jnp.float32) * sc, 'shared_gate_w': jax.random.normal(ks[4], (IS, H), jnp.float32) * sc, 'shared_up_w': jax.random.normal(ks[5], (IS, H), jnp.float32) * sc, 'shared_down_w': jax.random.normal(ks[6], (H, IS), jnp.float32) * sc}
    _L1_ffn_all = _L1_ffn_setup()
    _L1_ffn_in = {k: v for k, v in _L1_ffn_all.items() if k in ('router_weight', 'e_score_bias', 'gate_up_proj', 'down_proj', 'shared_gate_w', 'shared_up_w', 'shared_down_w')}
    del _L1_ffn_all
    return {'x': x, 'L0_tok_W': _L0_tok_in['W'], 'L0_tok_b': _L0_tok_in['b'], 'L0_tok_cls_token': _L0_tok_in['cls_token'], 'L0_tok_pos_embedding': _L0_tok_in['pos_embedding'], 'L0_tok_gamma': _L0_tok_in['gamma'], 'L0_tok_beta': _L0_tok_in['beta'], 'L0_attn_time_maa_x': _L0_attn_in['time_maa_x'], 'L0_attn_time_maa_w': _L0_attn_in['time_maa_w'], 'L0_attn_time_maa_k': _L0_attn_in['time_maa_k'], 'L0_attn_time_maa_v': _L0_attn_in['time_maa_v'], 'L0_attn_time_maa_r': _L0_attn_in['time_maa_r'], 'L0_attn_time_maa_w1': _L0_attn_in['time_maa_w1'], 'L0_attn_time_maa_w2': _L0_attn_in['time_maa_w2'], 'L0_attn_time_decay': _L0_attn_in['time_decay'], 'L0_attn_time_decay_w1': _L0_attn_in['time_decay_w1'], 'L0_attn_time_decay_w2': _L0_attn_in['time_decay_w2'], 'L0_attn_time_faaaa': _L0_attn_in['time_faaaa'], 'L0_attn_W_r': _L0_attn_in['W_r'], 'L0_attn_W_k': _L0_attn_in['W_k'], 'L0_attn_W_v': _L0_attn_in['W_v'], 'L0_attn_W_o': _L0_attn_in['W_o'], 'L0_attn_ln_g': _L0_attn_in['ln_g'], 'L0_attn_ln_b': _L0_attn_in['ln_b'], 'L0_ffn_router_w': _L0_ffn_in['router_w'], 'L0_ffn_w1': _L0_ffn_in['w1'], 'L0_ffn_w2': _L0_ffn_in['w2'], 'L0_ffn_expert_scale': _L0_ffn_in['expert_scale'], 'L1_attn_Wq': _L1_attn_in['Wq'], 'L1_attn_Wkv': _L1_attn_in['Wkv'], 'L1_attn_Wout': _L1_attn_in['Wout'], 'L1_attn_lambda_q1': _L1_attn_in['lambda_q1'], 'L1_attn_lambda_k1': _L1_attn_in['lambda_k1'], 'L1_attn_lambda_q2': _L1_attn_in['lambda_q2'], 'L1_attn_lambda_k2': _L1_attn_in['lambda_k2'], 'L1_attn_gamma': _L1_attn_in['gamma'], 'L1_ffn_router_weight': _L1_ffn_in['router_weight'], 'L1_ffn_e_score_bias': _L1_ffn_in['e_score_bias'], 'L1_ffn_gate_up_proj': _L1_ffn_in['gate_up_proj'], 'L1_ffn_down_proj': _L1_ffn_in['down_proj'], 'L1_ffn_shared_gate_w': _L1_ffn_in['shared_gate_w'], 'L1_ffn_shared_up_w': _L1_ffn_in['shared_up_w'], 'L1_ffn_shared_down_w': _L1_ffn_in['shared_down_w']}

def reference(x, L0_tok_W, L0_tok_b, L0_tok_cls_token, L0_tok_pos_embedding, L0_tok_gamma, L0_tok_beta, L0_attn_time_maa_x, L0_attn_time_maa_w, L0_attn_time_maa_k, L0_attn_time_maa_v, L0_attn_time_maa_r, L0_attn_time_maa_w1, L0_attn_time_maa_w2, L0_attn_time_decay, L0_attn_time_decay_w1, L0_attn_time_decay_w2, L0_attn_time_faaaa, L0_attn_W_r, L0_attn_W_k, L0_attn_W_v, L0_attn_W_o, L0_attn_ln_g, L0_attn_ln_b, L0_ffn_router_w, L0_ffn_w1, L0_ffn_w2, L0_ffn_expert_scale, L1_attn_Wq, L1_attn_Wkv, L1_attn_Wout, L1_attn_lambda_q1, L1_attn_lambda_k1, L1_attn_lambda_q2, L1_attn_lambda_k2, L1_attn_gamma, L1_ffn_router_weight, L1_ffn_e_score_bias, L1_ffn_gate_up_proj, L1_ffn_down_proj, L1_ffn_shared_gate_w, L1_ffn_shared_up_w, L1_ffn_shared_down_w):
    import jax
    import jax.numpy as jnp

    def _L0_tok_ref(x, W, b, cls_token, pos_embedding, gamma, beta):
        import jax, jax.numpy as jnp
        import numpy as np
        PATCH = 16
        EPS = 1e-05

        def _patchify(x, p):
            B, C, H, W = x.shape
            hp, wp = (H // p, W // p)
            x = x.reshape(B, C, hp, p, wp, p)
            x = x.transpose(0, 2, 4, 1, 3, 5)
            return x.reshape(B, hp * wp, C * p * p)
        B = x.shape[0]
        patches = _patchify(x, PATCH)
        tok = jnp.einsum('bnd,de->bne', patches, W) + b
        cls = jnp.broadcast_to(cls_token, (B, 1, tok.shape[-1]))
        h = jnp.concatenate([cls, tok], axis=1) + pos_embedding
        mu = jnp.mean(h, axis=-1, keepdims=True)
        var = jnp.mean(jnp.square(h - mu), axis=-1, keepdims=True)
        out = (h - mu) * jax.lax.rsqrt(var + EPS) * gamma + beta
        return out

    def _L0_attn_ref(x, time_maa_x, time_maa_w, time_maa_k, time_maa_v, time_maa_r, time_maa_w1, time_maa_w2, time_decay, time_decay_w1, time_decay_w2, time_faaaa, W_r, W_k, W_v, W_o, ln_g, ln_b):
        import jax, jax.numpy as jnp
        import numpy as np
        B, T, C, HS = (4, 512, 256, 16)
        H = C // HS
        LAYER_ID, N_LAYER = (2, 24)
        D_MIX, D_DECAY = (32, 64)
        LN_EPS = 1e-05

        def _wkv6(r, k, v, w, u):
            wd = jnp.exp(-jnp.exp(w))
            rT, kT, vT, wT = (a.transpose(1, 0, 2, 3) for a in (r, k, v, wd))

            def step(S, ins):
                r_t, k_t, v_t, w_t = ins
                kv = jnp.einsum('bhi,bhj->bhij', k_t, v_t)
                y_t = jnp.einsum('bhi,bhij->bhj', r_t, S + u[None, :, :, None] * kv)
                return (w_t[..., None] * S + kv, y_t)
            S0 = jnp.zeros((r.shape[0], H, HS, HS), r.dtype)
            _, ys = jax.lax.scan(step, S0, (rT, kT, vT, wT))
            return ys.transpose(1, 0, 2, 3)
        b, t, c = x.shape
        xx = jnp.concatenate([jnp.zeros_like(x[:, :1]), x[:, :-1]], axis=1) - x
        xxx = x + xx * time_maa_x
        m = jnp.tanh(xxx @ time_maa_w1).reshape(b, t, 4, D_MIX)
        m = jnp.einsum('btfd,fdc->fbtc', m, time_maa_w2)
        mw, mk, mv, mr = (m[0], m[1], m[2], m[3])
        xw = x + xx * (time_maa_w + mw)
        xk = x + xx * (time_maa_k + mk)
        xv = x + xx * (time_maa_v + mv)
        xr = x + xx * (time_maa_r + mr)
        r = (xr @ W_r).reshape(b, t, H, HS)
        k = (xk @ W_k).reshape(b, t, H, HS)
        v = (xv @ W_v).reshape(b, t, H, HS)
        ww = jnp.tanh(xw @ time_decay_w1) @ time_decay_w2
        w = (time_decay + ww).reshape(b, t, H, HS)
        y = _wkv6(r, k, v, w, time_faaaa).reshape(b, t, c)
        mu = jnp.mean(y, axis=-1, keepdims=True)
        var = jnp.mean(jnp.square(y - mu), axis=-1, keepdims=True)
        y = (y - mu) * jax.lax.rsqrt(var + LN_EPS) * ln_g + ln_b
        return y @ W_o

    def _L0_ffn_ref(hidden_states, router_w, w1, w2, expert_scale):
        import jax, jax.numpy as jnp
        import numpy as np
        B, S, D, F_DIM, E, TOPK = (2, 256, 256, 1024, 8, 2)
        b, s, d = hidden_states.shape
        xf = hidden_states.reshape(-1, d)
        logits = xf @ router_w.T
        probs = jax.nn.softmax(logits, axis=-1)
        top_w, top_idx = jax.lax.top_k(probs, TOPK)
        top_w = jax.nn.softmax(top_w, axis=-1)
        combine = jnp.sum(jax.nn.one_hot(top_idx, E, dtype=xf.dtype) * top_w[..., None], axis=1)
        h = jax.nn.silu(jnp.einsum('td,efd->tef', xf, w1))
        y = jnp.einsum('tef,edf->ted', h, w2)
        y = y * expert_scale[None, :, None]
        out = jnp.einsum('te,ted->td', combine, y)
        return out.reshape(b, s, d)

    def _L1_attn_ref(x, Wq, Wkv, Wout, lambda_q1, lambda_k1, lambda_q2, lambda_k2, gamma):
        import jax, jax.numpy as jnp
        import numpy as np
        import math
        H = 8
        D = 32
        DEPTH = 1
        LAMBDA_INIT = 0.8 - 0.6 * math.exp(-0.3 * DEPTH)
        EPS = 1e-08
        B, T, _ = x.shape
        scaling = D ** (-0.5)
        q = (x @ Wq).reshape(B, T, 2 * H, D).transpose(0, 2, 1, 3) * scaling
        kv = x @ Wkv
        k, v = jnp.split(kv, 2, axis=-1)
        k = k.reshape(B, T, 2 * H, D).transpose(0, 2, 1, 3)
        v = v.reshape(B, T, H, 2 * D).transpose(0, 2, 1, 3)
        dots = jnp.einsum('bhqd,bhkd->bhqk', q, k)
        attn_w = jax.nn.softmax(dots.astype(jnp.float32), axis=-1).astype(dots.dtype)
        lam1 = jnp.exp(jnp.sum(lambda_q1 * lambda_k1))
        lam2 = jnp.exp(jnp.sum(lambda_q2 * lambda_k2))
        lam = lam1 - lam2 + LAMBDA_INIT
        attn_w = attn_w.reshape(B, H, 2, T, T)
        attn_w = attn_w[:, :, 0] - lam * attn_w[:, :, 1]
        attn = jnp.einsum('bhqk,bhkd->bhqd', attn_w, v)
        rms = jnp.sqrt(jnp.mean(attn * attn, axis=-1, keepdims=True))
        attn = gamma * (attn / (rms + EPS))
        attn = attn * (1.0 - LAMBDA_INIT)
        attn = attn.transpose(0, 2, 1, 3).reshape(B, T, 2 * H * D)
        return attn @ Wout

    def _L1_ffn_ref(hidden_states, router_weight, e_score_bias, gate_up_proj, down_proj, shared_gate_w, shared_up_w, shared_down_w):
        import jax, jax.numpy as jnp
        import numpy as np
        H = 256
        E = 32
        I = 128
        TOP_K = 6
        IS = 256
        NORM_MIN = 1e-12
        B, S = (2, 256)
        b, s, h = hidden_states.shape
        x = hidden_states.reshape(-1, h)
        T = x.shape[0]
        shared_out = jax.nn.silu(x @ shared_gate_w.T) * (x @ shared_up_w.T) @ shared_down_w.T
        xf = x.astype(jnp.float32)
        router_logits = xf @ router_weight.T
        routing_weights = jax.nn.softmax(router_logits, axis=-1)
        corrected = routing_weights + e_score_bias
        _, top_idx = jax.lax.top_k(corrected, TOP_K)
        top_w = jnp.take_along_axis(routing_weights, top_idx, axis=-1)
        top_w = top_w / jnp.clip(top_w.sum(axis=-1, keepdims=True), NORM_MIN)
        top_w = top_w.astype(x.dtype)
        combine = jnp.zeros((T, E), x.dtype).at[jnp.arange(T)[:, None], top_idx].add(top_w)
        gu = jnp.einsum('th,eih->tei', x, gate_up_proj)
        gate, up = jnp.split(gu, 2, axis=-1)
        hmid = jax.nn.silu(gate) * up
        y = jnp.einsum('tei,ehi->teh', hmid, down_proj)
        out = jnp.einsum('teh,te->th', y, combine) + shared_out
        return out.reshape(b, s, h)
    h = _L0_tok_ref(x, L0_tok_W, L0_tok_b, L0_tok_cls_token, L0_tok_pos_embedding, L0_tok_gamma, L0_tok_beta)
    h = h + _L0_attn_ref(_layernorm(h, axis=-1), L0_attn_time_maa_x, L0_attn_time_maa_w, L0_attn_time_maa_k, L0_attn_time_maa_v, L0_attn_time_maa_r, L0_attn_time_maa_w1, L0_attn_time_maa_w2, L0_attn_time_decay, L0_attn_time_decay_w1, L0_attn_time_decay_w2, L0_attn_time_faaaa, L0_attn_W_r, L0_attn_W_k, L0_attn_W_v, L0_attn_W_o, L0_attn_ln_g, L0_attn_ln_b)
    h = h + _L0_ffn_ref(_layernorm(h, axis=-1), L0_ffn_router_w, L0_ffn_w1, L0_ffn_w2, L0_ffn_expert_scale)
    h = h + _L1_attn_ref(_layernorm(h, axis=-1), L1_attn_Wq, L1_attn_Wkv, L1_attn_Wout, L1_attn_lambda_q1, L1_attn_lambda_k1, L1_attn_lambda_q2, L1_attn_lambda_k2, L1_attn_gamma)
    h = h + _L1_ffn_ref(_layernorm(h, axis=-1), L1_ffn_router_weight, L1_ffn_e_score_bias, L1_ffn_gate_up_proj, L1_ffn_down_proj, L1_ffn_shared_gate_w, L1_ffn_shared_up_w, L1_ffn_shared_down_w)
    return h

_drawn_inputs = setup_inputs


def setup_inputs(seed=0):
    import zlib

    import numpy as np

    out = dict(_drawn_inputs(seed))
    spreads = {'L0_tok_b': (0.0, 0.1),
     'L0_tok_gamma': (1.0, 0.2),
     'L0_tok_beta': (0.0, 0.1),
     'L0_attn_ln_g': (1.0, 0.2),
     'L0_attn_ln_b': (0.0, 0.1),
     'L0_ffn_expert_scale': (1.0, 0.6),
     'L1_attn_gamma': (1.0, 0.2),
     'L1_ffn_e_score_bias': (0.0, 0.8)}
    factors = {'L0_attn_time_maa_x': 8.0,
     'L0_attn_time_maa_w': 8.0,
     'L0_attn_time_maa_w1': 8.0,
     'L0_attn_time_maa_w2': 8.0,
     'L0_attn_time_decay_w1': 8.0,
     'L0_attn_time_decay_w2': 8.0,
     'L1_attn_lambda_q2': 4.682,
     'L1_attn_lambda_k2': 4.481,
     'L1_ffn_router_weight': 8.0,
     'L1_ffn_gate_up_proj': 8.0,
     'L1_ffn_down_proj': 8.0,
     'L1_ffn_shared_gate_w': 4.304,
     'L1_ffn_shared_up_w': 4.265,
     'L1_ffn_shared_down_w': 4.259}
    for name, (base, spread) in spreads.items():
        noise = np.random.default_rng([zlib.crc32(name.encode()), seed]).standard_normal(out[name].shape)
        drawn = base * np.exp(spread * noise) if base else spread * noise
        out[name] = jnp.asarray(drawn.astype(out[name].dtype))
    for name, factor in factors.items():
        out[name] = (out[name] * factor).astype(out[name].dtype)
    return out
```

```python
import concourse.bass as bass
from concourse import mybir
from contextlib import ExitStack

F32 = mybir.dt.float32
F32R = mybir.dt.float32r
BF16 = mybir.dt.bfloat16
ALU = mybir.AluOpType
ACT = mybir.ActivationFunctionType
AX = mybir.AxisListType

P = 128
IMAGES, SEQ, C = 32, 37, 256
PATCHES = SEQ - 1
TOK = IMAGES * SEQ
KH = C // P
CH_IMAGES = 8
CH = CH_IMAGES * SEQ
CHUNKS = IMAGES // CH_IMAGES
STREAMS = 2
PATCH_D = 768
PB = PATCH_D // P
HS = 16
LN_EPS = 1e-5
GT = 74
TILES = STREAMS * CH // GT
EROWS = 34
HEADS, HD = 8, 32
LAMBDA_INIT = 0.8 - 0.6 * 2.718281828459045 ** -0.3
PAIRS = CH_IMAGES // 2
QP = 64
PAD_LOW, PICKED = -3.0e38, -3.2e38

VEC = {name: i for i, name in enumerate(
    ["tok_b", "cls", "tok_gamma", "tok_beta", "maa_x", "maa_w", "maa_k", "maa_v", "maa_r",
     "decay", "faaaa", "ln_g", "ln_b"])}


class Shared:
    pass


class Norm:

    def __init__(self, sem, name):
        self.mean_ready, self.centred, self.squared = sem(f"{name}_mean"), sem(f"{name}_centred"), sem(f"{name}_squared")
        self.var_ready, self.std_ready = sem(f"{name}_var"), sem(f"{name}_std")
        self.rstd_ready, self.normed = sem(f"{name}_rstd"), sem(f"{name}_normed")


class Routing:

    def __init__(self, sb, sem, E):
        self.m, self.a, self.e = sb("m", [GT, TILES]), sb("a", [GT, TILES, E]), sb("e", [GT, TILES, E])
        self.p, self.q = sb("p", [GT, TILES, E + 8]), sb("q", [GT, TILES, E + 8])
        self.top, self.take = sb("top", [GT, TILES, 8]), sb("take", [GT, TILES, 8])
        self.rest, self.picked = sb("rest", [GT, TILES, E + 8]), sb("picked", [GT, TILES, E])
        self.parts = sb("parts", [GT, TILES, 3 * EROWS], BF16)
        self.step, self.parts_ready = sem("step"), sem("parts_ready")


class Link:

    def __init__(self, eng, sem, it=0, per=0):
        self.eng, self.sem, self.base, self.n, self.per = eng, sem, it * per, 0, per

    def __call__(self, ins):
        self.n += 1
        ins.then_inc(self.sem, 1)
        self.eng.wait_ge(self.sem, self.base + self.n)

    def close(self):
        assert not self.per or self.n == self.per, (self.n, self.per)


def wait_alone(c, eng, sem, value):
    eng.wait_ge(sem, value)
    eng.sem_inc(c.passed, 1)


def over_halves(ap, k=KH):
    return ap.unsqueeze(1).to_broadcast([ap.shape[0], k, ap.shape[1]])



def norm_mean_pe(pe, c, nm, s, halves):
    for k in range(KH):
        last = pe.matmul(c.stat[s], c.mean_w[:, :], halves[k], start=(k == 0), stop=(k == KH - 1))
    last.then_inc(nm.mean_ready, 1)


def norm_var_pe(pe, c, nm, s, n):
    pe.wait_ge(nm.squared, n)
    for k in range(KH):
        last = pe.matmul(c.stat[s], c.mean_w[:, :], c.sq[s][:, k, :], start=(k == 0), stop=(k == KH - 1))
    last.then_inc(nm.var_ready, 1)


def norm_centre_dve(dve, c, nm, s, n, src):
    dve.wait_ge(nm.mean_ready, n)
    dve.tensor_tensor(c.xc[s][:, :, :], src, over_halves(c.stat[s]), ALU.subtract).then_inc(nm.centred, 1)


def norm_square_act(act, c, nm, s, n):
    act.wait_ge(nm.centred, n)
    act.activation(c.sq[s][:, :, :], c.xc[s][:, :, :], ACT.Square).then_inc(nm.squared, 1)


def norm_std_act(act, c, nm, s, n):
    act.wait_ge(nm.var_ready, n)
    act.activation(c.std[s][:, :], c.stat[s], ACT.Sqrt, bias=c.eps[:, :]).then_inc(nm.std_ready, 1)


def norm_scale_dve(dve, c, nm, s, n, out):
    dve.wait_ge(nm.std_ready, n)
    dve.reciprocal(c.rstd[s][:, :], c.std[s][:, :]).then_inc(nm.rstd_ready, 1)
    dve.wait_ge(nm.rstd_ready, n)
    dve.tensor_tensor(out, c.xc[s][:, :, :], over_halves(c.rstd[s][:, :]), ALU.mult).then_inc(nm.normed, 1)


def setup_stream_buffers(ctx, nc, c, tag):
    sb = lambda name, shape, dt=F32: ctx.enter_context(nc.sbuf_tensor(f"{tag}_{name}", shape, dt))
    c.xc = [sb(f"xc{s}", [P, KH, CH]) for s in range(STREAMS)]
    c.sq = [sb(f"sq{s}", [P, KH, CH]) for s in range(STREAMS)]
    c.std = [sb(f"std{s}", [P, CH]) for s in range(STREAMS)]
    c.rstd = [sb(f"rstd{s}", [P, CH]) for s in range(STREAMS)]
    c.pA = [ctx.enter_context(nc.psum_tensor(f"{tag}_pA{s}", [P, 2, 512], F32)) for s in range(STREAMS)]
    c.pB = [ctx.enter_context(nc.psum_tensor(f"{tag}_pB{s}", [P, 2, 512], F32)) for s in range(STREAMS)]
    c.stat = [c.pB[s][:, 0, 0:CH] for s in range(STREAMS)]



def phase_tokens(nc, c):
    with ExitStack() as ctx:
        sb = lambda name, shape, dt=F32: ctx.enter_context(nc.sbuf_tensor(name, shape, dt))
        setup_stream_buffers(ctx, nc, c, "tk")
        S2 = range(STREAMS)
        wtok = sb("wtok", [P, PB, C])
        pos = sb("pos", [P, KH, SEQ])
        patches = [sb(f"patches{s}", [P, PB, CH_IMAGES * PATCHES]) for s in S2]
        h0 = [sb(f"h0_{s}", [P, KH, CH]) for s in S2]
        xn = [sb(f"xn{s}", [P, KH, CH]) for s in S2]
        xx = [sb(f"xx{s}", [P, KH, CH]) for s in S2]
        mixed = [sb(f"mixed{s}", [P, KH, CH]) for s in S2]
        xf = [sb(f"xf{s}", [P, KH, CH]) for s in S2]
        tanh_m = [sb(f"tanh_m{s}", [P, CH]) for s in S2]
        tanh_d = [sb(f"tanh_d{s}", [64, CH]) for s in S2]
        vf = [sb(f"vf{s}", [P, KH, CH]) for s in S2]
        w_lora = sb("w_lora", [P, KH, P])
        w_lora2 = sb("w_lora2", [P, C])
        w_rkv = sb("w_rkv", [P, 3, KH, C])
        w_decay = sb("w_decay", [P, KH, 64])
        w_decay2 = sb("w_decay2", [64, C])
        head_ones = sb("head_ones", [P, P])
        sem = c.sem
        first_loaded, consts_loaded = sem("tok_w_loaded"), sem("mix_w_loaded")
        x_loaded = [sem(f"x_loaded{s}") for s in S2]
        tok_mm, tokens_ready, pos_ready, h_ready = sem("tok_mm"), sem("tokens_ready"), sem("pos_ready"), sem("h_ready")
        n0, n1 = c.norm("tok_norm"), c.norm("rwkv_norm")
        shifted, xxx_ready = sem("shifted"), sem("xxx_ready")
        lora_ready, tanh_ready = sem("lora_ready"), sem("tanh_ready")
        mix_ready, mix_applied, xf_ready, proj_ready, evacuated = (
            sem("mix_ready"), sem("mix_applied"), sem("xf_ready"), sem("proj_ready"), sem("evacuated"))
        decay1_ready, decay_tanh, decay_exp, decay_done = sem("decay1_ready"), sem("decay_tanh"), sem("decay_exp"), sem("decay_done")
        v_hi_done, v_lo_done = sem("v_hi_done"), sem("v_lo_done")
        ruk_ready, bonus_mm, bonus_done = sem("ruk_ready"), sem("bonus_mm"), sem("bonus_done")
        start_ready = sem("start_ready")
        d = c.dram
        MIX = [("maa_w", 0), ("maa_k", 1), ("maa_v", 2), ("maa_r", 3)]
        RKV = {"maa_r": 0, "maa_k": 1, "maa_v": 2}

        with nc.Block() as block:
            @block.sync
            def _(sp):
                sp.dma_start(wtok[:, :, :], d["wtok"]).then_inc(first_loaded, 16)
                for s in S2:
                    sp.dma_start(patches[s][:, :, :], d["patches"][s]).then_inc(x_loaded[s], 16)
                for dst, src in ((c.vec[:, :], d["vec"]), (pos[:, :, :], d["pos"]),
                                 (c.mean_w[:, :], d["mean_w"]), (w_lora[:, :, :], d["w_lora"]),
                                 (w_lora2[:, :], d["w_lora2"]), (w_rkv[:, :, :, :], d["w_rkv"]),
                                 (w_decay[:, :, :], d["w_decay"]), (w_decay2[:, :], d["w_decay2"]),
                                 (head_ones[:, :], d["head_ones"])):
                    sp.dma_start(dst, src).then_inc(consts_loaded, 16)
                for s in S2:
                    sp.wait_ge(tok_mm, s + 1)
                    sp.dma_start(patches[s][:, :, :], d["patches"][STREAMS + s]).then_inc(x_loaded[s], 16)
                sp.dma_start(c.w_o[:, :, :], d["w_o"]).then_inc(c.late_loaded, 16)
                sp.dma_start(c.router0[:, :, :], d["router0"]).then_inc(c.late_loaded, 16)
                sp.dma_start(c.escale[:, :], d["escale"].partition_broadcast(GT)).then_inc(c.late_loaded, 16)
                sp.dma_start(c.red[:, :, :], d["red"]).then_inc(c.scan_tables_loaded, 16)
                sp.dma_start(c.sel_f[:, :, :], d["sel"]).then_inc(c.scan_tables_loaded, 16)
            CONSTS = 9 * 16

            @block.tensor
            def _(pe):
                pe.wait_ge(first_loaded, 16)
                with pe.Fori(0, CHUNKS // STREAMS) as it:
                    n = [it * STREAMS + s + 1 for s in S2]
                    for s in S2:
                        pe.wait_ge(bonus_done, n[s])
                        pe.wait_ge(x_loaded[s], it * 16 + 16)
                        for m in range(KH):
                            for k in range(PB):
                                last = pe.matmul(c.pA[s][:, m, 0:CH_IMAGES * PATCHES], wtok[:, k, m * P:(m + 1) * P],
                                                 patches[s][:, k, :], start=(k == 0), stop=(k == PB - 1))
                        last.then_inc(tok_mm, 1)
                    pe.wait_ge(consts_loaded, CONSTS)
                    for s in S2:
                        pe.wait_ge(tokens_ready, n[s])
                        norm_mean_pe(pe, c, n0, s, [h0[s][:, k, :] for k in range(KH)])
                    for s in S2:
                        norm_var_pe(pe, c, n0, s, n[s])
                    for s in S2:
                        pe.wait_ge(h_ready, n[s])
                        at = it * (STREAMS * CH) + s * CH
                        norm_mean_pe(pe, c, n1, s, [c.h[:, k, bass.ds(at, CH)] for k in range(KH)])
                    for s in S2:
                        norm_var_pe(pe, c, n1, s, n[s])
                    for s in S2:
                        pe.wait_ge(xxx_ready, n[s])
                        for k in range(KH):
                            last = pe.matmul(c.pB[s][:, 0, 0:CH], w_lora[:, k, :], xf[s][:, k, :],
                                             start=(k == 0), stop=(k == KH - 1))
                        last.then_inc(lora_ready, 1)
                    for f, (name, row) in enumerate(MIX):
                        for s in S2:
                            if f == 0:
                                pe.wait_ge(tanh_ready, n[s])
                            else:
                                pe.wait_ge(mix_applied, it * 8 + 2 * (f - 1) + s + 1)
                            for m in range(KH):
                                last = pe.matmul(c.pA[s][:, m, 0:CH], w_lora2[32 * row:32 * row + 32, m * P:(m + 1) * P],
                                                 tanh_m[s][32 * row:32 * row + 32, :], start=True, stop=True)
                            last.then_inc(mix_ready, 1)
                        for s in S2:
                            pe.wait_ge(xf_ready, it * 8 + 2 * f + s + 1)
                            if f:
                                pe.wait_ge(evacuated, it * 8 + 2 * (f - 1) + s + 1)
                            if name == "maa_w":
                                for k in range(KH):
                                    last = pe.matmul(c.pB[s][0:64, 0, 0:CH], w_decay[:, k, :], xf[s][:, k, :],
                                                     start=(k == 0), stop=(k == KH - 1))
                                last.then_inc(decay1_ready, 1)
                            else:
                                for m in range(KH):
                                    for k in range(KH):
                                        last = pe.matmul(c.pB[s][:, m, 0:CH], w_rkv[:, RKV[name], k, m * P:(m + 1) * P],
                                                         xf[s][:, k, :], start=(k == 0), stop=(k == KH - 1))
                                last.then_inc(proj_ready, 1)
                        if name == "maa_w":
                            for s in S2:
                                pe.wait_ge(decay_tanh, n[s])
                                for m in range(KH):
                                    last = pe.matmul(c.pB[s][:, m, 0:CH], w_decay2[:, m * P:(m + 1) * P],
                                                     tanh_d[s][:, :], start=True, stop=True)
                                last.then_inc(proj_ready, 1)
                    for s in S2:
                        pe.wait_ge(ruk_ready, n[s])
                        for m in range(KH):
                            last = pe.matmul(c.pA[s][:, m, 0:CH], head_ones[:, :], mixed[s][:, m, :], start=True, stop=True)
                        last.then_inc(bonus_mm, 1)

            @block.vector
            def _(dve):
                dve.memset(c.eps[:, :], LN_EPS).then_inc(start_ready, 1)
                dve.sem_inc(bonus_done, STREAMS)
                dve.wait_ge(consts_loaded, CONSTS)
                for k in range(KH):
                    dve.tensor_scalar(pos[:, k, 1:SEQ], pos[:, k, 1:SEQ], c.vcol("tok_b", k), None, ALU.add).then_inc(pos_ready, 1)
                    dve.tensor_scalar(pos[:, k, 0:1], pos[:, k, 0:1], c.vcol("cls", k), None, ALU.add).then_inc(pos_ready, 1)
                dve.wait_ge(pos_ready, 2 * KH)
                with dve.Fori(0, CHUNKS // STREAMS) as it:
                    n = [it * STREAMS + s + 1 for s in S2]
                    at = [it * (STREAMS * CH) + s * CH for s in S2]
                    for s in S2:
                        dve.wait_ge(tok_mm, n[s])
                        hv = h0[s][:, :, :].rearrange("p k (b t) -> p k b t", t=SEQ)
                        for k in range(KH):
                            dve.tensor_tensor(hv[:, k, :, 1:SEQ],
                                              c.pA[s][:, k, 0:CH_IMAGES * PATCHES].rearrange("p (b t) -> p b t", t=PATCHES),
                                              pos[:, k, 1:SEQ].unsqueeze(1).to_broadcast([P, CH_IMAGES, PATCHES]), ALU.add)
                        dve.tensor_copy(hv[:, :, :, 0], pos[:, :, 0:1].to_broadcast([P, KH, CH_IMAGES])).then_inc(tokens_ready, 1)
                    for s in S2:
                        norm_centre_dve(dve, c, n0, s, n[s], h0[s][:, :, :])
                    for s in S2:
                        norm_scale_dve(dve, c, n0, s, n[s], xn[s][:, :, :])
                    for s in S2:
                        dve.wait_ge(n0.normed, n[s])
                        for k in range(KH):
                            last = dve.tensor_scalar(c.h[:, k, bass.ds(at[s], CH)], xn[s][:, k, :], c.vcol("tok_gamma", k),
                                                     c.vcol("tok_beta", k), ALU.mult, ALU.add)
                        last.then_inc(h_ready, 1)
                    for s in S2:
                        dve.wait_ge(h_ready, n[s])
                        norm_centre_dve(dve, c, n1, s, n[s], c.h[:, :, bass.ds(at[s], CH)])
                    for s in S2:
                        norm_scale_dve(dve, c, n1, s, n[s], xn[s][:, :, :])
                    for s in S2:
                        dve.wait_ge(n1.normed, n[s])
                        xv, yv = (t[s][:, :, :].rearrange("p k (b t) -> p k b t", t=SEQ) for t in (xn, xx))
                        dve.tensor_tensor(yv[:, :, :, 1:SEQ], xv[:, :, :, 0:SEQ - 1], xv[:, :, :, 1:SEQ], ALU.subtract)
                        dve.tensor_scalar(yv[:, :, :, 0:1], xv[:, :, :, 0:1], -1.0, None, ALU.mult).then_inc(shifted, 1)
                    for s in S2:
                        dve.wait_ge(shifted, n[s])
                        for k in range(KH):
                            last = dve.scalar_tensor_tensor(xf[s][:, k, :], xx[s][:, k, :], c.vcol("maa_x", k), xn[s][:, k, :],
                                                            ALU.mult, ALU.add)
                        last.then_inc(xxx_ready, 1)
                    for f, (name, row) in enumerate(MIX):
                        for s in S2:
                            dve.wait_ge(mix_ready, it * 8 + 2 * f + s + 1)
                            if f:
                                dve.wait_ge(xf_ready, it * 8 + 2 * (f - 1) + s + 1)
                            for k in range(KH):
                                last = dve.scalar_tensor_tensor(mixed[s][:, k, :], c.pA[s][:, k, 0:CH], c.vcol(name, k),
                                                                xx[s][:, k, :], ALU.add, ALU.mult)
                            last.then_inc(mix_applied, 1)
                    for s in S2:
                        dve.wait_ge(evacuated, it * 8 + 2 * 3 + s + 1)
                        dve.wait_ge(xf_ready, it * 8 + 2 * 3 + s + 1)
                        for k in range(KH):
                            last = dve.scalar_tensor_tensor(mixed[s][:, k, :], c.r[:, k, bass.ds(at[s], CH)], c.vcol("faaaa", k),
                                                            c.k[:, k, bass.ds(at[s], CH)], ALU.mult, ALU.mult)
                        last.then_inc(ruk_ready, 1)
                    for s in S2:
                        dve.wait_ge(bonus_mm, n[s])
                        dve.wait_ge(v_lo_done, n[s])
                        dve.wait_ge(decay_done, n[s])
                        dve.tensor_tensor(c.y[:, :, bass.ds(at[s], CH)], c.pA[s][:, :, 0:CH], vf[s][:, :, :],
                                          ALU.mult).then_inc(bonus_done, 1)

            @block.scalar
            def _(act):
                act.wait_ge(start_ready, 1)
                act.wait_ge(consts_loaded, CONSTS)
                with act.Fori(0, CHUNKS // STREAMS) as it:
                    n = [it * STREAMS + s + 1 for s in S2]
                    at = [it * (STREAMS * CH) + s * CH for s in S2]
                    for nm in (n0, n1):
                        for s in S2:
                            norm_square_act(act, c, nm, s, n[s])
                        for s in S2:
                            norm_std_act(act, c, nm, s, n[s])
                    for s in S2:
                        act.wait_ge(lora_ready, n[s])
                        act.activation(tanh_m[s][:, :], c.pB[s][:, 0, 0:CH], ACT.Tanh).then_inc(tanh_ready, 1)
                    for s in S2:
                        act.wait_ge(decay1_ready, n[s])
                        act.activation(tanh_d[s][:, :], c.pB[s][0:64, 0, 0:CH], ACT.Tanh).then_inc(decay_tanh, 1)
                    for s in S2:
                        act.wait_ge(proj_ready, it * 8 + s + 1)
                        for k in range(KH):
                            last = act.activation(c.sq[s][:, k, :], c.pB[s][:, k, 0:CH], ACT.Exp, bias=c.vcol("decay", k))
                        last.then_inc(evacuated, 1)
                    for s in S2:
                        act.wait_ge(evacuated, it * 8 + s + 1)
                        act.activation(c.w[:, :, bass.ds(at[s], CH)], c.sq[s][:, :, :], ACT.Exp, scale=-1.0).then_inc(decay_done, 1)
                    for f, dst in ((1, c.k), (2, None), (3, c.r)):
                        for s in S2:
                            act.wait_ge(proj_ready, it * 8 + 2 * f + s + 1)
                            out = vf[s][:, :, :] if dst is None else dst[:, :, bass.ds(at[s], CH)]
                            act.activation(out, c.pB[s][:, :, 0:CH], ACT.Copy).then_inc(evacuated, 1)

            @block.gpsimd
            def _(pool):
                with pool.Fori(0, CHUNKS // STREAMS) as it:
                    at = [it * (STREAMS * CH) + s * CH for s in S2]
                    for f in range(4):
                        for s in S2:
                            pool.wait_ge(mix_applied, it * 8 + 2 * f + s + 1)
                            if f == 0:
                                pool.wait_ge(lora_ready, it * STREAMS + s + 1)
                            elif f == 1:
                                pool.wait_ge(decay1_ready, it * STREAMS + s + 1)
                            else:
                                pool.wait_ge(proj_ready, it * 8 + 2 * (f - 1) + s + 1)
                            pool.tensor_tensor(xf[s][:, :, :], mixed[s][:, :, :], xn[s][:, :, :], ALU.add).then_inc(xf_ready, 1)
                    for s in S2:
                        pool.wait_ge(evacuated, it * 8 + 2 * 2 + s + 1)
                        pool.tensor_copy(c.hi[:, :, bass.ds(at[s], CH)], vf[s][:, :, :]).then_inc(v_hi_done, 1)
                    for s in S2:
                        wait_alone(c, pool, v_hi_done, it * STREAMS + s + 1)
                        pool.tensor_tensor(c.lo[:, :, bass.ds(at[s], CH)], vf[s][:, :, :],
                                           c.hi[:, :, bass.ds(at[s], CH)].bitcast(F32), ALU.subtract).then_inc(v_lo_done, 1)



def phase_scan(nc, c):
    SPAN = STREAMS * CH
    SPAN_IMAGES = STREAMS * CH_IMAGES
    with ExitStack() as ctx:
        sb = lambda name, shape, dt=F32: ctx.enter_context(nc.sbuf_tensor(name, shape, dt))
        sem = c.sem
        kv = [sb(f"kv{b}", [P, SPAN]) for b in range(2)]
        state = [sb(f"state{b}", [P, SPAN]) for b in range(2)]
        rs = [sb(f"rs{b}", [P, SPAN]) for b in range(2)]
        sel = sb("sel_r", [P, HS, P], F32R)
        pv = [ctx.enter_context(nc.psum_tensor(f"pv{b}", [P, 2, 512], F32)) for b in range(2)]
        py = ctx.enter_context(nc.psum_tensor("py", [P, 2, 512], F32))
        v_out, kv_ready, scanned, rs_ready, summed, y_done = (
            sem("v_out"), sem("kv_ready"), sem("scanned"), sem("rs_ready"), sem("summed"), sem("y_done"))
        sel_ready, w_zeroed = sem("sel_ready"), sem("w_zeroed")
        flat = lambda t: t[:, :, :].rearrange("p k n -> p (k n)")
        HALVES = KH * TOK // SPAN

        with nc.Block() as block:
            @block.tensor
            def _(pe):
                pe.wait_ge(sel_ready, 1)
                pe.wait_ge(c.scan_tables_loaded, 32)

                def repeat_v(i, j):
                    pe.wait_ge(kv_ready, i * HS + j + 1)
                    for q in range(2):
                        for a, part in enumerate((c.hi, c.lo)):
                            last = pe.matmul(pv[j % 2][:, q, 0:CH], sel[:, j, :],
                                             flat(part)[:, bass.ds(i * SPAN + q * CH, CH)], start=(a == 0), stop=(a == 1))
                    last.then_inc(v_out, 1)

                with pe.Fori(0, HALVES) as i:
                    repeat_v(i, 0)
                    for j in range(HS):
                        if j + 1 < HS:
                            repeat_v(i, j + 1)
                        pe.wait_ge(rs_ready, i * HS + j + 1 + 2)
                        if j == 0:
                            pe.wait_ge(y_done, i + 1)
                        for q in range(2):
                            last = pe.matmul(py[:, q, 0:CH], c.red[:, j, :], rs[j % 2][:, q * CH:(q + 1) * CH],
                                             start=(j == 0), stop=(j == HS - 1))
                        last.then_inc(summed, 1)

            @block.vector
            def _(dve):
                dve.sem_inc(kv_ready, 2)
                dve.sem_inc(y_done, 1)
                dve.sem_inc(summed, 2)
                dve.memset(c.w[:, :, :].rearrange("p k (b t) -> p (k b) t", t=SEQ)[:, :, 0:1], 0.0).then_inc(w_zeroed, 1)
                dve.wait_ge(w_zeroed, 1)
                with dve.Fori(0, HALVES) as i:
                    span = lambda t: flat(t)[:, bass.ds(i * SPAN, SPAN)]

                    def times_k(j):
                        dve.wait_ge(v_out, i * HS + j + 1)
                        dve.tensor_tensor(kv[j % 2][:, :].rearrange("p (q n) -> p q n", q=2), pv[j % 2][:, :, 0:CH],
                                          span(c.k).rearrange("p (q n) -> p q n", q=2), ALU.mult).then_inc(kv_ready, 1)

                    times_k(0)
                    for j in range(HS):
                        if j + 1 < HS:
                            times_k(j + 1)
                        dve.wait_ge(kv_ready, i * HS + j + 1 + 2)
                        dve.wait_ge(rs_ready, i * HS + j + 1)
                        dve.tensor_tensor_scan(state[j % 2][:, :], span(c.w), kv[j % 2][:, :], 0.0,
                                               op0=ALU.mult, op1=ALU.add).then_inc(scanned, 1)
                    dve.wait_ge(summed, i * HS + HS + 2)
                    yq = span(c.y).rearrange("p (q n) -> p q n", q=2)
                    dve.tensor_tensor(yq, py[:, :, 0:CH], yq, ALU.add).then_inc(y_done, 1)

            @block.gpsimd
            def _(pool):
                pool.wait_ge(c.scan_tables_loaded, 32)
                pool.tensor_copy(sel[:, :, :], c.sel_f[:, :, :]).then_inc(sel_ready, 1)
                pool.memset(rs[0][:, :], 0.0).then_inc(rs_ready, 1)
                pool.memset(rs[1][:, :], 0.0).then_inc(rs_ready, 1)
                pool.wait_ge(rs_ready, 2)
                with pool.Fori(0, HALVES) as i:
                    for j in range(HS):
                        pool.wait_ge(scanned, i * HS + j + 1)
                        wait_alone(c, pool, summed, i * HS + j + 1)
                        im = lambda t: t[:, :].rearrange("p (b t) -> p b t", t=SEQ)
                        rv = flat(c.r)[:, bass.ds(i * SPAN, SPAN)].rearrange("p (b t) -> p b t", t=SEQ)
                        pool.tensor_tensor(im(rs[j % 2])[:, :, 1:SEQ], im(state[j % 2])[:, :, 0:SEQ - 1], rv[:, :, 1:SEQ],
                                           ALU.mult).then_inc(rs_ready, 1)



def gate_weights_dve(dve, act_sems, c, r, it, experts, top, logits):
    exp_in, exp_out = act_sems
    E, T = experts, TILES
    link = Link(dve, r.step, it, 16 if top == 2 else 17)
    two = top == 2
    ex = lambda ap: ap.unsqueeze(2).to_broadcast([GT, T, E])
    link(dve.tensor_reduce(r.m[:, :], logits, AX.X, ALU.max))
    dve.tensor_tensor(r.a[:, :, 0:E], logits, ex(r.m[:, :]), ALU.subtract).then_inc(exp_in, 1)
    dve.wait_ge(exp_out, it * (2 if two else 1) + 1)
    link(dve.tensor_reduce(r.m[:, :], r.e[:, :, 0:E], AX.X, ALU.add))
    link(dve.reciprocal(r.m[:, :], r.m[:, :]))
    link(dve.tensor_tensor(r.p[:, :, 0:E], r.e[:, :, 0:E], ex(r.m[:, :]), ALU.mult))
    if two:
        chosen_from = r.p
    else:
        link(dve.tensor_tensor(r.q[:, :, 0:E], r.p[:, :, 0:E],
                               c.score_bias[:, :].unsqueeze(1).to_broadcast([GT, T, E]), ALU.add))
        chosen_from = r.q
    dve.sem_inc(c.passed, 1)
    for t in range(T):
        last = dve.max(r.top[:, t, :], chosen_from[:, t, 0:E])
    link(last)
    link(dve.tensor_copy(r.take[:, :, 0:top], r.top[:, :, 0:top]))
    dve.sem_inc(c.passed, 1)
    for t in range(T):
        last = dve.match_replace(r.rest[:, t, 0:E + 8], r.take[:, t, :], chosen_from[:, t, 0:E + 8], PICKED)
    link(last)
    link(dve.tensor_scalar(r.picked[:, :, 0:E], r.rest[:, :, 0:E], PICKED, None, ALU.is_equal))
    if two:
        dve.tensor_tensor(r.a[:, :, 0:E], r.p[:, :, 0:E], ex(r.top[:, :, 0]), ALU.subtract).then_inc(exp_in, 1)
        dve.wait_ge(exp_out, it * 2 + 2)
        link(dve.tensor_tensor(r.a[:, :, 0:E], r.e[:, :, 0:E], r.picked[:, :, 0:E], ALU.mult))
    else:
        link(dve.tensor_tensor(r.a[:, :, 0:E], r.p[:, :, 0:E], r.picked[:, :, 0:E], ALU.mult))
    link(dve.tensor_reduce(r.m[:, :], r.a[:, :, 0:E], AX.X, ALU.add))
    if not two:
        link(dve.tensor_scalar(r.m[:, :], r.m[:, :], 1e-12, None, ALU.max))
    link(dve.reciprocal(r.m[:, :], r.m[:, :]))
    link(dve.tensor_tensor(r.a[:, :, 0:E], r.a[:, :, 0:E], ex(r.m[:, :]), ALU.mult))
    if two:
        link(dve.tensor_tensor(r.a[:, :, 0:E], r.a[:, :, 0:E],
                               c.escale[:, :].unsqueeze(1).to_broadcast([GT, T, E]), ALU.mult))
    part = lambda i: r.parts[:, :, i * EROWS:i * EROWS + E]
    link(dve.tensor_copy(part(0), r.a[:, :, 0:E]))
    link(dve.tensor_tensor(r.a[:, :, 0:E], r.a[:, :, 0:E], part(0), ALU.subtract))
    link(dve.tensor_copy(part(1), r.a[:, :, 0:E]))
    dve.tensor_tensor(part(2), r.a[:, :, 0:E], part(1), ALU.subtract).then_inc(r.parts_ready, 1)
    link.close()


def phase_route(nc, c, tag, experts, top, rwkv_out):
    S2 = range(STREAMS)
    E = experts
    with ExitStack() as ctx:
        sb = lambda name, shape, dt=F32: ctx.enter_context(nc.sbuf_tensor(f"{tag}_{name}", shape, dt))
        sem = lambda name: c.sem(f"{tag}_{name}")
        setup_stream_buffers(ctx, nc, c, tag)
        xn = [sb(f"xn{s}", [P, KH, CH]) for s in S2]
        yn = [sb(f"yn{s}", [P, KH, CH]) for s in S2]
        ident = sb("ident", [GT, GT], BF16)
        r = Routing(sb, sem, E)
        ny, nx = c.norm(f"{tag}_ynorm"), c.norm(f"{tag}_xnorm")
        y_affine, wo_mm, h_added = sem("y_affine"), sem("wo_mm"), sem("h_added")
        hi_done, lo_done = sem("hi_done"), sem("lo_done")
        logits_ready, exp_in, exp_out, turned, rows_done = (
            sem("logits_ready"), sem("exp_in"), sem("exp_out"), sem("turned"), sem("rows_done"))
        init = sem("init")
        router = c.router0 if top == 2 else c.router1
        exps = 2 if top == 2 else 1

        with nc.Block() as block:
            @block.sync
            def _(sp):
                sp.dma_start(ident[:, :], c.dram["ident"][0:GT, 0:GT]).then_inc(c.ident_loaded, 16)

            @block.tensor
            def _(pe):
                pe.wait_ge(c.ident_loaded, 16 * (1 if rwkv_out else 2))
                pe.wait_ge(c.late_loaded, c.late_count[tag] * 16)
                with pe.Fori(0, CHUNKS // STREAMS) as it:
                    n = [it * STREAMS + s + 1 for s in S2]
                    at = [it * (STREAMS * CH) + s * CH for s in S2]
                    pe.wait_ge(rows_done, it + 1)
                    if rwkv_out:
                        for s in S2:
                            norm_mean_pe(pe, c, ny, s, [c.y[:, k, bass.ds(at[s], CH)] for k in range(KH)])
                        for s in S2:
                            norm_var_pe(pe, c, ny, s, n[s])
                        for s in S2:
                            pe.wait_ge(y_affine, n[s])
                            for m in range(KH):
                                for k in range(KH):
                                    last = pe.matmul(c.pA[s][:, m, 0:CH], c.w_o[:, k, m * P:(m + 1) * P], yn[s][:, k, :],
                                                     start=(k == 0), stop=(k == KH - 1))
                            last.then_inc(wo_mm, 1)
                    for s in S2:
                        if rwkv_out:
                            pe.wait_ge(h_added, n[s])
                        norm_mean_pe(pe, c, nx, s, [c.h[:, k, bass.ds(at[s], CH)] for k in range(KH)])
                    for s in S2:
                        norm_var_pe(pe, c, nx, s, n[s])
                    for s in S2:
                        pe.wait_ge(nx.normed, n[s])
                        for t in range(CH // GT):
                            for k in range(KH):
                                last = pe.matmul(c.pB[0][0:GT, 1, (s * (CH // GT) + t) * E:(s * (CH // GT) + t + 1) * E],
                                                 xn[s][:, k, t * GT:(t + 1) * GT], router[:, k, :],
                                                 start=(k == 0), stop=(k == KH - 1))
                    last.then_inc(logits_ready, 1)
                    pe.wait_ge(r.parts_ready, it + 1)
                    for t in range(TILES):
                        last = pe.transpose(c.pB[1][0:3 * EROWS, 1, :].bitcast(BF16)[:, t * GT:(t + 1) * GT],
                                            r.parts[:, t, :], ident[:, :])
                    last.then_inc(turned, 1)

            @block.vector
            def _(dve):
                dve.memset(r.take[:, :, :], PAD_LOW).then_inc(init, 1)
                dve.memset(r.p[:, :, :], PAD_LOW).then_inc(init, 1)
                dve.memset(r.q[:, :, :], PAD_LOW).then_inc(init, 1)
                dve.memset(r.parts[:, :, :], 0.0).then_inc(init, 1)
                dve.sem_inc(rows_done, 1)
                dve.wait_ge(init, 4)
                dve.memset(r.parts[:, :, EROWS - 2:EROWS], 1.0).then_inc(init, 1)
                dve.wait_ge(init, 5)
                dve.wait_ge(c.late_loaded, c.late_count[tag] * 16)
                with dve.Fori(0, CHUNKS // STREAMS) as it:
                    n = [it * STREAMS + s + 1 for s in S2]
                    at = [it * (STREAMS * CH) + s * CH for s in S2]
                    if rwkv_out:
                        for s in S2:
                            norm_centre_dve(dve, c, ny, s, n[s], c.y[:, :, bass.ds(at[s], CH)])
                        for s in S2:
                            norm_scale_dve(dve, c, ny, s, n[s], xn[s][:, :, :])
                        for s in S2:
                            dve.wait_ge(ny.normed, n[s])
                            for k in range(KH):
                                last = dve.tensor_scalar(yn[s][:, k, :], xn[s][:, k, :], c.vcol("ln_g", k), c.vcol("ln_b", k),
                                                         ALU.mult, ALU.add)
                            last.then_inc(y_affine, 1)
                        for s in S2:
                            dve.wait_ge(wo_mm, n[s])
                            hv = c.h[:, :, bass.ds(at[s], CH)]
                            dve.tensor_tensor(hv, c.pA[s][:, :, 0:CH], hv, ALU.add).then_inc(h_added, 1)
                    for s in S2:
                        if rwkv_out:
                            dve.wait_ge(h_added, n[s])
                        norm_centre_dve(dve, c, nx, s, n[s], c.h[:, :, bass.ds(at[s], CH)])
                    for s in S2:
                        norm_scale_dve(dve, c, nx, s, n[s], xn[s][:, :, :])
                    dve.wait_ge(logits_ready, it + 1)
                    gate_weights_dve(dve, (exp_in, exp_out), c, r, it, E, top,
                                     c.pB[0][0:GT, 1, 0:TILES * E].rearrange("p (t e) -> p t e", e=E))

            @block.scalar
            def _(act):
                with act.Fori(0, CHUNKS // STREAMS) as it:
                    n = [it * STREAMS + s + 1 for s in S2]
                    for nm in ((ny, nx) if rwkv_out else (nx,)):
                        for s in S2:
                            norm_square_act(act, c, nm, s, n[s])
                        for s in S2:
                            norm_std_act(act, c, nm, s, n[s])
                    for i in range(exps):
                        act.wait_ge(exp_in, it * exps + i + 1)
                        act.activation(r.e[:, :, 0:E], r.a[:, :, 0:E], ACT.Exp).then_inc(exp_out, 1)
                    act.wait_ge(turned, it + 1)
                    act.wait_ge(lo_done, n[-1])
                    act.activation(c.gates[:, bass.ds(it * (STREAMS * CH), STREAMS * CH)],
                                   c.pB[1][0:3 * EROWS, 1, :].bitcast(BF16)[:, 0:STREAMS * CH], ACT.Copy).then_inc(rows_done, 1)

            @block.gpsimd
            def _(pool):
                with pool.Fori(0, CHUNKS // STREAMS) as it:
                    n = [it * STREAMS + s + 1 for s in S2]
                    at = [it * (STREAMS * CH) + s * CH for s in S2]
                    for s in S2:
                        pool.wait_ge(nx.normed, n[s])
                        pool.tensor_copy(c.hi[:, :, bass.ds(at[s], CH)], xn[s][:, :, :]).then_inc(hi_done, 1)
                        wait_alone(c, pool, hi_done, n[s])
                        pool.tensor_tensor(c.lo[:, :, bass.ds(at[s], CH)], xn[s][:, :, :],
                                           c.hi[:, :, bass.ds(at[s], CH)].bitcast(F32), ALU.subtract).then_inc(lo_done, 1)



def phase_experts(nc, c, tag, units, gated, weights, after=None):
    UP, DOWN = 4, 2 if gated else 4
    WIDTH = KH * UP * P + DOWN * C
    EXP = 2 if gated else 1
    with ExitStack() as ctx:
        sb = lambda name, shape, dt=F32: ctx.enter_context(nc.sbuf_tensor(f"{tag}_{name}", shape, dt))
        sem = lambda name: c.sem(f"{tag}_{name}")
        raw = [sb(f"raw{b}", [P, WIDTH]) for b in range(2)]
        whi = [sb(f"whi{b}", [P, WIDTH], F32R) for b in range(2)]
        wlo = [sb(f"wlo{b}", [P, WIDTH], F32R) for b in range(2)]
        act_out = [sb(f"act_out{b}", [P, DOWN, CH]) for b in range(2)]
        hid = [sb(f"hid{b}", [P, DOWN, CH]) for b in range(2)]
        hhi = [sb(f"hhi{b}", [P, DOWN, CH], F32R) for b in range(2)]
        hlo = [sb(f"hlo{b}", [P, DOWN, CH], F32R) for b in range(2)]
        pick = sb("pick", [3 * EROWS, EROWS, P], BF16)
        pick_id = sb("pick_id", [3 * EROWS, EROWS], BF16)
        pu = [ctx.enter_context(nc.psum_tensor(f"{tag}_pu{j}", [P, 512], F32)) for j in range(UP)]
        pg = [ctx.enter_context(nc.psum_tensor(f"{tag}_pg{j}", [P, 512], F32)) for j in range(2)]
        pd = ctx.enter_context(nc.psum_tensor(f"{tag}_pd", [P, 2, 512], F32))
        loaded = [sem(f"w_loaded{b}") for b in range(2)]
        hi_done, split_done = sem("w_hi"), sem("w_split")
        gate_out, up_out, act_done, weighted, hi_ready, hid_split, down_out, added = (
            sem("gate_out"), sem("up_out"), sem("act_done"), sem("weighted"), sem("hid_hi"), sem("hid_split"),
            sem("down_out"), sem("added"))
        multiplied = sem("multiplied")
        pick_loaded, pick_ready = sem("pick_loaded"), sem("pick_ready")
        LOOPS = units // 2 if units % 2 else units // 2 - 1
        acts = UP // 2 if gated else UP

        def whole(eng, body):
            with eng.Fori(0, LOOPS) as it:
                for slot in range(2):
                    body(it * 2 + slot, slot, it, True)
            for i in range(LOOPS * 2, units):
                body(i, i % 2, i // 2, i + 1 < units)

        up_at = lambda t, k, j: t[:, (k * UP + j) * P:(k * UP + j + 1) * P]
        down_at = lambda t, j, m: t[:, KH * UP * P + j * C + m * P:KH * UP * P + j * C + (m + 1) * P]

        with nc.Block() as block:
            @block.sync
            def _(sp):
                sp.dma_start(pick_id[:, :], c.dram["pick_id"]).then_inc(pick_loaded, 16)
                for b in range(2):
                    sp.dma_start(raw[b][:, :], weights[b]).then_inc(loaded[b], 16)
                if after:
                    after(sp)
                with sp.Fori(0, (units - 2) // 2) as it:
                    for b in range(2):
                        sp.wait_ge(split_done, it * 2 + b + 1)
                        sp.dma_start(raw[b][:, :], weights[it * 2 + b + 2]).then_inc(loaded[b], 16)
                if units % 2:
                    sp.wait_ge(split_done, units - 2)
                    sp.dma_start(raw[0][:, :], weights[units - 1]).then_inc(loaded[0], 16)

            @block.gpsimd
            def _(pool):
                def split(i, b, uses):
                    wait_alone(c, pool, loaded[b], uses * 16)
                    pool.tensor_copy(whi[b][:, :], raw[b][:, :]).then_inc(hi_done, 1)
                    pool.wait_ge(hi_done, i + 1)
                    pool.tensor_tensor(wlo[b][:, :], raw[b][:, :], whi[b][:, :].bitcast(F32), ALU.subtract).then_inc(split_done, 1)

                for b in range(2):
                    split(b, b, 1)
                with pool.Fori(0, (units - 2) // 2) as it:
                    for b in range(2):
                        pool.wait_ge(down_out, (it * 2 + b + 1) * CHUNKS)
                        split(it * 2 + b + 2, b, it + 2)
                if units % 2:
                    pool.wait_ge(down_out, (units - 2) * CHUNKS)
                    split(units - 1, 0, units // 2 + 1)

            @block.tensor
            def _(pe):
                def go_up(i, b, pair, ch):
                    v = i * CHUNKS + ch
                    at = slice(ch * CH, (ch + 1) * CH)
                    for j in range(UP):
                        if gated and j % 2:
                            pe.wait_ge(multiplied, v * 2 + j // 2 + 1)
                        else:
                            pe.wait_ge(act_done, v * acts + (j // 2 if gated else j) + 1)
                        n = 0
                        for wt, xt in ((whi, c.hi), (wlo, c.hi), (whi, c.lo)):
                            for k in range(KH):
                                last = pe.matmul(pu[j][:, 0:CH], up_at(wt[b], k, j), xt[:, k, at], start=(n == 0), stop=(n == 5))
                                n += 1
                        last.then_inc(up_out, 1)
                    for a in range(EXP):
                        g = a if gated else ch % 2
                        pe.wait_ge(weighted, v + (2 if gated else 1))
                        row = pair * 4 + 2 * b + a if gated else pair
                        last = pe.matmul(pg[g][:, 0:CH], pick[:, row, :] if isinstance(row, int) else pick[:, bass.ds(row, 1), :].rearrange("r o p -> r (o p)"),
                                         c.gates[:, at], start=True, stop=True)
                    last.then_inc(gate_out, 1)

                def go_down(i, b, ch):
                    v = i * CHUNKS + ch
                    pe.wait_ge(hid_split, v + 1)
                    pe.wait_ge(added, v + 1)
                    for m in range(KH):
                        n = 0
                        for wt, xt in ((whi, hhi), (wlo, hhi), (whi, hlo)):
                            for j in range(DOWN):
                                last = pe.matmul(pd[:, m, 0:CH], down_at(wt[b], j, m), xt[ch % 2][:, j, :],
                                                 start=(n == 0), stop=(n == 3 * DOWN - 1))
                                n += 1
                    last.then_inc(down_out, 1)

                pe.wait_ge(pick_ready, 1)
                pe.wait_ge(split_done, 1)
                go_up(0, 0, 0, 0)

                def body(i, b, pair, more):
                    for ch in range(CHUNKS):
                        if ch + 1 < CHUNKS:
                            go_up(i, b, pair, ch + 1)
                        elif more:
                            pe.wait_ge(split_done, i + 2)
                            go_up(i + 1, 1 - b, pair + b, 0)
                        go_down(i, b, ch)

                whole(pe, body)

            @block.scalar
            def _(act):
                def body(i, b, pair, more):
                    for ch in range(CHUNKS):
                        v = i * CHUNKS + ch
                        o = act_out[ch % 2]
                        act.wait_ge(weighted, v + 1)
                        for j in range(acts):
                            bank = 2 * j if gated else j
                            act.wait_ge(up_out, v * UP + bank + 1)
                            act.activation(o[:, j, :], pu[bank][:, 0:CH], ACT.Silu).then_inc(act_done, 1)
                        act.wait_ge(weighted, v + 1 + 2)
                        act.activation(hhi[ch % 2][:, :, :], hid[ch % 2][:, :, :], ACT.Copy).then_inc(hi_ready, 1)

                whole(act, body)

            @block.vector
            def _(dve):
                dve.wait_ge(pick_loaded, 16)
                dve.tensor_copy(pick[:, :, :], pick_id[:, :].unsqueeze(2).to_broadcast([3 * EROWS, EROWS, P])).then_inc(pick_ready, 1)
                dve.sem_inc(weighted, 2)
                dve.sem_inc(act_done, acts)
                dve.sem_inc(added, 1)
                if gated:
                    dve.sem_inc(multiplied, 2)

                def weigh(i, ch):
                    v = i * CHUNKS + ch
                    q = ch % 2
                    if gated:
                        for a in range(2):
                            dve.wait_ge(act_done, v * acts + a + 1 + acts)
                            dve.wait_ge(up_out, v * UP + 2 * a + 2)
                            dve.tensor_tensor(act_out[q][:, a, :], pu[2 * a + 1][:, 0:CH], act_out[q][:, a, :],
                                              ALU.mult).then_inc(multiplied, 1)
                        dve.wait_ge(gate_out, v + 1)
                        for a in range(2):
                            dve.wait_ge(multiplied, v * 2 + a + 1 + 2)
                            last = dve.tensor_tensor(hid[q][:, a, :], pg[a][:, 0:CH], act_out[q][:, a, :], ALU.mult)
                        last.then_inc(weighted, 1)
                    else:
                        dve.wait_ge(act_done, v * acts + acts + acts)
                        dve.wait_ge(gate_out, v + 1)
                        dve.tensor_tensor(hid[q][:, :, :], act_out[q][:, :, :], over_halves(pg[q][:, 0:CH], DOWN),
                                          ALU.mult).then_inc(weighted, 1)
                    dve.wait_ge(hi_ready, v + 1)
                    dve.tensor_tensor(hlo[q][:, :, :], hid[q][:, :, :], hhi[q][:, :, :].bitcast(F32), ALU.subtract).then_inc(hid_split, 1)

                def add(i, ch):
                    dve.wait_ge(down_out, i * CHUNKS + ch + 1)
                    hv = c.h[:, :, ch * CH:(ch + 1) * CH]
                    dve.tensor_tensor(hv, pd[:, :, 0:CH], hv, ALU.add).then_inc(added, 1)

                weigh(0, 0)

                def body(i, b, pair, more):
                    for ch in range(CHUNKS):
                        if ch + 1 < CHUNKS:
                            weigh(i, ch + 1)
                        elif more:
                            weigh(i + 1, 0)
                        add(i, ch)

                whole(dve, body)



def phase_attention(nc, c):
    G = 4
    with ExitStack() as ctx:
        sb = lambda name, shape, dt=F32: ctx.enter_context(nc.sbuf_tensor(f"at_{name}", shape, dt))
        pb = lambda name, shape: ctx.enter_context(nc.psum_tensor(f"at_{name}", shape, F32))
        sem = lambda name: c.sem(f"at_{name}")
        c.xc, c.sq = [sb("xc", [P, KH, CH])], [sb("sq", [P, KH, CH])]
        c.std, c.rstd = [sb("std", [P, CH])], [sb("rstd", [P, CH])]
        wqkv = sb("wqkv", [P, 3, KH, 512])
        w_out = sb("w_out", [P, G, C])
        x64 = sb("x64", [P, KH, CH_IMAGES, QP])
        q64 = sb("q64", [P, G, CH_IMAGES, QP])
        kT = sb("kT", [P, G, CH])
        v2 = sb("v2", [P, PAIRS, 512])
        dif = [sb(f"dif{b}", [P, G, G, SEQ]) for b in range(2)]
        ex = [sb(f"ex{b}", [P, G, G, SEQ]) for b in range(2)]
        top = sb("top", [P, G, G])
        den = sb("den", [P, G, G])
        wts = [sb(f"wts{b}", [P, HEADS, 2 * QP]) for b in range(2)]
        wT = [sb(f"wT{b}", [P, HEADS, 2 * QP]) for b in range(2)]
        o_sq = sb("o_sq", [P, 512])
        o_ms = sb("o_ms", [P, PAIRS, HEADS])
        o_tok = sb("o_tok", [P, PAIRS, 512])
        o_n = sb("o_n", [P, PAIRS, 512])
        oT = sb("oT", [P, G, CH])
        gam = sb("gam", [P, 1])
        lam4 = sb("lam4", [P, 4, HD])
        lam_t = sb("lam_t", [P, 2, HD])
        lam_s = sb("lam_s", [P, 2])
        neg_lam = sb("neg_lam", [P, 1])
        ident = sb("ident", [P, P])
        score = pb("score", [P, G, 512])
        pu = pb("pu", [P, 2, 512])
        pw = pb("pw", [P, 2, 512])
        c.stat = [pw[:, 0, 0:CH]]
        banks = [pu[:, 0, :], pu[:, 1, :], pw[:, 0, :], pw[:, 1, :]]
        nm = c.norm("attn_norm")
        loaded, init, link_sem = sem("loaded"), sem("init"), sem("link")
        x_ready, qk_out, q_done, k_done, v_out, v_done = (
            sem("x_ready"), sem("qk_out"), sem("q_done"), sem("k_done"), sem("v_out"), sem("v_done"))
        scores_out, tops_found, topped, exp_done, wts_done, turned, wT_done = (
            sem("scores_out"), sem("tops_found"), sem("topped"), sem("exp_done"), sem("wts_done"), sem("turned"), sem("wT_done"))
        o_out, squared, o_copied, ms_done, rms_done, o_normed, oT_out, oT_done, proj_out, chunk_done = (
            sem("o_out"), sem("squared"), sem("o_copied"), sem("ms_done"), sem("rms_done"), sem("o_normed"),
            sem("oT_out"), sem("oT_done"), sem("proj_out"), sem("chunk_done"))
        consts_ready, steps, tail_steps = sem("consts_ready"), sem("steps"), sem("tail_steps")
        lam_ready, lam_exp = sem("lam_ready"), sem("lam_exp")
        d = c.dram
        LOADS = 6

        with nc.Block() as block:
            @block.sync
            def _(sp):
                sp.dma_start(wqkv[:, :, :, :], d["wqkv"]).then_inc(loaded, 16)
                sp.dma_start(w_out[:, :, :], d["w_out"]).then_inc(loaded, 16)
                sp.dma_start(ident[:, :], d["ident_f"]).then_inc(loaded, 16)
                sp.dma_start(lam4[:, :, :].rearrange("p a d -> p (a d)"), d["lambdas"].partition_broadcast(P)).then_inc(loaded, 16)
                for half in range(2):
                    sp.dma_start(gam[64 * half:64 * half + 64, :], d["gamma1"]).then_inc(loaded, 16)
                sp.dma_start(c.router1[:, :, :], d["router1"]).then_inc(c.late_loaded, 16)
                sp.dma_start(c.score_bias[:, :], d["score_bias"].partition_broadcast(GT)).then_inc(c.late_loaded, 16)

            @block.tensor
            def _(pe):
                pe.wait_ge(loaded, LOADS * 16)
                pe.wait_ge(consts_ready, 1)
                with pe.Fori(0, CHUNKS) as it:
                    n = it + 1
                    at = it * CH
                    pe.wait_ge(chunk_done, n)
                    norm_mean_pe(pe, c, nm, 0, [c.h[:, k, bass.ds(at, CH)] for k in range(KH)])
                    norm_var_pe(pe, c, nm, 0, n)
                    pe.wait_ge(nm.normed, n)
                    for g in range(4):
                        if g == 2:
                            pe.wait_ge(q_done, it * 2 + 1)
                        if g == 3:
                            pe.wait_ge(q_done, it * 2 + 2)
                        for mm in range(2):
                            m = (g % 2) * 2 + mm
                            for k in range(KH):
                                last = pe.matmul(banks[(g % 2) * 2 + mm][:, 0:CH], wqkv[:, g // 2, k, m * P:(m + 1) * P],
                                                 x64[:, k, :, 0:SEQ], start=(k == 0), stop=(k == KH - 1))
                        last.then_inc(qk_out, 1)
                    for p in range(PAIRS):
                        if p % 2 == 0:
                            pe.wait_ge(k_done, it * 2 + p // 2 + 1)
                        for k in range(KH):
                            last = pe.matmul(banks[p], x64[:, k, 2 * p:2 * p + 2, :].rearrange("p b t -> p (b t)"),
                                             wqkv[:, 2, k, :], start=(k == 0), stop=(k == KH - 1))
                        last.then_inc(v_out, 1)

                    def scores(p):
                        pe.wait_ge(topped, it * PAIRS + p + 1)
                        for b in range(2):
                            img = 2 * p + b
                            for m in range(G):
                                for g in range(G):
                                    last = pe.matmul(score[QP * b:QP * b + QP, g, m * SEQ:(m + 1) * SEQ],
                                                     q64[HD * g:HD * g + HD, m, img, :],
                                                     kT[HD * g:HD * g + HD, m, img * SEQ:(img + 1) * SEQ],
                                                     start=True, stop=True, tile_position=(HD * g, QP * b))
                        last.then_inc(scores_out, 1)

                    scores(0)
                    pe.wait_ge(v_done, it * PAIRS + PAIRS)
                    for p in range(PAIRS):
                        v = it * PAIRS + p
                        if p + 1 < PAIRS:
                            scores(p + 1)
                        pe.wait_ge(wts_done, v + 1)
                        if p:
                            pe.wait_ge(wT_done, v)
                        for h in range(HEADS):
                            last = pe.transpose(pu[:, h // 4, (h % 4) * P:(h % 4 + 1) * P], wts[p % 2][:, h, :], ident[:, :])
                        last.then_inc(turned, 1)
                        pe.wait_ge(wT_done, v + 1)
                        if p >= 2:
                            pe.wait_ge(o_copied, v - 1)
                        for h in range(HEADS):
                            hd = 2 * (h % 4) + h // 4
                            last = pe.matmul(pw[:, p % 2, hd * 64:(hd + 1) * 64], wT[p % 2][:, h, :],
                                             v2[:, p, hd * 64:(hd + 1) * 64], start=True, stop=True)
                        last.then_inc(o_out, 1)
                    for p in range(PAIRS):
                        pe.wait_ge(o_normed, it * PAIRS + p + 1)
                        for m in range(G):
                            last = pe.transpose(banks[p][:, m * P:(m + 1) * P], o_n[:, p, m * P:(m + 1) * P], ident[:, :])
                        last.then_inc(oT_out, 1)
                    pe.wait_ge(oT_done, it * PAIRS + PAIRS)
                    for m in range(KH):
                        for k in range(G):
                            last = pe.matmul(score[:, m, 0:CH], w_out[:, k, m * P:(m + 1) * P], oT[:, k, :],
                                             start=(k == 0), stop=(k == G - 1))
                    last.then_inc(proj_out, 1)

            @block.scalar
            def _(act):
                act.wait_ge(lam_ready, 1)
                act.activation(lam_s[:, :], lam_s[:, :], ACT.Exp).then_inc(lam_exp, 1)
                with act.Fori(0, CHUNKS) as it:
                    n = it + 1
                    norm_square_act(act, c, nm, 0, n)
                    norm_std_act(act, c, nm, 0, n)
                    for g in range(2):
                        act.wait_ge(qk_out, it * 4 + g + 1)
                        for mm in range(2):
                            last = act.activation(q64[:, 2 * g + mm, :, 0:SEQ],
                                                  banks[2 * g + mm][:, 0:CH].rearrange("p (b t) -> p b t", t=SEQ), ACT.Copy)
                        last.then_inc(q_done, 1)
                    for p in range(PAIRS):
                        act.wait_ge(v_out, it * PAIRS + p + 1)
                        act.activation(v2[:, p, :], banks[p], ACT.Copy).then_inc(v_done, 1)
                    for p in range(PAIRS):
                        v = it * PAIRS + p
                        act.wait_ge(topped, v + 2)
                        act.activation(ex[p % 2][:, :, :, :], dif[p % 2][:, :, :, :], ACT.Exp, scale=HD ** -0.5).then_inc(exp_done, 1)
                        act.wait_ge(turned, v + 1)
                        act.activation(wT[p % 2][:, :, :].rearrange("p (a h) q -> p a (h q)", a=2), pu[:, :, :], ACT.Copy).then_inc(wT_done, 1)
                        act.wait_ge(o_out, v + 1)
                        act.activation(o_tok[:, p, :], pw[:, p % 2, :], ACT.Copy).then_inc(o_copied, 1)
                        act.wait_ge(o_copied, v + 1)
                        if p:
                            act.wait_ge(ms_done, v)
                        act.activation(o_sq[:, :], o_tok[:, p, :], ACT.Square).then_inc(squared, 1)
                    act.wait_ge(ms_done, it * PAIRS + PAIRS)
                    act.activation(o_ms[:, :, :], o_ms[:, :, :], ACT.Sqrt, scale=1.0 / 64).then_inc(rms_done, 1)
                    for p in range(PAIRS):
                        act.wait_ge(oT_out, it * PAIRS + p + 1)
                        act.activation(oT[:, :, p * 2 * SEQ:(p + 1) * 2 * SEQ].rearrange("p m (b t) -> p m b t", t=SEQ),
                                       banks[p].rearrange("p (m b t) -> p m b t", m=G, b=2)[:, :, :, 0:SEQ],
                                       ACT.Copy).then_inc(oT_done, 1)

            @block.vector
            def _(dve):
                link = Link(dve, link_sem)
                for t in (x64, q64, wts[0], wts[1]):
                    dve.memset(t[:], 0.0).then_inc(init, 1)
                dve.sem_inc(chunk_done, 1)
                dve.sem_inc(topped, 1)
                dve.wait_ge(init, 4)
                dve.wait_ge(loaded, LOADS * 16)
                link(dve.tensor_tensor(lam_t[:, :, :], lam4[:, 0::2, :], lam4[:, 1::2, :], ALU.mult))
                dve.tensor_reduce(lam_s[:, :], lam_t[:, :, :], AX.X, ALU.add).then_inc(lam_ready, 1)
                dve.wait_ge(lam_exp, 1)
                link(dve.tensor_tensor(neg_lam[:, :], lam_s[:, 1:2], lam_s[:, 0:1], ALU.subtract))
                link(dve.tensor_scalar(neg_lam[:, :], neg_lam[:, :], -LAMBDA_INIT, None, ALU.add))
                link(dve.tensor_scalar(gam[:, :], gam[:, :], 1.0 - LAMBDA_INIT, None, ALU.mult))
                dve.tensor_scalar(w_out[:, :, :], w_out[:, :, :], gam[:, 0:1], None, ALU.mult).then_inc(consts_ready, 1)
                with dve.Fori(0, CHUNKS) as it:
                    n = it + 1
                    at = it * CH
                    norm_centre_dve(dve, c, nm, 0, n, c.h[:, :, bass.ds(at, CH)])
                    dve.wait_ge(nm.std_ready, n)
                    dve.reciprocal(c.rstd[0][:, :], c.std[0][:, :]).then_inc(nm.rstd_ready, 1)
                    dve.wait_ge(nm.rstd_ready, n)
                    im = lambda t: t.rearrange("p (b t) -> p b t", t=SEQ)
                    for k in range(KH):
                        last = dve.tensor_tensor(x64[:, k, :, 0:SEQ], im(c.xc[0][:, k, :]), im(c.rstd[0][:, :]), ALU.mult)
                    last.then_inc(nm.normed, 1)
                    for g in range(2):
                        dve.wait_ge(qk_out, it * 4 + 2 + g + 1)
                        dve.tensor_copy(kT[:, 2 * g:2 * g + 2, :], (pu if g == 0 else pw)[:, :, 0:CH]).then_inc(k_done, 1)

                    def less_top(p):
                        v = it * PAIRS + p
                        dve.wait_ge(scores_out, v + 1)
                        sc = score[:, :, 0:G * SEQ].rearrange("p g (m t) -> p g m t", t=SEQ)
                        dve.tensor_reduce(top[:, :, :], sc, AX.X, ALU.max).then_inc(tops_found, 1)
                        dve.wait_ge(tops_found, v + 1)
                        dve.tensor_tensor(dif[p % 2][:, :, :, :], sc, top[:, :, :].unsqueeze(3).to_broadcast([P, G, G, SEQ]),
                                          ALU.subtract).then_inc(topped, 1)

                    less_top(0)
                    for p in range(PAIRS):
                        v = it * PAIRS + p
                        if p + 1 < PAIRS:
                            less_top(p + 1)
                        e = ex[p % 2]
                        link = Link(dve, steps, v, 4)
                        dve.wait_ge(exp_done, v + 1)
                        link(dve.tensor_reduce(den[:, :, :], e[:, :, :, :], AX.X, ALU.add))
                        link(dve.reciprocal(den[:, :, :], den[:, :, :]))
                        link(dve.tensor_scalar(den[:, 1::2, :], den[:, 1::2, :], neg_lam[:, 0:1], None, ALU.mult))
                        link(dve.tensor_tensor(e[:, :, :, :], e[:, :, :, :], den[:, :, :].unsqueeze(3).to_broadcast([P, G, G, SEQ]), ALU.mult))
                        link.close()
                        for b in range(2):
                            rows = slice(QP * b, QP * b + QP)
                            last = dve.tensor_tensor(
                                wts[p % 2][rows, :, QP * b:QP * b + SEQ].rearrange("p (u m) t -> p u m t", u=2),
                                e[rows, 0::2, :, :], e[rows, 1::2, :, :], ALU.add)
                        last.then_inc(wts_done, 1)
                        dve.wait_ge(squared, v + 1)
                        dve.tensor_reduce(o_ms[:, p, :], o_sq[:, :].rearrange("p (h d) -> p h d", d=64), AX.X, ALU.add).then_inc(ms_done, 1)
                    dve.wait_ge(rms_done, n)
                    link = Link(dve, tail_steps, it, 2)
                    link(dve.tensor_scalar(o_ms[:, :, :], o_ms[:, :, :], 1e-8, None, ALU.add))
                    link(dve.reciprocal(o_ms[:, :, :], o_ms[:, :, :]))
                    link.close()
                    for p in range(PAIRS):
                        hd = lambda t: t[:, p, :].rearrange("p (h d) -> p h d", d=64)
                        dve.tensor_tensor(hd(o_n), hd(o_tok), o_ms[:, p, :].unsqueeze(2).to_broadcast([P, HEADS, 64]),
                                          ALU.mult).then_inc(o_normed, 1)
                    dve.wait_ge(proj_out, n)
                    hv = c.h[:, :, bass.ds(at, CH)]
                    dve.tensor_tensor(hv, score[:, 0:KH, 0:CH], hv, ALU.add).then_inc(chunk_done, 1)


def phase_store(nc, c):
    with nc.Block() as block:
        @block.sync
        def _(sp):
            for k in range(KH):
                sp.dma_start(c.dram["out"][k], c.h[:, k, :]).then_inc(c.stored, 16)
            sp.wait_ge(c.stored, 16 * KH)


def tower(nc, dram, stop="all"):
    with ExitStack() as ctx:
        sb = lambda name, shape, dt=F32: ctx.enter_context(nc.sbuf_tensor(name, shape, dt))
        c = Shared()
        c.dram = dram
        c.taken = []

        def sem(name):
            s = nc.alloc_semaphore(name)
            c.taken.append(s)
            return s

        c.sem = sem
        c.norm = lambda name: Norm(c.sem, name)
        c.h = sb("h", [P, KH, TOK])
        c.vec = sb("vec", [P, len(VEC) * KH])
        c.vcol = lambda name, k: c.vec[:, VEC[name] * KH + k:VEC[name] * KH + k + 1]
        c.mean_w = sb("mean_w", [P, P])
        c.eps = sb("eps", [P, 1])
        c.hi, c.lo = sb("hi", [P, KH, TOK], F32R), sb("lo", [P, KH, TOK], F32R)
        c.w_o = sb("w_o", [P, KH, C])
        c.router0, c.router1 = sb("router0", [P, KH, 8]), sb("router1", [P, KH, 32])
        c.escale, c.score_bias = sb("escale", [GT, 8]), sb("score_bias", [GT, 32])
        c.gates = sb("gates", [3 * EROWS, TOK], BF16)
        c.late_loaded, c.scan_tables_loaded = c.sem("late_loaded"), c.sem("scan_tables_loaded")
        c.passed = c.sem("passed")
        c.ident_loaded, c.stored = c.sem("ident_loaded"), c.sem("stored")
        c.late_count = {"route0": 3, "route1": 5}
        c.taken = []

        def phase(build, *args):
            build(nc, c, *args)
            nc.clear_and_free_semaphores(c.taken)
            nc.all_engine_barrier()
            c.taken = []

        with ExitStack() as rwkv:
            rb = lambda name, shape, dt=F32: rwkv.enter_context(nc.sbuf_tensor(name, shape, dt))
            c.r, c.k, c.w, c.y = (rb(name, [P, KH, TOK]) for name in ("r", "k", "w", "y"))
            c.red, c.sel_f = rb("red", [P, HS, P]), rb("sel_f", [P, HS, P])
            phase(phase_tokens)
            phase(phase_scan)
            phase(phase_route, "route0", 8, 2, True)
        if stop != "rwkv":
            phase(phase_experts, "moe0", 16, False, dram["moe0"])
            if stop != "moe0":
                phase(phase_attention)
                if stop != "attn":
                    phase(phase_route, "route1", 32, 6, False)
                    phase(phase_experts, "moe1", 17, True, dram["moe1"])
        phase_store(nc, c)


STOP = "all"


def kernel(**inputs):
    import numpy as np
    import concourse.bacc as bacc
    from concourse.bass_utils import run_bass_kernel_spmd

    nc = bacc.Bacc("TRN2", target_bir_lowering=False, num_devices=1)
    a = {name: np.asarray(x) for name, x in inputs.items()}
    f = np.float32

    def rows(w):
        return w.reshape(-1, P, w.shape[1]).transpose(1, 0, 2)

    put = {}
    x = a["x"].reshape(CHUNKS, CH_IMAGES, 3, 6, 16, 6, 16).transpose(0, 2, 4, 6, 1, 3, 5)
    put["patches"] = x.reshape(CHUNKS, PB, P, CH_IMAGES * PATCHES).transpose(0, 2, 1, 3)
    put["wtok"] = rows(a["L0_tok_W"])
    A0 = "L0_attn_time_"
    vectors = [a["L0_tok_b"], a["L0_tok_cls_token"], a["L0_tok_gamma"], a["L0_tok_beta"], a[A0 + "maa_x"], a[A0 + "maa_w"],
               a[A0 + "maa_k"], a[A0 + "maa_v"], a[A0 + "maa_r"], a[A0 + "decay"], a[A0 + "faaaa"],
               a["L0_attn_ln_g"], a["L0_attn_ln_b"]]
    put["vec"] = np.stack([v.reshape(KH, P) for v in vectors]).transpose(2, 0, 1).reshape(P, -1)
    put["pos"] = rows(a["L0_tok_pos_embedding"][0].T)
    put["mean_w"] = np.full((P, P), 1.0 / C, f)
    put["w_lora"] = rows(a[A0 + "maa_w1"])
    put["w_lora2"] = a[A0 + "maa_w2"].reshape(P, C)
    put["w_rkv"] = np.stack([rows(a["L0_attn_W_" + n]) for n in "rkv"], axis=1)
    put["w_decay"] = rows(a[A0 + "decay_w1"])
    put["w_decay2"] = a[A0 + "decay_w2"]
    put["w_o"] = rows(a["L0_attn_W_o"])
    row = np.arange(P)
    put["head_ones"] = (row[:, None] // HS == row[None, :] // HS).astype(f)
    same = row[:, None, None] // HS == row[None, None, :] // HS
    j = np.arange(HS)[None, :, None]
    put["sel"] = (same & (row[:, None, None] % HS == j)).astype(f)
    put["red"] = (same & (row[None, None, :] % HS == j)).astype(f)
    put["router0"] = rows(a["L0_ffn_router_w"].T)
    put["router1"] = rows(a["L1_ffn_router_weight"].T)
    put["escale"] = a["L0_ffn_expert_scale"].reshape(1, 8)
    put["score_bias"] = a["L1_ffn_e_score_bias"].reshape(1, 32)
    put["ident"] = np.eye(P, dtype=mybir.dt.np(BF16))
    put["ident_f"] = np.eye(P, dtype=f)
    part_row = np.arange(3 * EROWS)[:, None] % EROWS
    put["pick_id"] = (part_row == np.arange(EROWS)[None, :]).astype(mybir.dt.np(BF16))
    w1 = a["L0_ffn_w1"].reshape(8, 2, 512, KH, P).transpose(0, 1, 4, 3, 2)
    w2 = a["L0_ffn_w2"].reshape(8, C, 2, 4, P).transpose(0, 2, 4, 3, 1)
    put["moe0"] = np.concatenate([w1.reshape(16, P, -1), w2.reshape(16, P, -1)], axis=2)
    shared = np.stack([a["L1_ffn_shared_gate_w"].reshape(2, P, C), a["L1_ffn_shared_up_w"].reshape(2, P, C)], axis=1)
    up = np.concatenate([a["L1_ffn_gate_up_proj"], shared.reshape(2, 2 * P, C)])
    up = up.reshape(17, 512, KH, P).transpose(0, 3, 2, 1)
    down = np.concatenate([a["L1_ffn_down_proj"], a["L1_ffn_shared_down_w"].reshape(C, 2, P).transpose(1, 0, 2)])
    down = down.reshape(17, 2, C, P).transpose(0, 3, 1, 2)
    put["moe1"] = np.concatenate([up.reshape(17, P, -1), down.reshape(17, P, -1)], axis=2)
    wq, wkv = a["L1_attn_Wq"], a["L1_attn_Wkv"]
    put["wqkv"] = np.stack([rows(wq), rows(wkv[:, :512]), rows(wkv[:, 512:])], axis=1)
    put["w_out"] = rows(a["L1_attn_Wout"])
    put["lambdas"] = np.concatenate([a["L1_attn_lambda_" + n] for n in ("q1", "k1", "q2", "k2")]).reshape(1, 4 * HD)
    put["gamma1"] = a["L1_attn_gamma"].reshape(64, 1)

    arrays = {f"in_{name}": np.ascontiguousarray(v) for name, v in put.items()}
    dram = {name: nc.dram_tensor(f"in_{name}", v.shape, mybir.dt.from_np(v.dtype), kind="ExternalInput").ap()
            for name, v in ((n[3:], v) for n, v in arrays.items())}
    dram["out"] = nc.dram_tensor("out", (KH, P, TOK), F32, kind="ExternalOutput").ap()
    tower(nc, dram, STOP)
    out = run_bass_kernel_spmd(nc, [arrays], core_ids=[0]).results[0]["out"]
    return np.ascontiguousarray(out.reshape(C, IMAGES, SEQ).transpose(1, 2, 0))
```

```python
import concourse.bass as bass
from concourse import mybir
from contextlib import ExitStack

F32 = mybir.dt.float32
F32R = mybir.dt.float32r
BF16 = mybir.dt.bfloat16
ALU = mybir.AluOpType
ACT = mybir.ActivationFunctionType
AX = mybir.AxisListType

P = 128
IMAGES, SEQ, C = 32, 37, 256
PATCHES = SEQ - 1
TOK = IMAGES * SEQ
KH = C // P
CH_IMAGES = 8
CH = CH_IMAGES * SEQ
CHUNKS = IMAGES // CH_IMAGES
STREAMS = CHUNKS
PATCH_D = 768
PB = PATCH_D // P
HS = 16
LN_EPS = 1e-5
GT = 74
TILES = TOK // GT
EROWS = 34
HEADS, HD = 8, 32
LAMBDA_INIT = 0.8 - 0.6 * 2.718281828459045 ** -0.3
PAIRS = CH_IMAGES // 2
QP = 64
PAD_LOW, PICKED = -3.0e38, -3.2e38

VEC = {name: i for i, name in enumerate(
    ["tok_b", "cls", "tok_gamma", "tok_beta", "maa_x", "maa_w", "maa_k", "maa_v", "maa_r",
     "decay", "faaaa", "ln_g", "ln_b"])}


class Shared:
    pass


class Norm:

    def __init__(self, sem, name):
        self.mean_ready, self.centred, self.squared = sem(f"{name}_mean"), sem(f"{name}_centred"), sem(f"{name}_squared")
        self.var_ready, self.std_ready = sem(f"{name}_var"), sem(f"{name}_std")
        self.rstd_ready, self.normed = sem(f"{name}_rstd"), sem(f"{name}_normed")


class Routing:

    def __init__(self, sb, sem, E):
        self.m, self.a, self.e = sb("m", [GT, TILES]), sb("a", [GT, TILES, E]), sb("e", [GT, TILES, E])
        self.p, self.q = sb("p", [GT, TILES, E + 8]), sb("q", [GT, TILES, E + 8])
        self.top, self.take = sb("top", [GT, TILES, 8]), sb("take", [GT, TILES, 8])
        self.rest, self.picked = sb("rest", [GT, TILES, E + 8]), sb("picked", [GT, TILES, E])
        self.parts = sb("parts", [GT, TILES, 3 * EROWS], BF16)
        self.step, self.parts_ready = sem("step"), sem("parts_ready")


class Link:

    def __init__(self, eng, sem, it=0, per=0):
        self.eng, self.sem, self.base, self.n, self.per = eng, sem, it * per, 0, per

    def __call__(self, ins):
        self.n += 1
        ins.then_inc(self.sem, 1)
        self.eng.wait_ge(self.sem, self.base + self.n)

    def close(self):
        assert not self.per or self.n == self.per, (self.n, self.per)


def wait_alone(c, eng, sem, value):
    eng.wait_ge(sem, value)
    eng.sem_inc(c.passed, 1)


def over_halves(ap, k=KH):
    return ap.unsqueeze(1).to_broadcast([ap.shape[0], k, ap.shape[1]])



def norm_mean_pe(pe, c, nm, s, halves):
    for k in range(KH):
        last = pe.matmul(c.stat[s], c.mean_w[:, :], halves[k], start=(k == 0), stop=(k == KH - 1))
    last.then_inc(nm.mean_ready, 1)


def norm_var_pe(pe, c, nm, s, n):
    pe.wait_ge(nm.squared, n)
    for k in range(KH):
        last = pe.matmul(c.stat[s], c.mean_w[:, :], c.sq[s][:, k, :], start=(k == 0), stop=(k == KH - 1))
    last.then_inc(nm.var_ready, 1)


def norm_centre_dve(dve, c, nm, s, n, src):
    dve.wait_ge(nm.mean_ready, n)
    dve.tensor_tensor(c.xc[s][:, :, :], src, over_halves(c.stat[s]), ALU.subtract).then_inc(nm.centred, 1)


def norm_square_act(act, c, nm, s, n):
    act.wait_ge(nm.centred, n)
    act.activation(c.sq[s][:, :, :], c.xc[s][:, :, :], ACT.Square).then_inc(nm.squared, 1)


def norm_std_act(act, c, nm, s, n):
    act.wait_ge(nm.var_ready, n)
    act.activation(c.std[s][:, :], c.stat[s], ACT.Sqrt, bias=c.eps[:, :]).then_inc(nm.std_ready, 1)


def norm_scale_dve(dve, c, nm, s, n, out):
    dve.wait_ge(nm.std_ready, n)
    dve.reciprocal(c.rstd[s][:, :], c.std[s][:, :]).then_inc(nm.rstd_ready, 1)
    dve.wait_ge(nm.rstd_ready, n)
    dve.tensor_tensor(out, c.xc[s][:, :, :], over_halves(c.rstd[s][:, :]), ALU.mult).then_inc(nm.normed, 1)


def setup_stream_buffers(ctx, nc, c, tag):
    sb = lambda name, shape, dt=F32: ctx.enter_context(nc.sbuf_tensor(f"{tag}_{name}", shape, dt))
    c.xc = [sb(f"xc{s}", [P, KH, CH]) for s in range(STREAMS)]
    c.sq = [sb(f"sq{s}", [P, KH, CH]) for s in range(STREAMS)]
    c.std = [sb(f"std{s}", [P, CH]) for s in range(STREAMS)]
    c.rstd = [sb(f"rstd{s}", [P, CH]) for s in range(STREAMS)]
    c.ps = [ctx.enter_context(nc.psum_tensor(f"{tag}_ps{s}", [P, 2, 512], F32)) for s in range(STREAMS)]
    c.stat = [c.ps[s][:, 0, 0:CH] for s in range(STREAMS)]



def phase_tokens(nc, c):
    with ExitStack() as ctx:
        sb = lambda name, shape, dt=F32: ctx.enter_context(nc.sbuf_tensor(name, shape, dt))
        setup_stream_buffers(ctx, nc, c, "tk")
        S2 = range(STREAMS)
        wtok = sb("wtok", [P, PB, C])
        pos = sb("pos", [P, KH, SEQ])
        patches = [t[:, :, :].rearrange("p k n -> p (k n)")[:, 0:PB * CH_IMAGES * PATCHES].rearrange("p (b n) -> p b n", b=PB)
                   for t in (c.r, c.k, c.w, c.y)]
        xn = [sb(f"xn{s}", [P, KH, CH]) for s in S2]
        xx = [sb(f"xx{s}", [P, KH, CH]) for s in S2]
        h0 = xx
        mixed = [sb(f"mixed{s}", [P, KH, CH]) for s in S2]
        xf = [sb(f"xf{s}", [P, KH, CH]) for s in S2]
        tanh_m = [sb(f"tanh_m{s}", [P, CH]) for s in S2]
        tanh_d = [sb(f"tanh_d{s}", [64, CH]) for s in S2]
        vf = [sb(f"vf{s}", [P, KH, CH]) for s in S2]
        w_lora = sb("w_lora", [P, KH, P])
        w_lora2 = sb("w_lora2", [P, C])
        w_rkv = sb("w_rkv", [P, 3, KH, C])
        w_decay = sb("w_decay", [P, KH, 64])
        w_decay2 = sb("w_decay2", [64, C])
        head_ones = sb("head_ones", [P, P])
        sem = c.sem
        first_loaded, consts_loaded = sem("tok_w_loaded"), sem("mix_w_loaded")
        x_loaded = [sem(f"x_loaded{s}") for s in S2]
        tok_mm, tokens_ready, pos_ready, h_ready = sem("tok_mm"), sem("tokens_ready"), sem("pos_ready"), sem("h_ready")
        n0, n1 = c.norm("tok_norm"), c.norm("rwkv_norm")
        shifted, xxx_ready = sem("shifted"), sem("xxx_ready")
        lora_ready, tanh_ready = sem("lora_ready"), sem("tanh_ready")
        mix_ready, mix_applied, xf_ready, proj_ready, evacuated = (
            sem("mix_ready"), sem("mix_applied"), sem("xf_ready"), sem("proj_ready"), sem("evacuated"))
        decay1_ready, decay_tanh, decay_done = sem("decay1_ready"), sem("decay_tanh"), sem("decay_done")
        v_hi_done, v_lo_done = sem("v_hi_done"), sem("v_lo_done")
        ruk_ready, bonus_mm, bonus_done = sem("ruk_ready"), sem("bonus_mm"), sem("bonus_done")
        start_ready = sem("start_ready")
        d = c.dram
        MIX = [("maa_w", 0), ("maa_k", 1), ("maa_v", 2), ("maa_r", 3)]
        RKV = {"maa_r": 0, "maa_k": 1, "maa_v": 2}

        with nc.Block() as block:
            @block.sync
            def _(sp):
                sp.dma_start(wtok[:, :, :], d["wtok"]).then_inc(first_loaded, 16)
                for s in S2:
                    sp.dma_start(patches[s], d["patches"][s]).then_inc(x_loaded[s], 16)
                for dst, src in ((c.vec[:, :], d["vec"]), (pos[:, :, :], d["pos"]),
                                 (c.mean_w[:, :], d["mean_w"]), (w_lora[:, :, :], d["w_lora"]),
                                 (w_lora2[:, :], d["w_lora2"]), (w_rkv[:, :, :, :], d["w_rkv"]),
                                 (w_decay[:, :, :], d["w_decay"]), (w_decay2[:, :], d["w_decay2"]),
                                 (head_ones[:, :], d["head_ones"])):
                    sp.dma_start(dst, src).then_inc(consts_loaded, 16)
                sp.dma_start(c.w_o[:, :, :], d["w_o"]).then_inc(c.late_loaded, 16)
                sp.dma_start(c.router0[:, :, :], d["router0"]).then_inc(c.late_loaded, 16)
                sp.dma_start(c.escale[:, :], d["escale"].partition_broadcast(GT)).then_inc(c.late_loaded, 16)
                sp.dma_start(c.red[:, :, :], d["red"]).then_inc(c.scan_tables_loaded, 16)
            CONSTS = 9 * 16

            @block.tensor
            def _(pe):
                pe.wait_ge(first_loaded, 16)
                n = [s + 1 for s in S2]
                for s in S2:
                    pe.wait_ge(x_loaded[s], 16)
                    for m in range(KH):
                        for k in range(PB):
                            last = pe.matmul(c.ps[s][:, m, 0:CH_IMAGES * PATCHES], wtok[:, k, m * P:(m + 1) * P],
                                             patches[s][:, k, :], start=(k == 0), stop=(k == PB - 1))
                    last.then_inc(tok_mm, 1)
                pe.wait_ge(consts_loaded, CONSTS)
                for s in S2:
                    pe.wait_ge(tokens_ready, n[s])
                    norm_mean_pe(pe, c, n0, s, [h0[s][:, k, :] for k in range(KH)])
                for s in S2:
                    norm_var_pe(pe, c, n0, s, n[s])
                for s in S2:
                    pe.wait_ge(h_ready, n[s])
                    at = slice(s * CH, (s + 1) * CH)
                    norm_mean_pe(pe, c, n1, s, [c.h[:, k, at] for k in range(KH)])
                for s in S2:
                    norm_var_pe(pe, c, n1, s, n[s])
                for s in S2:
                    pe.wait_ge(xxx_ready, n[s])
                    for k in range(KH):
                        last = pe.matmul(c.ps[s][:, 0, 0:CH], w_lora[:, k, :], xf[s][:, k, :],
                                         start=(k == 0), stop=(k == KH - 1))
                    last.then_inc(lora_ready, 1)
                for f, (name, row) in enumerate(MIX):
                    for s in S2:
                        if f == 0:
                            pe.wait_ge(tanh_ready, n[s])
                        else:
                            pe.wait_ge(evacuated, (f - 1) * STREAMS + s + 1)
                        for m in range(KH):
                            last = pe.matmul(c.ps[s][:, m, 0:CH], w_lora2[32 * row:32 * row + 32, m * P:(m + 1) * P],
                                             tanh_m[s][32 * row:32 * row + 32, :], start=True, stop=True)
                        last.then_inc(mix_ready, 1)
                    for s in S2:
                        pe.wait_ge(xf_ready, f * STREAMS + s + 1)
                        if name == "maa_w":
                            for k in range(KH):
                                last = pe.matmul(c.ps[s][0:64, 0, 0:CH], w_decay[:, k, :], xf[s][:, k, :],
                                                 start=(k == 0), stop=(k == KH - 1))
                            last.then_inc(decay1_ready, 1)
                        else:
                            for m in range(KH):
                                for k in range(KH):
                                    last = pe.matmul(c.ps[s][:, m, 0:CH], w_rkv[:, RKV[name], k, m * P:(m + 1) * P],
                                                     xf[s][:, k, :], start=(k == 0), stop=(k == KH - 1))
                            last.then_inc(proj_ready, 1)
                    if name == "maa_w":
                        for s in S2:
                            pe.wait_ge(decay_tanh, n[s])
                            for m in range(KH):
                                last = pe.matmul(c.ps[s][:, m, 0:CH], w_decay2[:, m * P:(m + 1) * P],
                                                 tanh_d[s][:, :], start=True, stop=True)
                            last.then_inc(proj_ready, 1)
                for s in S2:
                    pe.wait_ge(ruk_ready, n[s])
                    for m in range(KH):
                        last = pe.matmul(c.ps[s][:, m, 0:CH], head_ones[:, :], mixed[s][:, m, :], start=True, stop=True)
                    last.then_inc(bonus_mm, 1)

            @block.vector
            def _(dve):
                dve.memset(c.eps[:, :], LN_EPS).then_inc(start_ready, 1)
                dve.wait_ge(consts_loaded, CONSTS)
                for k in range(KH):
                    dve.tensor_scalar(pos[:, k, 1:SEQ], pos[:, k, 1:SEQ], c.vcol("tok_b", k), None, ALU.add).then_inc(pos_ready, 1)
                    dve.tensor_scalar(pos[:, k, 0:1], pos[:, k, 0:1], c.vcol("cls", k), None, ALU.add).then_inc(pos_ready, 1)
                dve.wait_ge(pos_ready, 2 * KH)
                n = [s + 1 for s in S2]
                at = [slice(s * CH, (s + 1) * CH) for s in S2]
                for s in S2:
                    dve.wait_ge(tok_mm, n[s])
                    hv = h0[s][:, :, :].rearrange("p k (b t) -> p k b t", t=SEQ)
                    for k in range(KH):
                        dve.tensor_tensor(hv[:, k, :, 1:SEQ],
                                          c.ps[s][:, k, 0:CH_IMAGES * PATCHES].rearrange("p (b t) -> p b t", t=PATCHES),
                                          pos[:, k, 1:SEQ].unsqueeze(1).to_broadcast([P, CH_IMAGES, PATCHES]), ALU.add)
                    dve.tensor_copy(hv[:, :, :, 0], pos[:, :, 0:1].to_broadcast([P, KH, CH_IMAGES])).then_inc(tokens_ready, 1)
                for s in S2:
                    norm_centre_dve(dve, c, n0, s, n[s], h0[s][:, :, :])
                for s in S2:
                    norm_scale_dve(dve, c, n0, s, n[s], xn[s][:, :, :])
                for s in S2:
                    dve.wait_ge(n0.normed, n[s])
                    for k in range(KH):
                        last = dve.tensor_scalar(c.h[:, k, at[s]], xn[s][:, k, :], c.vcol("tok_gamma", k),
                                                 c.vcol("tok_beta", k), ALU.mult, ALU.add)
                    last.then_inc(h_ready, 1)
                for s in S2:
                    dve.wait_ge(h_ready, n[s])
                    norm_centre_dve(dve, c, n1, s, n[s], c.h[:, :, at[s]])
                for s in S2:
                    norm_scale_dve(dve, c, n1, s, n[s], xn[s][:, :, :])
                for s in S2:
                    dve.wait_ge(n1.normed, n[s])
                    xv, yv = (t[s][:, :, :].rearrange("p k (b t) -> p k b t", t=SEQ) for t in (xn, xx))
                    dve.tensor_tensor(yv[:, :, :, 1:SEQ], xv[:, :, :, 0:SEQ - 1], xv[:, :, :, 1:SEQ], ALU.subtract)
                    dve.tensor_scalar(yv[:, :, :, 0:1], xv[:, :, :, 0:1], -1.0, None, ALU.mult).then_inc(shifted, 1)
                for s in S2:
                    dve.wait_ge(shifted, n[s])
                    for k in range(KH):
                        last = dve.scalar_tensor_tensor(xf[s][:, k, :], xx[s][:, k, :], c.vcol("maa_x", k), xn[s][:, k, :],
                                                        ALU.mult, ALU.add)
                    last.then_inc(xxx_ready, 1)
                for f, (name, row) in enumerate(MIX):
                    for s in S2:
                        dve.wait_ge(mix_ready, f * STREAMS + s + 1)
                        if f:
                            dve.wait_ge(xf_ready, (f - 1) * STREAMS + s + 1)
                        for k in range(KH):
                            last = dve.scalar_tensor_tensor(mixed[s][:, k, :], c.ps[s][:, k, 0:CH], c.vcol(name, k),
                                                            xx[s][:, k, :], ALU.add, ALU.mult)
                        last.then_inc(mix_applied, 1)
                for s in S2:
                    dve.wait_ge(evacuated, 3 * STREAMS + s + 1)
                    dve.wait_ge(xf_ready, 3 * STREAMS + s + 1)
                    for k in range(KH):
                        last = dve.scalar_tensor_tensor(mixed[s][:, k, :], c.r[:, k, at[s]], c.vcol("faaaa", k),
                                                        c.k[:, k, at[s]], ALU.mult, ALU.mult)
                    last.then_inc(ruk_ready, 1)
                for s in S2:
                    dve.wait_ge(bonus_mm, n[s])
                    dve.wait_ge(v_lo_done, n[s])
                    dve.wait_ge(decay_done, n[s])
                    dve.tensor_tensor(c.y[:, :, at[s]], c.ps[s][:, :, 0:CH], vf[s][:, :, :],
                                      ALU.mult).then_inc(bonus_done, 1)

            @block.scalar
            def _(act):
                act.wait_ge(start_ready, 1)
                act.wait_ge(consts_loaded, CONSTS)
                n = [s + 1 for s in S2]
                at = [slice(s * CH, (s + 1) * CH) for s in S2]
                for nm in (n0, n1):
                    for s in S2:
                        norm_square_act(act, c, nm, s, n[s])
                    for s in S2:
                        norm_std_act(act, c, nm, s, n[s])
                for s in S2:
                    act.wait_ge(lora_ready, n[s])
                    act.activation(tanh_m[s][:, :], c.ps[s][:, 0, 0:CH], ACT.Tanh).then_inc(tanh_ready, 1)
                for s in S2:
                    act.wait_ge(decay1_ready, n[s])
                    act.activation(tanh_d[s][:, :], c.ps[s][0:64, 0, 0:CH], ACT.Tanh).then_inc(decay_tanh, 1)
                for s in S2:
                    act.wait_ge(proj_ready, s + 1)
                    for k in range(KH):
                        last = act.activation(c.sq[s][:, k, :], c.ps[s][:, k, 0:CH], ACT.Exp, bias=c.vcol("decay", k))
                    last.then_inc(evacuated, 1)
                for s in S2:
                    act.wait_ge(evacuated, s + 1)
                    act.activation(c.w[:, :, at[s]], c.sq[s][:, :, :], ACT.Exp, scale=-1.0).then_inc(decay_done, 1)
                for f, dst in ((1, c.k), (2, None), (3, c.r)):
                    for s in S2:
                        act.wait_ge(proj_ready, f * STREAMS + s + 1)
                        out = vf[s][:, :, :] if dst is None else dst[:, :, at[s]]
                        act.activation(out, c.ps[s][:, :, 0:CH], ACT.Copy).then_inc(evacuated, 1)

            @block.gpsimd
            def _(pool):
                at = [slice(s * CH, (s + 1) * CH) for s in S2]
                for f in range(4):
                    for s in S2:
                        pool.wait_ge(mix_applied, f * STREAMS + s + 1)
                        if f == 0:
                            pool.wait_ge(lora_ready, s + 1)
                        elif f == 1:
                            pool.wait_ge(decay1_ready, s + 1)
                        else:
                            pool.wait_ge(proj_ready, (f - 1) * STREAMS + s + 1)
                        pool.tensor_tensor(xf[s][:, :, :], mixed[s][:, :, :], xn[s][:, :, :], ALU.add).then_inc(xf_ready, 1)
                for s in S2:
                    pool.wait_ge(evacuated, 2 * STREAMS + s + 1)
                    pool.tensor_copy(c.hi[:, :, at[s]], vf[s][:, :, :]).then_inc(v_hi_done, 1)
                for s in S2:
                    pool.wait_ge(v_hi_done, s + 1)
                    pool.tensor_tensor(c.lo[:, :, at[s]], vf[s][:, :, :],
                                       c.hi[:, :, at[s]].bitcast(F32), ALU.subtract).then_inc(v_lo_done, 1)



def phase_scan(nc, c):
    SPAN = 2 * CH
    AHEAD = 3
    with ExitStack() as ctx:
        sb = lambda name, shape, dt=F32: ctx.enter_context(nc.sbuf_tensor(name, shape, dt))
        sem = c.sem
        kv = [sb(f"kv{b}", [P, SPAN]) for b in range(4)]
        state = [sb(f"state{b}", [P, SPAN]) for b in range(2)]
        rs = [sb(f"rs{b}", [P, SPAN]) for b in range(2)]
        sel = sb("sel_r", [P, HS, P], F32R)
        pv = [ctx.enter_context(nc.psum_tensor(f"pv{b}", [P, 2, 512], F32)) for b in range(AHEAD)]
        py = ctx.enter_context(nc.psum_tensor("py", [P, 2, 512], F32))
        v_out, kv_ready, scanned, rs_ready, summed, y_done = (
            sem("v_out"), sem("kv_ready"), sem("scanned"), sem("rs_ready"), sem("summed"), sem("y_done"))
        sel_ready, w_zeroed = sem("sel_ready"), sem("w_zeroed")
        flat = lambda t: t[:, :, :].rearrange("p k n -> p (k n)")
        HALVES = KH * TOK // SPAN

        with nc.Block() as block:
            @block.tensor
            def _(pe):
                pe.wait_ge(sel_ready, 16)
                pe.wait_ge(c.scan_tables_loaded, 16)

                def repeat_v(i, j):
                    held = j - AHEAD if j >= AHEAD else max(x for x in range(HS) if x % AHEAD == j) - HS
                    pe.wait_ge(kv_ready, i * HS + held + 1 + AHEAD)
                    bank = pv[j % AHEAD]
                    for q in range(2):
                        for a, part in enumerate((c.hi, c.lo)):
                            last = pe.matmul(bank[:, q, 0:CH], sel[:, j, :],
                                             flat(part)[:, bass.ds(i * SPAN + q * CH, CH)], start=(a == 0), stop=(a == 1))
                    last.then_inc(v_out, 1)

                with pe.Fori(0, HALVES) as i:
                    repeat_v(i, 0)
                    repeat_v(i, 1)
                    for j in range(HS):
                        if j + 2 < HS:
                            repeat_v(i, j + 2)
                        pe.wait_ge(rs_ready, i * HS + j + 1 + 2)
                        if j == 0:
                            pe.wait_ge(y_done, i + 1)
                        for q in range(2):
                            last = pe.matmul(py[:, q, 0:CH], c.red[:, j, :], rs[j % 2][:, q * CH:(q + 1) * CH],
                                             start=(j == 0), stop=(j == HS - 1))
                        last.then_inc(summed, 1)

            @block.vector
            def _(dve):
                dve.sem_inc(kv_ready, AHEAD)
                dve.sem_inc(y_done, 1)
                dve.sem_inc(summed, 2)
                dve.memset(c.w[:, :, :].rearrange("p k (b t) -> p (k b) t", t=SEQ)[:, :, 0:1], 0.0).then_inc(w_zeroed, 1)
                dve.wait_ge(w_zeroed, 1)
                with dve.Fori(0, HALVES) as i:
                    span = lambda t: flat(t)[:, bass.ds(i * SPAN, SPAN)]

                    def times_k(j):
                        dve.wait_ge(v_out, i * HS + j + 1)
                        dve.tensor_tensor(kv[j % 4][:, :].rearrange("p (q n) -> p q n", q=2), pv[j % AHEAD][:, :, 0:CH],
                                          span(c.k).rearrange("p (q n) -> p q n", q=2), ALU.mult).then_inc(kv_ready, 1)

                    times_k(0)
                    for j in range(HS):
                        if j + 1 < HS:
                            times_k(j + 1)
                        dve.wait_ge(kv_ready, i * HS + j + 1 + AHEAD)
                        dve.wait_ge(rs_ready, i * HS + j + 1)
                        dve.tensor_tensor_scan(state[j % 2][:, :], span(c.w), kv[j % 4][:, :], 0.0,
                                               op0=ALU.mult, op1=ALU.add).then_inc(scanned, 1)
                    dve.wait_ge(summed, i * HS + HS + 2)
                    yq = span(c.y).rearrange("p (q n) -> p q n", q=2)
                    dve.tensor_tensor(yq, py[:, :, 0:CH], yq, ALU.add).then_inc(y_done, 1)

            @block.gpsimd
            def _(pool):
                pool.dma_start(sel[:, :, :], c.dram["sel"]).then_inc(sel_ready, 16)
                pool.memset(rs[0][:, :], 0.0).then_inc(rs_ready, 1)
                pool.memset(rs[1][:, :], 0.0).then_inc(rs_ready, 1)
                pool.wait_ge(rs_ready, 2)
                with pool.Fori(0, HALVES) as i:
                    for j in range(HS):
                        pool.wait_ge(scanned, i * HS + j + 1)
                        wait_alone(c, pool, summed, i * HS + j + 1)
                        im = lambda t: t[:, :].rearrange("p (b t) -> p b t", t=SEQ)
                        rv = flat(c.r)[:, bass.ds(i * SPAN, SPAN)].rearrange("p (b t) -> p b t", t=SEQ)
                        pool.tensor_tensor(im(rs[j % 2])[:, :, 1:SEQ], im(state[j % 2])[:, :, 0:SEQ - 1], rv[:, :, 1:SEQ],
                                           ALU.mult).then_inc(rs_ready, 1)



def gate_weights_dve(dve, act_sems, c, r, experts, top, logits):
    exp_in, exp_out = act_sems
    E, T = experts, TILES
    link = Link(dve, r.step)
    two = top == 2
    ex = lambda ap: ap.unsqueeze(2).to_broadcast([GT, T, E])
    link(dve.tensor_reduce(r.m[:, :], logits, AX.X, ALU.max))
    dve.tensor_tensor(r.a[:, :, 0:E], logits, ex(r.m[:, :]), ALU.subtract).then_inc(exp_in, 1)
    dve.wait_ge(exp_out, 1)
    link(dve.tensor_reduce(r.m[:, :], r.e[:, :, 0:E], AX.X, ALU.add))
    link(dve.reciprocal(r.m[:, :], r.m[:, :]))
    link(dve.tensor_tensor(r.p[:, :, 0:E], r.e[:, :, 0:E], ex(r.m[:, :]), ALU.mult))
    if two:
        chosen_from = r.p
    else:
        link(dve.tensor_tensor(r.q[:, :, 0:E], r.p[:, :, 0:E],
                               c.score_bias[:, :].unsqueeze(1).to_broadcast([GT, T, E]), ALU.add))
        chosen_from = r.q
    for t in range(T):
        last = dve.max(r.top[:, t, :], chosen_from[:, t, 0:E])
    link(last)
    link(dve.tensor_copy(r.take[:, :, 0:top], r.top[:, :, 0:top]))
    for t in range(T):
        last = dve.match_replace(r.rest[:, t, 0:E + 8], r.take[:, t, :], chosen_from[:, t, 0:E + 8], PICKED)
    link(last)
    link(dve.tensor_scalar(r.picked[:, :, 0:E], r.rest[:, :, 0:E], PICKED, None, ALU.is_equal))
    if two:
        dve.tensor_tensor(r.a[:, :, 0:E], r.p[:, :, 0:E], ex(r.top[:, :, 0]), ALU.subtract).then_inc(exp_in, 1)
        dve.wait_ge(exp_out, 2)
        link(dve.tensor_tensor(r.a[:, :, 0:E], r.e[:, :, 0:E], r.picked[:, :, 0:E], ALU.mult))
    else:
        link(dve.tensor_tensor(r.a[:, :, 0:E], r.p[:, :, 0:E], r.picked[:, :, 0:E], ALU.mult))
    link(dve.tensor_reduce(r.m[:, :], r.a[:, :, 0:E], AX.X, ALU.add))
    if not two:
        link(dve.tensor_scalar(r.m[:, :], r.m[:, :], 1e-12, None, ALU.max))
    link(dve.reciprocal(r.m[:, :], r.m[:, :]))
    link(dve.tensor_tensor(r.a[:, :, 0:E], r.a[:, :, 0:E], ex(r.m[:, :]), ALU.mult))
    if two:
        link(dve.tensor_tensor(r.a[:, :, 0:E], r.a[:, :, 0:E],
                               c.escale[:, :].unsqueeze(1).to_broadcast([GT, T, E]), ALU.mult))
    part = lambda i: r.parts[:, :, i * EROWS:i * EROWS + E]
    link(dve.tensor_copy(part(0), r.a[:, :, 0:E]))
    link(dve.tensor_tensor(r.a[:, :, 0:E], r.a[:, :, 0:E], part(0), ALU.subtract))
    link(dve.tensor_copy(part(1), r.a[:, :, 0:E]))
    dve.tensor_tensor(part(2), r.a[:, :, 0:E], part(1), ALU.subtract).then_inc(r.parts_ready, 1)


def phase_route(nc, c, tag, experts, top, rwkv_out):
    S2 = range(STREAMS)
    E = experts
    with ExitStack() as ctx:
        sb = lambda name, shape, dt=F32: ctx.enter_context(nc.sbuf_tensor(f"{tag}_{name}", shape, dt))
        sem = lambda name: c.sem(f"{tag}_{name}")
        setup_stream_buffers(ctx, nc, c, tag)
        xn = [sb(f"xn{s}", [P, KH, CH]) for s in S2]
        yn = [sb(f"yn{s}", [P, KH, CH]) for s in S2]
        ident = sb("ident", [GT, GT], BF16)
        r = Routing(sb, sem, E)
        ny, nx = c.norm(f"{tag}_ynorm"), c.norm(f"{tag}_xnorm")
        y_affine, wo_mm, h_added = sem("y_affine"), sem("wo_mm"), sem("h_added")
        hi_done, lo_done = sem("hi_done"), sem("lo_done")
        logits_ready, exp_in, exp_out, turned, rows_done = (
            sem("logits_ready"), sem("exp_in"), sem("exp_out"), sem("turned"), sem("rows_done"))
        init = sem("init")
        router = c.router0 if top == 2 else c.router1
        exps = 2 if top == 2 else 1
        HT = TILES // 2
        turned_rows = [c.ps[1 + half][0:3 * EROWS, 1, :].bitcast(BF16)[:, 0:HT * GT] for half in range(2)]

        with nc.Block() as block:
            @block.sync
            def _(sp):
                sp.dma_start(ident[:, :], c.dram["ident"][0:GT, 0:GT]).then_inc(c.ident_loaded, 16)

            @block.tensor
            def _(pe):
                pe.wait_ge(c.ident_loaded, 16 * (1 if rwkv_out else 2))
                pe.wait_ge(c.late_loaded, c.late_count[tag] * 16)
                n = [s + 1 for s in S2]
                at = [slice(s * CH, (s + 1) * CH) for s in S2]
                if rwkv_out:
                    for s in S2:
                        norm_mean_pe(pe, c, ny, s, [c.y[:, k, at[s]] for k in range(KH)])
                    for s in S2:
                        norm_var_pe(pe, c, ny, s, n[s])
                    for s in S2:
                        pe.wait_ge(y_affine, n[s])
                        for m in range(KH):
                            for k in range(KH):
                                last = pe.matmul(c.ps[s][:, m, 0:CH], c.w_o[:, k, m * P:(m + 1) * P], yn[s][:, k, :],
                                                 start=(k == 0), stop=(k == KH - 1))
                        last.then_inc(wo_mm, 1)
                for s in S2:
                    if rwkv_out:
                        pe.wait_ge(h_added, n[s])
                    norm_mean_pe(pe, c, nx, s, [c.h[:, k, at[s]] for k in range(KH)])
                for s in S2:
                    norm_var_pe(pe, c, nx, s, n[s])
                for s in S2:
                    pe.wait_ge(nx.normed, n[s])
                    for t in range(CH // GT):
                        for k in range(KH):
                            last = pe.matmul(c.ps[0][0:GT, 1, (s * (CH // GT) + t) * E:(s * (CH // GT) + t + 1) * E],
                                             xn[s][:, k, t * GT:(t + 1) * GT], router[:, k, :],
                                             start=(k == 0), stop=(k == KH - 1))
                last.then_inc(logits_ready, 1)
                pe.wait_ge(r.parts_ready, 1)
                for t in range(TILES):
                    pe.transpose(turned_rows[t // HT][:, (t % HT) * GT:(t % HT + 1) * GT], r.parts[:, t, :], ident[:, :]) \
                        .then_inc(turned, 1)

            @block.vector
            def _(dve):
                dve.memset(r.take[:, :, :], PAD_LOW).then_inc(init, 1)
                dve.memset(r.p[:, :, :], PAD_LOW).then_inc(init, 1)
                dve.memset(r.q[:, :, :], PAD_LOW).then_inc(init, 1)
                dve.memset(r.parts[:, :, :], 0.0).then_inc(init, 1)
                dve.wait_ge(init, 4)
                dve.memset(r.parts[:, :, EROWS - 2:EROWS], 1.0).then_inc(init, 1)
                dve.wait_ge(init, 5)
                dve.wait_ge(c.late_loaded, c.late_count[tag] * 16)
                n = [s + 1 for s in S2]
                at = [slice(s * CH, (s + 1) * CH) for s in S2]
                if rwkv_out:
                    for s in S2:
                        norm_centre_dve(dve, c, ny, s, n[s], c.y[:, :, at[s]])
                    for s in S2:
                        norm_scale_dve(dve, c, ny, s, n[s], xn[s][:, :, :])
                    for s in S2:
                        dve.wait_ge(ny.normed, n[s])
                        for k in range(KH):
                            last = dve.tensor_scalar(yn[s][:, k, :], xn[s][:, k, :], c.vcol("ln_g", k), c.vcol("ln_b", k),
                                                     ALU.mult, ALU.add)
                        last.then_inc(y_affine, 1)
                    for s in S2:
                        dve.wait_ge(wo_mm, n[s])
                        hv = c.h[:, :, at[s]]
                        dve.tensor_tensor(hv, c.ps[s][:, :, 0:CH], hv, ALU.add).then_inc(h_added, 1)
                for s in S2:
                    if rwkv_out:
                        dve.wait_ge(h_added, n[s])
                    norm_centre_dve(dve, c, nx, s, n[s], c.h[:, :, at[s]])
                for s in S2:
                    norm_scale_dve(dve, c, nx, s, n[s], xn[s][:, :, :])
                dve.wait_ge(logits_ready, 1)
                gate_weights_dve(dve, (exp_in, exp_out), c, r, E, top,
                                 c.ps[0][0:GT, 1, 0:TILES * E].rearrange("p (t e) -> p t e", e=E))

            @block.scalar
            def _(act):
                n = [s + 1 for s in S2]
                for nm in ((ny, nx) if rwkv_out else (nx,)):
                    for s in S2:
                        norm_square_act(act, c, nm, s, n[s])
                    for s in S2:
                        norm_std_act(act, c, nm, s, n[s])
                for i in range(exps):
                    act.wait_ge(exp_in, i + 1)
                    act.activation(r.e[:, :, 0:E], r.a[:, :, 0:E], ACT.Exp).then_inc(exp_out, 1)
                for half in range(2):
                    act.wait_ge(turned, (half + 1) * HT)
                    act.activation(c.gates[:, half * HT * GT:(half + 1) * HT * GT], turned_rows[half], ACT.Copy).then_inc(rows_done, 1)
                act.wait_ge(rows_done, 2)

            @block.gpsimd
            def _(pool):
                n = [s + 1 for s in S2]
                at = [slice(s * CH, (s + 1) * CH) for s in S2]
                for s in S2:
                    pool.wait_ge(nx.normed, n[s])
                    pool.tensor_copy(c.hi[:, :, at[s]], xn[s][:, :, :]).then_inc(hi_done, 1)
                    pool.wait_ge(hi_done, n[s])
                    pool.tensor_tensor(c.lo[:, :, at[s]], xn[s][:, :, :],
                                       c.hi[:, :, at[s]].bitcast(F32), ALU.subtract).then_inc(lo_done, 1)



def phase_experts(nc, c, tag, units, gated, weights, after=None):
    UP, DOWN = 4, 2 if gated else 4
    WIDTH = KH * UP * P + DOWN * C
    EXP = 2 if gated else 1
    with ExitStack() as ctx:
        sb = lambda name, shape, dt=F32: ctx.enter_context(nc.sbuf_tensor(f"{tag}_{name}", shape, dt))
        sem = lambda name: c.sem(f"{tag}_{name}")
        raw = [sb(f"raw{b}", [P, WIDTH]) for b in range(2)]
        whi = [sb(f"whi{b}", [P, WIDTH], F32R) for b in range(2)]
        wlo = [sb(f"wlo{b}", [P, WIDTH], F32R) for b in range(2)]
        act_out = [sb(f"act_out{b}", [P, DOWN, CH]) for b in range(2)]
        hid = [sb(f"hid{b}", [P, DOWN, CH]) for b in range(2)]
        hhi = [sb(f"hhi{b}", [P, DOWN, CH], F32R) for b in range(2)]
        hlo = [sb(f"hlo{b}", [P, DOWN, CH], F32R) for b in range(2)]
        pick = sb("pick", [3 * EROWS, EROWS, P], BF16)
        pick_id = sb("pick_id", [3 * EROWS, EROWS], BF16)
        pu = [ctx.enter_context(nc.psum_tensor(f"{tag}_pu{j}", [P, 512], F32)) for j in range(UP)]
        pg = [ctx.enter_context(nc.psum_tensor(f"{tag}_pg{j}", [P, 512], F32)) for j in range(2)]
        pd = ctx.enter_context(nc.psum_tensor(f"{tag}_pd", [P, 2, 512], F32))
        loaded = [sem(f"w_loaded{b}") for b in range(2)]
        hi_done, split_done = sem("w_hi"), sem("w_split")
        gate_out, up_out, act_done, weighted, hi_ready, hid_split, down_out, added = (
            sem("gate_out"), sem("up_out"), sem("act_done"), sem("weighted"), sem("hid_hi"), sem("hid_split"),
            sem("down_out"), sem("added"))
        multiplied = sem("multiplied")
        pick_loaded, pick_ready = sem("pick_loaded"), sem("pick_ready")
        LOOPS = units // 2 if units % 2 else units // 2 - 1
        acts = UP // 2 if gated else UP

        def whole(eng, body):
            with eng.Fori(0, LOOPS) as it:
                for slot in range(2):
                    body(it * 2 + slot, slot, it, True)
            for i in range(LOOPS * 2, units):
                body(i, i % 2, i // 2, i + 1 < units)

        up_at = lambda t, k, j: t[:, (k * UP + j) * P:(k * UP + j + 1) * P]
        down_at = lambda t, j, m: t[:, KH * UP * P + j * C + m * P:KH * UP * P + j * C + (m + 1) * P]

        with nc.Block() as block:
            @block.sync
            def _(sp):
                sp.dma_start(pick_id[:, :], c.dram["pick_id"]).then_inc(pick_loaded, 16)
                for b in range(2):
                    sp.dma_start(raw[b][:, :], weights[b]).then_inc(loaded[b], 16)
                if after:
                    after(sp)
                with sp.Fori(0, (units - 2) // 2) as it:
                    for b in range(2):
                        sp.wait_ge(split_done, it * 2 + b + 1)
                        sp.dma_start(raw[b][:, :], weights[it * 2 + b + 2]).then_inc(loaded[b], 16)
                if units % 2:
                    sp.wait_ge(split_done, units - 2)
                    sp.dma_start(raw[0][:, :], weights[units - 1]).then_inc(loaded[0], 16)

            @block.gpsimd
            def _(pool):
                def split(i, b, uses):
                    wait_alone(c, pool, loaded[b], uses * 16)
                    pool.tensor_copy(whi[b][:, :], raw[b][:, :]).then_inc(hi_done, 1)
                    pool.wait_ge(hi_done, i + 1)
                    pool.tensor_tensor(wlo[b][:, :], raw[b][:, :], whi[b][:, :].bitcast(F32), ALU.subtract).then_inc(split_done, 1)

                for b in range(2):
                    split(b, b, 1)
                with pool.Fori(0, (units - 2) // 2) as it:
                    for b in range(2):
                        pool.wait_ge(down_out, (it * 2 + b + 1) * CHUNKS)
                        split(it * 2 + b + 2, b, it + 2)
                if units % 2:
                    pool.wait_ge(down_out, (units - 2) * CHUNKS)
                    split(units - 1, 0, units // 2 + 1)

            @block.tensor
            def _(pe):
                def go_up(i, b, pair, ch):
                    v = i * CHUNKS + ch
                    at = slice(ch * CH, (ch + 1) * CH)
                    for j in range(UP):
                        if gated and j % 2:
                            pe.wait_ge(multiplied, v * 2 + j // 2 + 1)
                        else:
                            pe.wait_ge(act_done, v * acts + (j // 2 if gated else j) + 1)
                        n = 0
                        for wt, xt in ((whi, c.hi), (wlo, c.hi), (whi, c.lo)):
                            for k in range(KH):
                                last = pe.matmul(pu[j][:, 0:CH], up_at(wt[b], k, j), xt[:, k, at], start=(n == 0), stop=(n == 5))
                                n += 1
                        last.then_inc(up_out, 1)
                    for a in range(EXP):
                        g = a if gated else ch % 2
                        pe.wait_ge(weighted, v + (2 if gated else 1))
                        row = pair * 4 + 2 * b + a if gated else pair
                        last = pe.matmul(pg[g][:, 0:CH], pick[:, row, :] if isinstance(row, int) else pick[:, bass.ds(row, 1), :].rearrange("r o p -> r (o p)"),
                                         c.gates[:, at], start=True, stop=True)
                    last.then_inc(gate_out, 1)

                def go_down(i, b, ch):
                    v = i * CHUNKS + ch
                    pe.wait_ge(hid_split, v + 1)
                    pe.wait_ge(added, v + 1)
                    for m in range(KH):
                        n = 0
                        for wt, xt in ((whi, hhi), (wlo, hhi), (whi, hlo)):
                            for j in range(DOWN):
                                last = pe.matmul(pd[:, m, 0:CH], down_at(wt[b], j, m), xt[ch % 2][:, j, :],
                                                 start=(n == 0), stop=(n == 3 * DOWN - 1))
                                n += 1
                    last.then_inc(down_out, 1)

                pe.wait_ge(pick_ready, 1)
                pe.wait_ge(split_done, 1)
                go_up(0, 0, 0, 0)

                def body(i, b, pair, more):
                    for ch in range(CHUNKS):
                        if ch + 1 < CHUNKS:
                            go_up(i, b, pair, ch + 1)
                        elif more:
                            pe.wait_ge(split_done, i + 2)
                            go_up(i + 1, 1 - b, pair + b, 0)
                        go_down(i, b, ch)

                whole(pe, body)

            @block.scalar
            def _(act):
                def body(i, b, pair, more):
                    for ch in range(CHUNKS):
                        v = i * CHUNKS + ch
                        o = act_out[ch % 2]
                        act.wait_ge(weighted, v + 1)
                        for j in range(acts):
                            bank = 2 * j if gated else j
                            act.wait_ge(up_out, v * UP + bank + 1)
                            act.activation(o[:, j, :], pu[bank][:, 0:CH], ACT.Silu).then_inc(act_done, 1)
                        act.wait_ge(weighted, v + 1 + 2)
                        act.activation(hhi[ch % 2][:, :, :], hid[ch % 2][:, :, :], ACT.Copy).then_inc(hi_ready, 1)

                whole(act, body)

            @block.vector
            def _(dve):
                dve.wait_ge(pick_loaded, 16)
                dve.tensor_copy(pick[:, :, :], pick_id[:, :].unsqueeze(2).to_broadcast([3 * EROWS, EROWS, P])).then_inc(pick_ready, 1)
                dve.sem_inc(weighted, 2)
                dve.sem_inc(act_done, acts)
                dve.sem_inc(added, 1)
                if gated:
                    dve.sem_inc(multiplied, 2)

                def weigh(i, ch):
                    v = i * CHUNKS + ch
                    q = ch % 2
                    if gated:
                        for a in range(2):
                            dve.wait_ge(act_done, v * acts + a + 1 + acts)
                            dve.wait_ge(up_out, v * UP + 2 * a + 2)
                            dve.tensor_tensor(act_out[q][:, a, :], pu[2 * a + 1][:, 0:CH], act_out[q][:, a, :],
                                              ALU.mult).then_inc(multiplied, 1)
                        dve.wait_ge(gate_out, v + 1)
                        for a in range(2):
                            dve.wait_ge(multiplied, v * 2 + a + 1 + 2)
                            last = dve.tensor_tensor(hid[q][:, a, :], pg[a][:, 0:CH], act_out[q][:, a, :], ALU.mult)
                        last.then_inc(weighted, 1)
                    else:
                        dve.wait_ge(act_done, v * acts + acts + acts)
                        dve.wait_ge(gate_out, v + 1)
                        dve.tensor_tensor(hid[q][:, :, :], act_out[q][:, :, :], over_halves(pg[q][:, 0:CH], DOWN),
                                          ALU.mult).then_inc(weighted, 1)
                    dve.wait_ge(hi_ready, v + 1)
                    dve.tensor_tensor(hlo[q][:, :, :], hid[q][:, :, :], hhi[q][:, :, :].bitcast(F32), ALU.subtract).then_inc(hid_split, 1)

                def add(i, ch):
                    dve.wait_ge(down_out, i * CHUNKS + ch + 1)
                    hv = c.h[:, :, ch * CH:(ch + 1) * CH]
                    dve.tensor_tensor(hv, pd[:, :, 0:CH], hv, ALU.add).then_inc(added, 1)

                weigh(0, 0)

                def body(i, b, pair, more):
                    for ch in range(CHUNKS):
                        if ch + 1 < CHUNKS:
                            weigh(i, ch + 1)
                        elif more:
                            weigh(i + 1, 0)
                        add(i, ch)

                whole(dve, body)



def phase_attention(nc, c):
    G = 4
    with ExitStack() as ctx:
        sb = lambda name, shape, dt=F32: ctx.enter_context(nc.sbuf_tensor(f"at_{name}", shape, dt))
        pb = lambda name, shape: ctx.enter_context(nc.psum_tensor(f"at_{name}", shape, F32))
        sem = lambda name: c.sem(f"at_{name}")
        c.xc, c.sq = [sb("xc", [P, KH, CH])], [sb("sq", [P, KH, CH])]
        c.std, c.rstd = [sb("std", [P, CH])], [sb("rstd", [P, CH])]
        wqkv = sb("wqkv", [P, 3, KH, 512])
        w_out = sb("w_out", [P, G, C])
        x64 = sb("x64", [P, KH, CH_IMAGES, QP])
        q64 = sb("q64", [P, G, CH_IMAGES, QP])
        kT = sb("kT", [P, G, CH])
        v2 = sb("v2", [P, PAIRS, 512])
        dif = [sb(f"dif{b}", [P, G, G, SEQ]) for b in range(2)]
        ex = [sb(f"ex{b}", [P, G, G, SEQ]) for b in range(2)]
        top = sb("top", [P, G, G])
        den = sb("den", [P, G, G])
        wts = [sb(f"wts{b}", [P, HEADS, 2 * QP]) for b in range(2)]
        wT = [sb(f"wT{b}", [P, HEADS, 2 * QP]) for b in range(2)]
        o_sq = sb("o_sq", [P, 512])
        o_ms = sb("o_ms", [P, PAIRS, HEADS])
        o_tok = sb("o_tok", [P, PAIRS, 512])
        o_n = sb("o_n", [P, PAIRS, 512])
        oT = sb("oT", [P, G, CH])
        gam = sb("gam", [P, 1])
        lam4 = sb("lam4", [P, 4, HD])
        lam_t = sb("lam_t", [P, 2, HD])
        lam_s = sb("lam_s", [P, 2])
        neg_lam = sb("neg_lam", [P, 1])
        ident = sb("ident", [P, P])
        score = pb("score", [P, G, 512])
        pu = pb("pu", [P, 2, 512])
        pw = pb("pw", [P, 2, 512])
        c.stat = [pw[:, 0, 0:CH]]
        banks = [pu[:, 0, :], pu[:, 1, :], pw[:, 0, :], pw[:, 1, :]]
        nm = c.norm("attn_norm")
        loaded, init, link_sem = sem("loaded"), sem("init"), sem("link")
        x_ready, qk_out, q_done, k_done, v_out, v_done = (
            sem("x_ready"), sem("qk_out"), sem("q_done"), sem("k_done"), sem("v_out"), sem("v_done"))
        scores_out, tops_found, topped, exp_done, wts_done, turned, wT_done = (
            sem("scores_out"), sem("tops_found"), sem("topped"), sem("exp_done"), sem("wts_done"), sem("turned"), sem("wT_done"))
        o_out, squared, o_copied, ms_done, rms_done, o_normed, oT_out, oT_done, proj_out, chunk_done = (
            sem("o_out"), sem("squared"), sem("o_copied"), sem("ms_done"), sem("rms_done"), sem("o_normed"),
            sem("oT_out"), sem("oT_done"), sem("proj_out"), sem("chunk_done"))
        consts_ready, steps, tail_steps = sem("consts_ready"), sem("steps"), sem("tail_steps")
        lam_ready, lam_exp = sem("lam_ready"), sem("lam_exp")
        d = c.dram
        LOADS = 6

        with nc.Block() as block:
            @block.sync
            def _(sp):
                sp.dma_start(wqkv[:, :, :, :], d["wqkv"]).then_inc(loaded, 16)
                sp.dma_start(w_out[:, :, :], d["w_out"]).then_inc(loaded, 16)
                sp.dma_start(ident[:, :], d["ident_f"]).then_inc(loaded, 16)
                sp.dma_start(lam4[:, :, :].rearrange("p a d -> p (a d)"), d["lambdas"].partition_broadcast(P)).then_inc(loaded, 16)
                for half in range(2):
                    sp.dma_start(gam[64 * half:64 * half + 64, :], d["gamma1"]).then_inc(loaded, 16)
                sp.dma_start(c.router1[:, :, :], d["router1"]).then_inc(c.late_loaded, 16)
                sp.dma_start(c.score_bias[:, :], d["score_bias"].partition_broadcast(GT)).then_inc(c.late_loaded, 16)

            @block.tensor
            def _(pe):
                pe.wait_ge(loaded, LOADS * 16)
                pe.wait_ge(consts_ready, 1)
                with pe.Fori(0, CHUNKS) as it:
                    n = it + 1
                    at = it * CH
                    pe.wait_ge(chunk_done, n)
                    norm_mean_pe(pe, c, nm, 0, [c.h[:, k, bass.ds(at, CH)] for k in range(KH)])
                    norm_var_pe(pe, c, nm, 0, n)
                    pe.wait_ge(nm.normed, n)
                    for g in range(4):
                        if g == 2:
                            pe.wait_ge(q_done, it * 2 + 1)
                        if g == 3:
                            pe.wait_ge(q_done, it * 2 + 2)
                        for mm in range(2):
                            m = (g % 2) * 2 + mm
                            for k in range(KH):
                                last = pe.matmul(banks[(g % 2) * 2 + mm][:, 0:CH], wqkv[:, g // 2, k, m * P:(m + 1) * P],
                                                 x64[:, k, :, 0:SEQ], start=(k == 0), stop=(k == KH - 1))
                        last.then_inc(qk_out, 1)
                    for p in range(PAIRS):
                        if p % 2 == 0:
                            pe.wait_ge(k_done, it * 2 + p // 2 + 1)
                        for k in range(KH):
                            last = pe.matmul(banks[p], x64[:, k, 2 * p:2 * p + 2, :].rearrange("p b t -> p (b t)"),
                                             wqkv[:, 2, k, :], start=(k == 0), stop=(k == KH - 1))
                        last.then_inc(v_out, 1)

                    def scores(p):
                        pe.wait_ge(topped, it * PAIRS + p + 1)
                        for b in range(2):
                            img = 2 * p + b
                            for m in range(G):
                                for g in range(G):
                                    last = pe.matmul(score[QP * b:QP * b + QP, g, m * SEQ:(m + 1) * SEQ],
                                                     q64[HD * g:HD * g + HD, m, img, :],
                                                     kT[HD * g:HD * g + HD, m, img * SEQ:(img + 1) * SEQ],
                                                     start=True, stop=True, tile_position=(HD * g, QP * b))
                        last.then_inc(scores_out, 1)

                    scores(0)
                    pe.wait_ge(v_done, it * PAIRS + PAIRS)
                    for p in range(PAIRS):
                        v = it * PAIRS + p
                        if p + 1 < PAIRS:
                            scores(p + 1)
                        pe.wait_ge(wts_done, v + 1)
                        if p:
                            pe.wait_ge(wT_done, v)
                        for h in range(HEADS):
                            last = pe.transpose(pu[:, h // 4, (h % 4) * P:(h % 4 + 1) * P], wts[p % 2][:, h, :], ident[:, :])
                        last.then_inc(turned, 1)
                        pe.wait_ge(wT_done, v + 1)
                        if p >= 2:
                            pe.wait_ge(o_copied, v - 1)
                        for h in range(HEADS):
                            hd = 2 * (h % 4) + h // 4
                            last = pe.matmul(pw[:, p % 2, hd * 64:(hd + 1) * 64], wT[p % 2][:, h, :],
                                             v2[:, p, hd * 64:(hd + 1) * 64], start=True, stop=True)
                        last.then_inc(o_out, 1)
                    for p in range(PAIRS):
                        pe.wait_ge(o_normed, it * PAIRS + p + 1)
                        for m in range(G):
                            last = pe.transpose(banks[p][:, m * P:(m + 1) * P], o_n[:, p, m * P:(m + 1) * P], ident[:, :])
                        last.then_inc(oT_out, 1)
                    pe.wait_ge(oT_done, it * PAIRS + PAIRS)
                    for m in range(KH):
                        for k in range(G):
                            last = pe.matmul(score[:, m, 0:CH], w_out[:, k, m * P:(m + 1) * P], oT[:, k, :],
                                             start=(k == 0), stop=(k == G - 1))
                    last.then_inc(proj_out, 1)

            @block.scalar
            def _(act):
                act.wait_ge(lam_ready, 1)
                act.activation(lam_s[:, :], lam_s[:, :], ACT.Exp).then_inc(lam_exp, 1)
                with act.Fori(0, CHUNKS) as it:
                    n = it + 1
                    norm_square_act(act, c, nm, 0, n)
                    norm_std_act(act, c, nm, 0, n)
                    for g in range(2):
                        act.wait_ge(qk_out, it * 4 + g + 1)
                        for mm in range(2):
                            last = act.activation(q64[:, 2 * g + mm, :, 0:SEQ],
                                                  banks[2 * g + mm][:, 0:CH].rearrange("p (b t) -> p b t", t=SEQ), ACT.Copy)
                        last.then_inc(q_done, 1)
                    for p in range(PAIRS):
                        act.wait_ge(v_out, it * PAIRS + p + 1)
                        act.activation(v2[:, p, :], banks[p], ACT.Copy).then_inc(v_done, 1)
                    for p in range(PAIRS):
                        v = it * PAIRS + p
                        act.wait_ge(topped, v + 2)
                        act.activation(ex[p % 2][:, :, :, :], dif[p % 2][:, :, :, :], ACT.Exp, scale=HD ** -0.5).then_inc(exp_done, 1)
                        act.wait_ge(turned, v + 1)
                        act.activation(wT[p % 2][:, :, :].rearrange("p (a h) q -> p a (h q)", a=2), pu[:, :, :], ACT.Copy).then_inc(wT_done, 1)
                        act.wait_ge(o_out, v + 1)
                        act.activation(o_tok[:, p, :], pw[:, p % 2, :], ACT.Copy).then_inc(o_copied, 1)
                        act.wait_ge(o_copied, v + 1)
                        if p:
                            act.wait_ge(ms_done, v)
                        act.activation(o_sq[:, :], o_tok[:, p, :], ACT.Square).then_inc(squared, 1)
                    act.wait_ge(ms_done, it * PAIRS + PAIRS)
                    act.activation(o_ms[:, :, :], o_ms[:, :, :], ACT.Sqrt, scale=1.0 / 64).then_inc(rms_done, 1)
                    for p in range(PAIRS):
                        act.wait_ge(oT_out, it * PAIRS + p + 1)
                        act.activation(oT[:, :, p * 2 * SEQ:(p + 1) * 2 * SEQ].rearrange("p m (b t) -> p m b t", t=SEQ),
                                       banks[p].rearrange("p (m b t) -> p m b t", m=G, b=2)[:, :, :, 0:SEQ],
                                       ACT.Copy).then_inc(oT_done, 1)

            @block.vector
            def _(dve):
                link = Link(dve, link_sem)
                for t in (x64, q64, wts[0], wts[1]):
                    dve.memset(t[:], 0.0).then_inc(init, 1)
                dve.sem_inc(chunk_done, 1)
                dve.sem_inc(topped, 1)
                dve.wait_ge(init, 4)
                dve.wait_ge(loaded, LOADS * 16)
                link(dve.tensor_tensor(lam_t[:, :, :], lam4[:, 0::2, :], lam4[:, 1::2, :], ALU.mult))
                dve.tensor_reduce(lam_s[:, :], lam_t[:, :, :], AX.X, ALU.add).then_inc(lam_ready, 1)
                dve.wait_ge(lam_exp, 1)
                link(dve.tensor_tensor(neg_lam[:, :], lam_s[:, 1:2], lam_s[:, 0:1], ALU.subtract))
                link(dve.tensor_scalar(neg_lam[:, :], neg_lam[:, :], -LAMBDA_INIT, None, ALU.add))
                link(dve.tensor_scalar(gam[:, :], gam[:, :], 1.0 - LAMBDA_INIT, None, ALU.mult))
                dve.tensor_scalar(w_out[:, :, :], w_out[:, :, :], gam[:, 0:1], None, ALU.mult).then_inc(consts_ready, 1)
                with dve.Fori(0, CHUNKS) as it:
                    n = it + 1
                    at = it * CH
                    norm_centre_dve(dve, c, nm, 0, n, c.h[:, :, bass.ds(at, CH)])
                    dve.wait_ge(nm.std_ready, n)
                    dve.reciprocal(c.rstd[0][:, :], c.std[0][:, :]).then_inc(nm.rstd_ready, 1)
                    dve.wait_ge(nm.rstd_ready, n)
                    im = lambda t: t.rearrange("p (b t) -> p b t", t=SEQ)
                    for k in range(KH):
                        last = dve.tensor_tensor(x64[:, k, :, 0:SEQ], im(c.xc[0][:, k, :]), im(c.rstd[0][:, :]), ALU.mult)
                    last.then_inc(nm.normed, 1)
                    for g in range(2):
                        dve.wait_ge(qk_out, it * 4 + 2 + g + 1)
                        dve.tensor_copy(kT[:, 2 * g:2 * g + 2, :], (pu if g == 0 else pw)[:, :, 0:CH]).then_inc(k_done, 1)

                    def less_top(p):
                        v = it * PAIRS + p
                        dve.wait_ge(scores_out, v + 1)
                        sc = score[:, :, 0:G * SEQ].rearrange("p g (m t) -> p g m t", t=SEQ)
                        dve.tensor_reduce(top[:, :, :], sc, AX.X, ALU.max).then_inc(tops_found, 1)
                        dve.wait_ge(tops_found, v + 1)
                        dve.tensor_tensor(dif[p % 2][:, :, :, :], sc, top[:, :, :].unsqueeze(3).to_broadcast([P, G, G, SEQ]),
                                          ALU.subtract).then_inc(topped, 1)

                    less_top(0)
                    for p in range(PAIRS):
                        v = it * PAIRS + p
                        if p + 1 < PAIRS:
                            less_top(p + 1)
                        e = ex[p % 2]
                        link = Link(dve, steps, v, 4)
                        dve.wait_ge(exp_done, v + 1)
                        link(dve.tensor_reduce(den[:, :, :], e[:, :, :, :], AX.X, ALU.add))
                        link(dve.reciprocal(den[:, :, :], den[:, :, :]))
                        link(dve.tensor_scalar(den[:, 1::2, :], den[:, 1::2, :], neg_lam[:, 0:1], None, ALU.mult))
                        link(dve.tensor_tensor(e[:, :, :, :], e[:, :, :, :], den[:, :, :].unsqueeze(3).to_broadcast([P, G, G, SEQ]), ALU.mult))
                        link.close()
                        for b in range(2):
                            rows = slice(QP * b, QP * b + QP)
                            last = dve.tensor_tensor(
                                wts[p % 2][rows, :, QP * b:QP * b + SEQ].rearrange("p (u m) t -> p u m t", u=2),
                                e[rows, 0::2, :, :], e[rows, 1::2, :, :], ALU.add)
                        last.then_inc(wts_done, 1)
                        dve.wait_ge(squared, v + 1)
                        dve.tensor_reduce(o_ms[:, p, :], o_sq[:, :].rearrange("p (h d) -> p h d", d=64), AX.X, ALU.add).then_inc(ms_done, 1)
                    dve.wait_ge(rms_done, n)
                    link = Link(dve, tail_steps, it, 2)
                    link(dve.tensor_scalar(o_ms[:, :, :], o_ms[:, :, :], 1e-8, None, ALU.add))
                    link(dve.reciprocal(o_ms[:, :, :], o_ms[:, :, :]))
                    link.close()
                    for p in range(PAIRS):
                        hd = lambda t: t[:, p, :].rearrange("p (h d) -> p h d", d=64)
                        dve.tensor_tensor(hd(o_n), hd(o_tok), o_ms[:, p, :].unsqueeze(2).to_broadcast([P, HEADS, 64]),
                                          ALU.mult).then_inc(o_normed, 1)
                    dve.wait_ge(proj_out, n)
                    hv = c.h[:, :, bass.ds(at, CH)]
                    dve.tensor_tensor(hv, score[:, 0:KH, 0:CH], hv, ALU.add).then_inc(chunk_done, 1)


def phase_store(nc, c):
    with nc.Block() as block:
        @block.sync
        def _(sp):
            for k in range(KH):
                sp.dma_start(c.dram["out"][k], c.h[:, k, :]).then_inc(c.stored, 16)
            sp.wait_ge(c.stored, 16 * KH)


def tower(nc, dram, stop="all"):
    with ExitStack() as ctx:
        sb = lambda name, shape, dt=F32: ctx.enter_context(nc.sbuf_tensor(name, shape, dt))
        c = Shared()
        c.dram = dram
        c.taken = []

        def sem(name):
            s = nc.alloc_semaphore(name)
            c.taken.append(s)
            return s

        c.sem = sem
        c.norm = lambda name: Norm(c.sem, name)
        c.h = sb("h", [P, KH, TOK])
        c.vec = sb("vec", [P, len(VEC) * KH])
        c.vcol = lambda name, k: c.vec[:, VEC[name] * KH + k:VEC[name] * KH + k + 1]
        c.mean_w = sb("mean_w", [P, P])
        c.eps = sb("eps", [P, 1])
        c.hi, c.lo = sb("hi", [P, KH, TOK], F32R), sb("lo", [P, KH, TOK], F32R)
        c.w_o = sb("w_o", [P, KH, C])
        c.router0, c.router1 = sb("router0", [P, KH, 8]), sb("router1", [P, KH, 32])
        c.escale, c.score_bias = sb("escale", [GT, 8]), sb("score_bias", [GT, 32])
        c.gates = sb("gates", [3 * EROWS, TOK], BF16)
        c.late_loaded, c.scan_tables_loaded = c.sem("late_loaded"), c.sem("scan_tables_loaded")
        c.passed = c.sem("passed")
        c.ident_loaded, c.stored = c.sem("ident_loaded"), c.sem("stored")
        c.late_count = {"route0": 3, "route1": 5}
        c.taken = []

        def phase(build, *args):
            build(nc, c, *args)
            nc.clear_and_free_semaphores(c.taken)
            nc.all_engine_barrier()
            c.taken = []

        with ExitStack() as rwkv:
            rb = lambda name, shape, dt=F32: rwkv.enter_context(nc.sbuf_tensor(name, shape, dt))
            c.r, c.k, c.w, c.y = (rb(name, [P, KH, TOK]) for name in ("r", "k", "w", "y"))
            c.red = rb("red", [P, HS, P])
            phase(phase_tokens)
            phase(phase_scan)
            phase(phase_route, "route0", 8, 2, True)
        if stop != "rwkv":
            phase(phase_experts, "moe0", 16, False, dram["moe0"])
            if stop != "moe0":
                phase(phase_attention)
                if stop != "attn":
                    phase(phase_route, "route1", 32, 6, False)
                    phase(phase_experts, "moe1", 17, True, dram["moe1"])
        phase_store(nc, c)


STOP = "all"


def kernel(**inputs):
    import numpy as np
    import concourse.bacc as bacc
    from concourse.bass_utils import run_bass_kernel_spmd

    nc = bacc.Bacc("TRN2", target_bir_lowering=False, num_devices=1)
    a = {name: np.asarray(x) for name, x in inputs.items()}
    f = np.float32

    def rows(w):
        return w.reshape(-1, P, w.shape[1]).transpose(1, 0, 2)

    put = {}
    x = a["x"].reshape(CHUNKS, CH_IMAGES, 3, 6, 16, 6, 16).transpose(0, 2, 4, 6, 1, 3, 5)
    put["patches"] = x.reshape(CHUNKS, PB, P, CH_IMAGES * PATCHES).transpose(0, 2, 1, 3)
    put["wtok"] = rows(a["L0_tok_W"])
    A0 = "L0_attn_time_"
    vectors = [a["L0_tok_b"], a["L0_tok_cls_token"], a["L0_tok_gamma"], a["L0_tok_beta"], a[A0 + "maa_x"], a[A0 + "maa_w"],
               a[A0 + "maa_k"], a[A0 + "maa_v"], a[A0 + "maa_r"], a[A0 + "decay"], a[A0 + "faaaa"],
               a["L0_attn_ln_g"], a["L0_attn_ln_b"]]
    put["vec"] = np.stack([v.reshape(KH, P) for v in vectors]).transpose(2, 0, 1).reshape(P, -1)
    put["pos"] = rows(a["L0_tok_pos_embedding"][0].T)
    put["mean_w"] = np.full((P, P), 1.0 / C, f)
    put["w_lora"] = rows(a[A0 + "maa_w1"])
    put["w_lora2"] = a[A0 + "maa_w2"].reshape(P, C)
    put["w_rkv"] = np.stack([rows(a["L0_attn_W_" + n]) for n in "rkv"], axis=1)
    put["w_decay"] = rows(a[A0 + "decay_w1"])
    put["w_decay2"] = a[A0 + "decay_w2"]
    put["w_o"] = rows(a["L0_attn_W_o"])
    row = np.arange(P)
    put["head_ones"] = (row[:, None] // HS == row[None, :] // HS).astype(f)
    same = row[:, None, None] // HS == row[None, None, :] // HS
    j = np.arange(HS)[None, :, None]
    put["sel"] = (same & (row[:, None, None] % HS == j)).astype(f)
    put["red"] = (same & (row[None, None, :] % HS == j)).astype(f)
    put["router0"] = rows(a["L0_ffn_router_w"].T)
    put["router1"] = rows(a["L1_ffn_router_weight"].T)
    put["escale"] = a["L0_ffn_expert_scale"].reshape(1, 8)
    put["score_bias"] = a["L1_ffn_e_score_bias"].reshape(1, 32)
    put["ident"] = np.eye(P, dtype=mybir.dt.np(BF16))
    put["ident_f"] = np.eye(P, dtype=f)
    part_row = np.arange(3 * EROWS)[:, None] % EROWS
    put["pick_id"] = (part_row == np.arange(EROWS)[None, :]).astype(mybir.dt.np(BF16))
    w1 = a["L0_ffn_w1"].reshape(8, 2, 512, KH, P).transpose(0, 1, 4, 3, 2)
    w2 = a["L0_ffn_w2"].reshape(8, C, 2, 4, P).transpose(0, 2, 4, 3, 1)
    put["moe0"] = np.concatenate([w1.reshape(16, P, -1), w2.reshape(16, P, -1)], axis=2)
    shared = np.stack([a["L1_ffn_shared_gate_w"].reshape(2, P, C), a["L1_ffn_shared_up_w"].reshape(2, P, C)], axis=1)
    up = np.concatenate([a["L1_ffn_gate_up_proj"], shared.reshape(2, 2 * P, C)])
    up = up.reshape(17, 512, KH, P).transpose(0, 3, 2, 1)
    down = np.concatenate([a["L1_ffn_down_proj"], a["L1_ffn_shared_down_w"].reshape(C, 2, P).transpose(1, 0, 2)])
    down = down.reshape(17, 2, C, P).transpose(0, 3, 1, 2)
    put["moe1"] = np.concatenate([up.reshape(17, P, -1), down.reshape(17, P, -1)], axis=2)
    wq, wkv = a["L1_attn_Wq"], a["L1_attn_Wkv"]
    put["wqkv"] = np.stack([rows(wq), rows(wkv[:, :512]), rows(wkv[:, 512:])], axis=1)
    put["w_out"] = rows(a["L1_attn_Wout"])
    put["lambdas"] = np.concatenate([a["L1_attn_lambda_" + n] for n in ("q1", "k1", "q2", "k2")]).reshape(1, 4 * HD)
    put["gamma1"] = a["L1_attn_gamma"].reshape(64, 1)

    arrays = {f"in_{name}": np.ascontiguousarray(v) for name, v in put.items()}
    dram = {name: nc.dram_tensor(f"in_{name}", v.shape, mybir.dt.from_np(v.dtype), kind="ExternalInput").ap()
            for name, v in ((n[3:], v) for n, v in arrays.items())}
    dram["out"] = nc.dram_tensor("out", (KH, P, TOK), F32, kind="ExternalOutput").ap()
    tower(nc, dram, STOP)
    out = run_bass_kernel_spmd(nc, [arrays], core_ids=[0]).results[0]["out"]
    return np.ascontiguousarray(out.reshape(C, IMAGES, SEQ).transpose(1, 2, 0))
```

```python
import concourse.bass as bass
from concourse import mybir
from contextlib import ExitStack

F32 = mybir.dt.float32
F32R = mybir.dt.float32r
BF16 = mybir.dt.bfloat16
ALU = mybir.AluOpType
ACT = mybir.ActivationFunctionType
AX = mybir.AxisListType

P = 128
IMAGES, SEQ, C = 32, 37, 256
PATCHES = SEQ - 1
TOK = IMAGES * SEQ
KH = C // P
CH_IMAGES = 8
CH = CH_IMAGES * SEQ
CHUNKS = IMAGES // CH_IMAGES
STREAMS = CHUNKS
PATCH_D = 768
PB = PATCH_D // P
HS = 16
LN_EPS = 1e-5
GT = 74
TILES = TOK // GT
EROWS = 34
E_AT = (0, 400, 792, TOK)
E_CHUNKS, E_MAX = len(E_AT) - 1, 400
RAW = KH * 512 + 4 * C
HEADS, HD = 8, 32
LAMBDA_INIT = 0.8 - 0.6 * 2.718281828459045 ** -0.3
PAIRS = IMAGES // 2
CHUNK_PAIRS = CH_IMAGES // 2
QP = 64
PAD_LOW, PICKED = -3.0e38, -3.2e38

VEC = {name: i for i, name in enumerate(
    ["tok_b", "cls", "tok_gamma", "tok_beta", "maa_x", "maa_w", "maa_k", "maa_v", "maa_r",
     "decay", "faaaa", "ln_g", "ln_b"])}


class Shared:
    pass


class Norm:

    def __init__(self, sem, name):
        self.mean_ready, self.centred, self.squared = sem(f"{name}_mean"), sem(f"{name}_centred"), sem(f"{name}_squared")
        self.var_ready, self.std_ready = sem(f"{name}_var"), sem(f"{name}_std")
        self.rstd_ready, self.diag_ready = sem(f"{name}_rstd"), sem(f"{name}_diag")
        self.spread, self.normed = sem(f"{name}_spread"), sem(f"{name}_normed")


class Routing:

    def __init__(self, sb, sem, E):
        self.m, self.a, self.e = sb("m", [GT, TILES]), sb("a", [GT, TILES, E]), sb("e", [GT, TILES, E])
        self.p, self.q = sb("p", [GT, TILES, E + 8]), sb("q", [GT, TILES, E + 8])
        self.top, self.take = sb("top", [GT, TILES, 8]), sb("take", [GT, TILES, 8])
        self.rest, self.picked = sb("rest", [GT, TILES, E + 8]), sb("picked", [GT, TILES, E])
        self.parts = sb("parts", [GT, TILES, 3 * EROWS], BF16)
        self.step, self.parts_ready = sem("step"), sem("parts_ready")


class Link:

    def __init__(self, eng, sem):
        self.eng, self.sem, self.n = eng, sem, 0

    def __call__(self, ins):
        self.n += 1
        ins.then_inc(self.sem, 1)
        self.eng.wait_ge(self.sem, self.n)


def wait_alone(c, eng, sem, value):
    eng.wait_ge(sem, value)
    eng.sem_inc(c.passed, 1)


def over_halves(ap, k=KH):
    return ap.unsqueeze(1).to_broadcast([ap.shape[0], k, ap.shape[1]])



def norm_mean_pe(pe, c, nm, s, halves):
    for k in range(KH):
        last = pe.matmul(c.stat[s], c.mean_w[:, :], halves[k], start=(k == 0), stop=(k == KH - 1))
    last.then_inc(nm.mean_ready, 1)


def norm_var_pe(pe, c, nm, s, n):
    pe.wait_ge(nm.squared, n)
    for t in range(CH // GT):
        for k in range(KH):
            last = pe.matmul(c.var[s][:, t:t + 1], c.sq[s][:, k, t * GT:(t + 1) * GT], c.mean_w[:, 0:1],
                             start=(k == 0), stop=(k == KH - 1))
    last.then_inc(nm.var_ready, 1)


def norm_spread_pe(pe, c, nm, s, n):
    pe.wait_ge(nm.diag_ready, n)
    pe.matmul(c.stat[s], c.mean_w[0:GT, :], c.diag[s][:, :, :].rearrange("p t q -> p (t q)"),
              start=True, stop=True).then_inc(nm.spread, 1)


def norm_centre_dve(dve, c, nm, s, n, src):
    dve.wait_ge(nm.mean_ready, n)
    dve.tensor_tensor(c.xc[s][:, :, :], src, over_halves(c.stat[s]), ALU.subtract).then_inc(nm.centred, 1)


def norm_square_act(act, c, nm, s, n):
    act.wait_ge(nm.centred, n)
    act.activation(c.sq[s][:, :, :], c.xc[s][:, :, :], ACT.Square).then_inc(nm.squared, 1)


def norm_std_act(act, c, nm, s, n):
    act.wait_ge(nm.var_ready, n)
    act.activation(c.std[s][:, :], c.var[s], ACT.Sqrt, bias=c.eps[0:GT, :]).then_inc(nm.std_ready, 1)


def norm_diag_dve(dve, c, nm, s, n):
    dve.wait_ge(nm.std_ready, n)
    dve.reciprocal(c.std[s][:, :], c.std[s][:, :]).then_inc(nm.rstd_ready, 1)
    dve.wait_ge(nm.rstd_ready, n)
    dve.tensor_tensor(c.diag[s][:, :, :], c.ident_c[:, :].unsqueeze(1).to_broadcast([GT, CH // GT, GT]),
                      c.std[s][:, :].unsqueeze(2).to_broadcast([GT, CH // GT, GT]), ALU.mult).then_inc(nm.diag_ready, 1)


def norm_scale_dve(dve, c, nm, s, n, out):
    dve.wait_ge(nm.spread, n)
    dve.tensor_tensor(out, c.xc[s][:, :, :], over_halves(c.stat[s]), ALU.mult).then_inc(nm.normed, 1)


def staggered(stages):
    for t in range(STREAMS + max(lag for lag, stage in stages)):
        for lag, stage in sorted(stages, key=lambda x: -x[0]):
            if 0 <= t - lag < STREAMS:
                stage(t - lag)


def in_turn(stages):
    for lag, stage in stages:
        for s in range(STREAMS):
            stage(s)


def norm_stages_pe(pe, c, nm, lag, halves):
    return [(lag, lambda s: norm_mean_pe(pe, c, nm, s, halves(s))),
            (lag + 1, lambda s: norm_var_pe(pe, c, nm, s, s + 1)),
            (lag + 2, lambda s: norm_spread_pe(pe, c, nm, s, s + 1))]


def norm_stages_act(act, c, nm, lag):
    return [(lag, lambda s: norm_square_act(act, c, nm, s, s + 1)),
            (lag + 1, lambda s: norm_std_act(act, c, nm, s, s + 1))]


def norm_stages_dve(dve, c, nm, lag, source, scale):
    return [(lag, lambda s: norm_centre_dve(dve, c, nm, s, s + 1, source(s))),
            (lag + 1, lambda s: norm_diag_dve(dve, c, nm, s, s + 1)),
            (lag + 2, scale)]


def setup_stream_buffers(ctx, nc, c, tag, area=None):
    sb = lambda name, shape, dt=F32: ctx.enter_context(nc.sbuf_tensor(f"{tag}_{name}", shape, dt))
    if area is None:
        c.xc, c.sq, c.xn = ([sb(f"{name}{s}", [P, KH, CH]) for s in range(STREAMS)] for name in ("xc", "sq", "xn"))
    else:
        c.xc, c.sq, c.xn = ([area[:, (i * STREAMS + s) * KH * CH:(i * STREAMS + s + 1) * KH * CH]
                             .rearrange("p (k n) -> p k n", k=KH) for s in range(STREAMS)] for i in range(3))
    c.std = [sb(f"std{s}", [GT, CH // GT]) for s in range(STREAMS)]
    c.diag = [sb(f"diag{s}", [GT, CH // GT, GT]) for s in range(STREAMS)]
    c.ps = [ctx.enter_context(nc.psum_tensor(f"{tag}_ps{s}", [P, 2, 512], F32)) for s in range(STREAMS)]
    c.stat = [c.ps[s][:, 0, 0:CH] for s in range(STREAMS)]
    c.var = [c.ps[s][0:GT, 0, CH:CH + CH // GT] for s in range(STREAMS)]



def phase_tokens(nc, c):
    with ExitStack() as ctx:
        sb = lambda name, shape, dt=F32: ctx.enter_context(nc.sbuf_tensor(name, shape, dt))
        setup_stream_buffers(ctx, nc, c, "tk")
        S2 = range(STREAMS)
        wtok = sb("wtok", [P, PB, C])
        pos = sb("pos", [P, KH, SEQ])
        patches = [t[:, :, :].rearrange("p k n -> p (k n)")[:, 0:PB * CH_IMAGES * PATCHES].rearrange("p (b n) -> p b n", b=PB)
                   for t in (c.r, c.k, c.w, c.y)]
        xn = c.xn
        xx = [sb(f"xx{s}", [P, KH, CH]) for s in S2]
        h0 = xx
        mixed = [sb(f"mixed{s}", [P, KH, CH]) for s in S2]
        xf = [sb(f"xf{s}", [P, KH, CH]) for s in S2]
        tanh_m = [sb(f"tanh_m{s}", [P, CH]) for s in S2]
        tanh_d = [sb(f"tanh_d{s}", [64, CH]) for s in S2]
        vf = [sb(f"vf{s}", [P, KH, CH]) for s in S2]
        w_lora = sb("w_lora", [P, KH, P])
        w_lora2 = sb("w_lora2", [P, C])
        w_rkv = sb("w_rkv", [P, 3, KH, C])
        w_decay = sb("w_decay", [P, KH, 64])
        w_decay2 = sb("w_decay2", [64, C])
        head_ones = sb("head_ones", [P, P])
        pick_id = sb("pick_id", [3 * EROWS, EROWS], BF16)
        sem = c.sem
        embed_loaded = [sem(f"embed_loaded{half}") for half in range(2)]
        PB_HALVES = (slice(0, PB // 2), slice(PB // 2, PB))
        norm_loaded, consts_loaded = sem("norm_loaded"), sem("mix_w_loaded")
        x_loaded = [sem(f"x_loaded{s}") for s in S2]
        tok_mm, tokens_ready, pos_ready, h_ready = sem("tok_mm"), sem("tokens_ready"), sem("pos_ready"), sem("h_ready")
        n0, n1 = c.norm("tok_norm"), c.norm("rwkv_norm")
        shifted, xxx_ready = sem("shifted"), sem("xxx_ready")
        lora_ready, tanh_ready = sem("lora_ready"), sem("tanh_ready")
        mix_ready, mix_applied, xf_ready, proj_ready, evacuated = (
            sem("mix_ready"), sem("mix_applied"), sem("xf_ready"), sem("proj_ready"), sem("evacuated"))
        decay1_ready, decay_tanh, decay_done = sem("decay1_ready"), sem("decay_tanh"), sem("decay_done")
        v_hi_done, v_lo_done = sem("v_hi_done"), sem("v_lo_done")
        ruk_ready, bonus_mm, bonus_done = sem("ruk_ready"), sem("bonus_mm"), sem("bonus_done")
        start_ready = sem("start_ready")
        pick_loaded, pick_ready = sem("pick_loaded"), sem("pick_ready")
        d = c.dram
        MIX = [("maa_w", 0), ("maa_k", 1), ("maa_v", 2), ("maa_r", 3)]
        RKV = {"maa_r": 0, "maa_k": 1, "maa_v": 2}

        with nc.Block() as block:
            @block.sync
            def _(sp):
                for half, ks in enumerate(PB_HALVES):
                    sp.dma_start(wtok[:, ks, :], d["wtok"][:, ks]).then_inc(embed_loaded[half], 16)
                    sp.dma_start(patches[0][:, ks, :], d["patches"][0][:, ks]).then_inc(embed_loaded[half], 16)
                for dst, src in ((c.vec[:, :], d["vec"]), (pos[:, :, :], d["pos"]),
                                 (c.mean_w[:, :], d["mean_w"]), (c.ident_c[:, :], d["ident_c"])):
                    sp.dma_start(dst, src).then_inc(norm_loaded, 16)
                for s in S2[1:]:
                    sp.dma_start(patches[s], d["patches"][s]).then_inc(x_loaded[s], 16)
                for dst, src in ((w_lora[:, :, :], d["w_lora"]),
                                 (w_lora2[:, :], d["w_lora2"]), (w_rkv[:, :, :, :], d["w_rkv"]),
                                 (w_decay[:, :, :], d["w_decay"]), (w_decay2[:, :], d["w_decay2"]),
                                 (head_ones[:, :], d["head_ones"])):
                    sp.dma_start(dst, src).then_inc(consts_loaded, 16)
                sp.dma_start(pick_id[:, :], d["pick_id"]).then_inc(pick_loaded, 16)
                sp.dma_start(c.w_o[:, :, :], d["w_o"]).then_inc(c.late_loaded, 16)
                sp.dma_start(c.router0[:, :, :], d["router0"]).then_inc(c.late_loaded, 16)
                sp.dma_start(c.escale[:, :], d["escale"].partition_broadcast(GT)).then_inc(c.late_loaded, 16)
                sp.dma_start(c.red[:, :, :], d["red"]).then_inc(c.scan_tables_loaded, 16)
                load_first_units_sp(sp, c, d["moe0"])
            CONSTS, NORM_CONSTS = 6 * 16, 4 * 16

            @block.tensor
            def _(pe):
                n = [s + 1 for s in S2]
                def embed(s):
                    for half, ks in enumerate(PB_HALVES):
                        if s == 0:
                            pe.wait_ge(embed_loaded[half], 32)
                        elif half == 0:
                            pe.wait_ge(x_loaded[s], 16)
                        for m in range(KH):
                            for k in range(ks.start, ks.stop):
                                last = pe.matmul(c.ps[s][:, m, 0:CH_IMAGES * PATCHES], wtok[:, k, m * P:(m + 1) * P],
                                                 patches[s][:, k, :], start=(k == 0), stop=(k == PB - 1))
                    last.then_inc(tok_mm, 1)

                def tokens_of(s):
                    pe.wait_ge(norm_loaded, NORM_CONSTS)
                    pe.wait_ge(tokens_ready, n[s])
                    return [h0[s][:, k, :] for k in range(KH)]

                def residual_of(s):
                    pe.wait_ge(h_ready, n[s])
                    return [c.h[:, k, s * CH:(s + 1) * CH] for k in range(KH)]

                def lora(s):
                    pe.wait_ge(consts_loaded, CONSTS)
                    pe.wait_ge(xxx_ready, n[s])
                    for k in range(KH):
                        last = pe.matmul(c.ps[s][:, 0, 0:CH], w_lora[:, k, :], xf[s][:, k, :],
                                         start=(k == 0), stop=(k == KH - 1))
                    last.then_inc(lora_ready, 1)

                def mix(f, s):
                    row = MIX[f][1]
                    if f == 0:
                        pe.wait_ge(tanh_ready, n[s])
                    else:
                        pe.wait_ge(evacuated, (f - 1) * STREAMS + s + 1)
                    for m in range(KH):
                        last = pe.matmul(c.ps[s][:, m, 0:CH], w_lora2[32 * row:32 * row + 32, m * P:(m + 1) * P],
                                         tanh_m[s][32 * row:32 * row + 32, :], start=True, stop=True)
                    last.then_inc(mix_ready, 1)

                def project(f, s):
                    pe.wait_ge(xf_ready, f * STREAMS + s + 1)
                    if f == 0:
                        for k in range(KH):
                            last = pe.matmul(c.ps[s][0:64, 0, 0:CH], w_decay[:, k, :], xf[s][:, k, :],
                                             start=(k == 0), stop=(k == KH - 1))
                        last.then_inc(decay1_ready, 1)
                    else:
                        for m in range(KH):
                            for k in range(KH):
                                last = pe.matmul(c.ps[s][:, m, 0:CH], w_rkv[:, RKV[MIX[f][0]], k, m * P:(m + 1) * P],
                                                 xf[s][:, k, :], start=(k == 0), stop=(k == KH - 1))
                        last.then_inc(proj_ready, 1)

                in_turn([(0, embed)] + norm_stages_pe(pe, c, n0, 1, tokens_of) + norm_stages_pe(pe, c, n1, 4, residual_of) +
                          [(7, lora), (8, lambda s: mix(0, s)), (9, lambda s: project(0, s))])
                for s in S2:
                    pe.wait_ge(decay_tanh, n[s])
                    for m in range(KH):
                        last = pe.matmul(c.ps[s][:, m, 0:CH], w_decay2[:, m * P:(m + 1) * P],
                                         tanh_d[s][:, :], start=True, stop=True)
                    last.then_inc(proj_ready, 1)
                AHEAD = 3
                order = [(f, s) for f in range(1, 4) for s in S2]
                for i in range(len(order) + AHEAD):
                    if i >= AHEAD:
                        project(*order[i - AHEAD])
                    if i < len(order):
                        mix(*order[i])
                for s in S2:
                    pe.wait_ge(ruk_ready, n[s])
                    for m in range(KH):
                        last = pe.matmul(c.ps[s][:, m, 0:CH], head_ones[:, :], mixed[s][:, m, :], start=True, stop=True)
                    last.then_inc(bonus_mm, 1)

            @block.vector
            def _(dve):
                dve.memset(c.eps[:, :], LN_EPS).then_inc(start_ready, 1)
                dve.wait_ge(norm_loaded, NORM_CONSTS)
                for k in range(KH):
                    dve.tensor_scalar(pos[:, k, 1:SEQ], pos[:, k, 1:SEQ], c.vcol("tok_b", k), None, ALU.add).then_inc(pos_ready, 1)
                    dve.tensor_scalar(pos[:, k, 0:1], pos[:, k, 0:1], c.vcol("cls", k), None, ALU.add).then_inc(pos_ready, 1)
                dve.wait_ge(pos_ready, 2 * KH)
                n = [s + 1 for s in S2]
                at = [slice(s * CH, (s + 1) * CH) for s in S2]
                def tokens(s):
                    dve.wait_ge(tok_mm, n[s])
                    hv = h0[s][:, :, :].rearrange("p k (b t) -> p k b t", t=SEQ)
                    for k in range(KH):
                        dve.tensor_tensor(hv[:, k, :, 1:SEQ],
                                          c.ps[s][:, k, 0:CH_IMAGES * PATCHES].rearrange("p (b t) -> p b t", t=PATCHES),
                                          pos[:, k, 1:SEQ].unsqueeze(1).to_broadcast([P, CH_IMAGES, PATCHES]), ALU.add)
                    dve.tensor_copy(hv[:, :, :, 0], pos[:, :, 0:1].to_broadcast([P, KH, CH_IMAGES])).then_inc(tokens_ready, 1)

                def tokens_of(s):
                    return h0[s][:, :, :]

                def residual(s):
                    norm_scale_dve(dve, c, n0, s, n[s], xn[s][:, :, :])
                    dve.wait_ge(n0.normed, n[s])
                    for k in range(KH):
                        last = dve.tensor_scalar(c.h[:, k, at[s]], xn[s][:, k, :], c.vcol("tok_gamma", k),
                                                 c.vcol("tok_beta", k), ALU.mult, ALU.add)
                    last.then_inc(h_ready, 1)

                def residual_of(s):
                    dve.wait_ge(h_ready, n[s])
                    return c.h[:, :, at[s]]

                def mix_input(s):
                    norm_scale_dve(dve, c, n1, s, n[s], xn[s][:, :, :])
                    dve.wait_ge(n1.normed, n[s])
                    xv, yv = (t[s][:, :, :].rearrange("p k (b t) -> p k b t", t=SEQ) for t in (xn, xx))
                    dve.tensor_tensor(yv[:, :, :, 1:SEQ], xv[:, :, :, 0:SEQ - 1], xv[:, :, :, 1:SEQ], ALU.subtract)
                    dve.tensor_scalar(yv[:, :, :, 0:1], xv[:, :, :, 0:1], -1.0, None, ALU.mult).then_inc(shifted, 1)
                    dve.wait_ge(shifted, n[s])
                    for k in range(KH):
                        last = dve.scalar_tensor_tensor(xf[s][:, k, :], xx[s][:, k, :], c.vcol("maa_x", k), xn[s][:, k, :],
                                                        ALU.mult, ALU.add)
                    last.then_inc(xxx_ready, 1)

                def apply_mix(f, s):
                    dve.wait_ge(mix_ready, f * STREAMS + s + 1)
                    if f:
                        dve.wait_ge(xf_ready, (f - 1) * STREAMS + s + 1)
                    for k in range(KH):
                        last = dve.scalar_tensor_tensor(mixed[s][:, k, :], c.ps[s][:, k, 0:CH], c.vcol(MIX[f][0], k),
                                                        xx[s][:, k, :], ALU.add, ALU.mult)
                    last.then_inc(mix_applied, 1)

                in_turn([(0, tokens)] + norm_stages_dve(dve, c, n0, 1, tokens_of, residual) +
                          norm_stages_dve(dve, c, n1, 4, residual_of, mix_input) + [(8, lambda s: apply_mix(0, s))])
                for f in range(1, 4):
                    for s in S2:
                        apply_mix(f, s)
                for s in S2:
                    dve.wait_ge(evacuated, 3 * STREAMS + s + 1)
                    dve.wait_ge(xf_ready, 3 * STREAMS + s + 1)
                    for k in range(KH):
                        last = dve.scalar_tensor_tensor(mixed[s][:, k, :], c.r[:, k, at[s]], c.vcol("faaaa", k),
                                                        c.k[:, k, at[s]], ALU.mult, ALU.mult)
                    last.then_inc(ruk_ready, 1)
                for s in S2:
                    dve.wait_ge(bonus_mm, n[s])
                    dve.wait_ge(v_lo_done, n[s])
                    dve.wait_ge(decay_done, n[s])
                    dve.tensor_tensor(c.y[:, :, at[s]], c.ps[s][:, :, 0:CH], vf[s][:, :, :],
                                      ALU.mult).then_inc(bonus_done, 1)

            @block.scalar
            def _(act):
                act.wait_ge(start_ready, 1)
                act.wait_ge(norm_loaded, NORM_CONSTS)
                n = [s + 1 for s in S2]
                at = [slice(s * CH, (s + 1) * CH) for s in S2]
                def tanh_mix(s):
                    act.wait_ge(lora_ready, n[s])
                    act.activation(tanh_m[s][:, :], c.ps[s][:, 0, 0:CH], ACT.Tanh).then_inc(tanh_ready, 1)

                in_turn(norm_stages_act(act, c, n0, 1) + norm_stages_act(act, c, n1, 4) + [(7, tanh_mix)])
                for s in S2:
                    act.wait_ge(decay1_ready, n[s])
                    act.activation(tanh_d[s][:, :], c.ps[s][0:64, 0, 0:CH], ACT.Tanh).then_inc(decay_tanh, 1)
                for s in S2:
                    act.wait_ge(proj_ready, s + 1)
                    for k in range(KH):
                        last = act.activation(c.sq[s][:, k, :], c.ps[s][:, k, 0:CH], ACT.Exp, bias=c.vcol("decay", k))
                    last.then_inc(evacuated, 1)
                for s in S2:
                    act.wait_ge(evacuated, s + 1)
                    act.activation(c.w[:, :, at[s]], c.sq[s][:, :, :], ACT.Exp, scale=-1.0).then_inc(decay_done, 1)
                for f, dst in ((1, c.k), (2, None), (3, c.r)):
                    for s in S2:
                        act.wait_ge(proj_ready, f * STREAMS + s + 1)
                        out = vf[s][:, :, :] if dst is None else dst[:, :, at[s]]
                        if f == 2:
                            act.activation(c.hi[:, :, at[s]], c.ps[s][:, :, 0:CH], ACT.Copy).then_inc(v_hi_done, 1)
                        act.activation(out, c.ps[s][:, :, 0:CH], ACT.Copy).then_inc(evacuated, 1)

            @block.gpsimd
            def _(pool):
                at = [slice(s * CH, (s + 1) * CH) for s in S2]
                pool.wait_ge(pick_loaded, 16)
                pool.tensor_copy(c.pick[:, :, :], pick_id[:, :].unsqueeze(2).to_broadcast([3 * EROWS, EROWS, P])).then_inc(pick_ready, 1)
                for f in range(4):
                    for s in S2:
                        pool.wait_ge(mix_applied, f * STREAMS + s + 1)
                        if f == 0:
                            pool.wait_ge(lora_ready, s + 1)
                        elif f == 1:
                            pool.wait_ge(decay1_ready, s + 1)
                        else:
                            pool.wait_ge(proj_ready, (f - 1) * STREAMS + s + 1)
                        pool.tensor_tensor(xf[s][:, :, :], mixed[s][:, :, :], xn[s][:, :, :], ALU.add).then_inc(xf_ready, 1)
                for s in S2:
                    pool.wait_ge(evacuated, 2 * STREAMS + s + 1)
                    pool.wait_ge(v_hi_done, s + 1)
                    pool.tensor_tensor(c.lo[:, :, at[s]], vf[s][:, :, :],
                                       c.hi[:, :, at[s]].bitcast(F32), ALU.subtract).then_inc(v_lo_done, 1)



def phase_scan(nc, c):
    SPAN = 2 * CH
    BANKS = 3
    KV_FREE = 4
    SLOTS = 4
    with ExitStack() as ctx:
        sb = lambda name, shape, dt=F32: ctx.enter_context(nc.sbuf_tensor(name, shape, dt))
        sem = c.sem
        kv = [sb(f"kv{b}", [P, SPAN]) for b in range(SLOTS)]
        state = [sb(f"state{b}", [P, SPAN]) for b in range(SLOTS)]
        rs = [sb(f"rs{b}", [P, SPAN]) for b in range(SLOTS)]
        sel = sb("sel_r", [P, HS, P], F32R)
        pv = [ctx.enter_context(nc.psum_tensor(f"pv{b}", [P, 2, 512], F32)) for b in range(BANKS)]
        py = ctx.enter_context(nc.psum_tensor("py", [P, 2, 512], F32))
        v_out, kv_ready, scanned, rs_ready, summed, y_done = (
            sem("v_out"), sem("kv_ready"), sem("scanned"), sem("rs_ready"), sem("summed"), sem("y_done"))
        sel_ready, w_zeroed = sem("sel_ready"), sem("w_zeroed")
        flat = lambda t: t[:, :, :].rearrange("p k n -> p (k n)")
        HALVES = KH * TOK // SPAN
        bank = lambda j: 1 if j == HS - 1 else j % BANKS

        def halves(eng, body):
            body(0, True, False)
            with eng.Fori(0, HALVES - 2) as it:
                body(it + 1, False, False)
            body(HALVES - 1, False, True)

        with nc.Block() as block:
            @block.tensor
            def _(pe):
                pe.wait_ge(sel_ready, 16)
                pe.wait_ge(c.scan_tables_loaded, 16)

                def repeat_v(i, j):
                    held = max([x for x in range(j) if bank(x) == bank(j)] or
                               [x - HS for x in range(HS) if bank(x) == bank(j)])
                    pe.wait_ge(kv_ready, i * HS + (held + 1 + KV_FREE))
                    for q in range(2):
                        for a, part in enumerate((c.hi, c.lo)):
                            at = i * SPAN + q * CH
                            last = pe.matmul(pv[bank(j)][:, q, 0:CH], sel[:, j, :],
                                             flat(part)[:, at:at + CH] if isinstance(at, int) else flat(part)[:, bass.ds(at, CH)],
                                             start=(a == 0), stop=(a == 1))
                    last.then_inc(v_out, 1)

                def reduce_rows(i, j):
                    pe.wait_ge(rs_ready, i * HS + (j + 1 + SLOTS))
                    if j == 0:
                        pe.wait_ge(y_done, i + 1)
                    for q in range(2):
                        last = pe.matmul(py[:, q, 0:CH], c.red[:, j, :], rs[j % SLOTS][:, q * CH:(q + 1) * CH],
                                         start=(j == 0), stop=(j == HS - 1))
                    last.then_inc(summed, 1)

                def body(i, first, last):
                    for j in range(HS):
                        if j + 2 < HS:
                            repeat_v(i, j + 2)
                        elif not last:
                            repeat_v(i + 1, j + 2 - HS)
                        if j > 0:
                            reduce_rows(i, j - 1)
                        elif not first:
                            reduce_rows(i - 1, HS - 1)
                    if last:
                        reduce_rows(i, HS - 1)

                repeat_v(0, 0)
                repeat_v(0, 1)
                halves(pe, body)

            @block.vector
            def _(dve):
                dve.sem_inc(kv_ready, KV_FREE)
                dve.sem_inc(y_done, 1)
                dve.sem_inc(summed, SLOTS)
                dve.memset(c.w[:, :, :].rearrange("p k (b t) -> p (k b) t", t=SEQ)[:, :, 0:1], 0.0).then_inc(w_zeroed, 1)
                dve.wait_ge(w_zeroed, 1)
                span = lambda t, i: (flat(t)[:, i * SPAN:(i + 1) * SPAN] if isinstance(i, int)
                                     else flat(t)[:, bass.ds(i * SPAN, SPAN)])
                by_bank = lambda ap: ap.rearrange("p (q n) -> p q n", q=2)

                def times_k(i, j):
                    dve.wait_ge(v_out, i * HS + (j + 1))
                    dve.tensor_tensor(by_bank(kv[j % SLOTS][:, :]), pv[bank(j)][:, :, 0:CH], by_bank(span(c.k, i)),
                                      ALU.mult).then_inc(kv_ready, 1)

                def take_y(i):
                    dve.wait_ge(summed, i * HS + (HS + SLOTS))
                    dve.tensor_tensor(by_bank(span(c.y, i)), py[:, :, 0:CH], by_bank(span(c.y, i)), ALU.add).then_inc(y_done, 1)

                def body(i, first, last):
                    for j in range(HS):
                        if j + 1 < HS:
                            times_k(i, j + 1)
                        elif not last:
                            times_k(i + 1, 0)
                        dve.wait_ge(kv_ready, i * HS + (j + 1 + KV_FREE))
                        dve.wait_ge(rs_ready, i * HS + (j + 1))
                        dve.tensor_tensor_scan(state[j % SLOTS][:, :], span(c.w, i), kv[j % SLOTS][:, :], 0.0,
                                               op0=ALU.mult, op1=ALU.add).then_inc(scanned, 1)
                        if j == 1 and not first:
                            take_y(i - 1)
                    if last:
                        take_y(i)

                times_k(0, 0)
                halves(dve, body)

            @block.gpsimd
            def _(pool):
                pool.dma_start(sel[:, :, :], c.dram["sel"]).then_inc(sel_ready, 16)
                for b in range(SLOTS):
                    pool.memset(rs[b][:, :], 0.0).then_inc(rs_ready, 1)
                pool.wait_ge(rs_ready, SLOTS)
                with pool.Fori(0, HALVES) as i:
                    for j in range(HS):
                        pool.wait_ge(scanned, i * HS + j + 1)
                        wait_alone(c, pool, summed, i * HS + j + 1)
                        im = lambda t: t[:, :].rearrange("p (b t) -> p b t", t=SEQ)
                        rv = flat(c.r)[:, bass.ds(i * SPAN, SPAN)].rearrange("p (b t) -> p b t", t=SEQ)
                        pool.tensor_tensor(im(rs[j % SLOTS])[:, :, 1:SEQ], im(state[j % SLOTS])[:, :, 0:SEQ - 1], rv[:, :, 1:SEQ],
                                           ALU.mult).then_inc(rs_ready, 1)



def gate_weights_dve(dve, act_sems, c, r, experts, top, logits):
    exp_in, exp_out = act_sems
    E, T = experts, TILES
    link = Link(dve, r.step)
    two = top == 2
    ex = lambda ap: ap.unsqueeze(2).to_broadcast([GT, T, E])
    link(dve.tensor_reduce(r.m[:, :], logits, AX.X, ALU.max))
    dve.tensor_tensor(r.a[:, :, 0:E], logits, ex(r.m[:, :]), ALU.subtract).then_inc(exp_in, 1)
    dve.wait_ge(exp_out, 1)
    link(dve.tensor_reduce(r.m[:, :], r.e[:, :, 0:E], AX.X, ALU.add))
    link(dve.reciprocal(r.m[:, :], r.m[:, :]))
    link(dve.tensor_tensor(r.p[:, :, 0:E], r.e[:, :, 0:E], ex(r.m[:, :]), ALU.mult))
    if two:
        chosen_from = r.p
    else:
        link(dve.tensor_tensor(r.q[:, :, 0:E], r.p[:, :, 0:E],
                               c.score_bias[:, :].unsqueeze(1).to_broadcast([GT, T, E]), ALU.add))
        chosen_from = r.q
    for t in range(T):
        last = dve.max(r.top[:, t, :], chosen_from[:, t, 0:E])
    link(last)
    link(dve.tensor_copy(r.take[:, :, 0:top], r.top[:, :, 0:top]))
    for t in range(T):
        last = dve.match_replace(r.rest[:, t, 0:E + 8], r.take[:, t, :], chosen_from[:, t, 0:E + 8], PICKED)
    link(last)
    link(dve.tensor_scalar(r.picked[:, :, 0:E], r.rest[:, :, 0:E], PICKED, None, ALU.is_equal))
    if two:
        dve.tensor_tensor(r.a[:, :, 0:E], r.p[:, :, 0:E], ex(r.top[:, :, 0]), ALU.subtract).then_inc(exp_in, 1)
        dve.wait_ge(exp_out, 2)
        link(dve.tensor_tensor(r.a[:, :, 0:E], r.e[:, :, 0:E], r.picked[:, :, 0:E], ALU.mult))
    else:
        link(dve.tensor_tensor(r.a[:, :, 0:E], r.p[:, :, 0:E], r.picked[:, :, 0:E], ALU.mult))
    link(dve.tensor_reduce(r.m[:, :], r.a[:, :, 0:E], AX.X, ALU.add))
    if not two:
        link(dve.tensor_scalar(r.m[:, :], r.m[:, :], 1e-12, None, ALU.max))
    link(dve.reciprocal(r.m[:, :], r.m[:, :]))
    link(dve.tensor_tensor(r.a[:, :, 0:E], r.a[:, :, 0:E], ex(r.m[:, :]), ALU.mult))
    if two:
        link(dve.tensor_tensor(r.a[:, :, 0:E], r.a[:, :, 0:E],
                               c.escale[:, :].unsqueeze(1).to_broadcast([GT, T, E]), ALU.mult))
    part = lambda i: r.parts[:, :, i * EROWS:i * EROWS + E]
    link(dve.tensor_copy(part(0), r.a[:, :, 0:E]))
    link(dve.tensor_tensor(r.a[:, :, 0:E], r.a[:, :, 0:E], part(0), ALU.subtract))
    link(dve.tensor_copy(part(1), r.a[:, :, 0:E]))
    dve.tensor_tensor(part(2), r.a[:, :, 0:E], part(1), ALU.subtract).then_inc(r.parts_ready, 1)


def phase_route(nc, c, tag, experts, top, rwkv_out, next_weights=None):
    S2 = range(STREAMS)
    E = experts
    with ExitStack() as ctx:
        sb = lambda name, shape, dt=F32: ctx.enter_context(nc.sbuf_tensor(f"{tag}_{name}", shape, dt))
        sem = lambda name: c.sem(f"{tag}_{name}")
        setup_stream_buffers(ctx, nc, c, tag)
        xn = c.xn
        if rwkv_out:
            yn = [sb(f"yn{s}", [P, KH, CH]) for s in S2]
        else:
            oT = [sb(f"oT{s}", [P, 4, CH]) for s in S2]
        ident = sb("ident", [GT, GT], BF16)
        r = Routing(sb, sem, E)
        ny, nx = c.norm(f"{tag}_ynorm"), c.norm(f"{tag}_xnorm")
        y_affine, wo_mm, h_added = sem("y_affine"), sem("wo_mm"), sem("h_added")
        oT2_out, oT2_done = sem("oT2_out"), sem("oT2_done")
        rms_done, rms_steps, o_normed, o_normed_pool, oT_out, oT_done = (
            sem("rms_done"), sem("rms_steps"), sem("o_normed"), sem("o_normed_pool"), sem("oT_out"), sem("oT_done"))

        def over_rms(eng, s, signal):
            pairs = slice(s * CHUNK_PAIRS, (s + 1) * CHUNK_PAIRS)
            by_head = c.o_tok[:, pairs, :].rearrange("p a (h d) -> p (a h) d", d=64)
            rec = c.o_ms[:, pairs, :].rearrange("p a h -> p (a h)")
            eng.tensor_tensor(by_head, by_head, rec.unsqueeze(2).to_broadcast([GT, CHUNK_PAIRS * HEADS, 64]),
                              ALU.mult).then_inc(signal, 1)

        hi_done, lo_done = sem("hi_done"), sem("lo_done")
        logits_ready, exp_in, exp_out, turned, rows_done = (
            sem("logits_ready"), sem("exp_in"), sem("exp_out"), sem("turned"), sem("rows_done"))
        init = sem("init")
        router = c.router0 if top == 2 else c.router1
        exps = 2 if top == 2 else 1
        NX_LAG = 4 if rwkv_out else 3
        HT = TILES // 2
        turned_rows = [c.ps[1 + half][0:3 * EROWS, 1, :].bitcast(BF16)[:, 0:HT * GT] for half in range(2)]

        with nc.Block() as block:
            @block.sync
            def _(sp):
                sp.dma_start(ident[:, :], c.dram["ident"][0:GT, 0:GT]).then_inc(c.ident_loaded, 16)
                if next_weights is not None:
                    load_first_units_sp(sp, c, next_weights)

            @block.tensor
            def _(pe):
                pe.wait_ge(c.ident_loaded, 16 * (1 if rwkv_out else 2))
                pe.wait_ge(c.late_loaded, c.late_count[tag] * 16)
                n = [s + 1 for s in S2]
                at = [slice(s * CH, (s + 1) * CH) for s in S2]
                def y_of(s):
                    return [c.y[:, k, at[s]] for k in range(KH)]

                def turn_o(half, s):
                    if half:
                        pe.wait_ge(oT_done, n[s])
                    else:
                        pe.wait_ge(*((o_normed, n[s]) if s < STREAMS - 1 else (o_normed_pool, 1)))
                    for m in range(2):
                        block = 2 * half + m
                        for p in range(CHUNK_PAIRS):
                            last = pe.matmul(c.ps[s][:, m, p * GT:(p + 1) * GT],
                                             c.o_tok[:, s * CHUNK_PAIRS + p, block * P:(block + 1) * P],
                                             c.ident_f[:, :], start=True, stop=True)
                    last.then_inc(oT_out if half == 0 else oT2_out, 1)

                def project(s, weights, source, blocks):
                    for m in range(KH):
                        for k in range(blocks):
                            last = pe.matmul(c.ps[s][:, m, 0:CH], weights[:, k, m * P:(m + 1) * P], source[s][:, k, :],
                                             start=(k == 0), stop=(k == blocks - 1))
                    last.then_inc(wo_mm, 1)

                def project_y(s):
                    pe.wait_ge(y_affine, n[s])
                    project(s, c.w_o, yn, KH)

                def project_o(s):
                    pe.wait_ge(oT2_done, n[s])
                    project(s, c.w_out, oT, 4)

                def residual_of(s):
                    pe.wait_ge(h_added, n[s])
                    return [c.h[:, k, at[s]] for k in range(KH)]

                def logits(s):
                    pe.wait_ge(nx.normed, n[s])
                    for t in range(CH // GT):
                        for k in range(KH):
                            last = pe.matmul(c.ps[0][0:GT, 1, (s * (CH // GT) + t) * E:(s * (CH // GT) + t + 1) * E],
                                             xn[s][:, k, t * GT:(t + 1) * GT], router[:, k, :],
                                             start=(k == 0), stop=(k == KH - 1))
                    last.then_inc(logits_ready, 1)

                if rwkv_out:
                    in_turn(norm_stages_pe(pe, c, ny, 0, y_of))
                    mixing = [(3, project_y)]
                else:
                    mixing = [(0, lambda s: turn_o(0, s)), (1, lambda s: turn_o(1, s)), (2, project_o)]
                staggered(mixing + norm_stages_pe(pe, c, nx, NX_LAG, residual_of) + [(NX_LAG + 3, logits)])
                pe.wait_ge(r.parts_ready, 1)
                for t in range(TILES):
                    pe.transpose(turned_rows[t // HT][:, (t % HT) * GT:(t % HT + 1) * GT], r.parts[:, t, :], ident[:, :]) \
                        .then_inc(turned, 1)

            @block.vector
            def _(dve):
                dve.memset(r.take[:, :, :], PAD_LOW).then_inc(init, 1)
                dve.memset(r.p[:, :, :], PAD_LOW).then_inc(init, 1)
                dve.memset(r.q[:, :, :], PAD_LOW).then_inc(init, 1)
                dve.memset(r.parts[:, :, :], 0.0).then_inc(init, 1)
                dve.wait_ge(init, 4)
                dve.memset(r.parts[:, :, EROWS - 2:EROWS], 1.0).then_inc(init, 1)
                dve.wait_ge(init, 5)
                dve.wait_ge(c.late_loaded, c.late_count[tag] * 16)
                n = [s + 1 for s in S2]
                at = [slice(s * CH, (s + 1) * CH) for s in S2]
                def y_of(s):
                    return c.y[:, :, at[s]]

                def affine(s):
                    norm_scale_dve(dve, c, ny, s, n[s], xn[s][:, :, :])
                    dve.wait_ge(ny.normed, n[s])
                    for k in range(KH):
                        last = dve.tensor_scalar(yn[s][:, k, :], xn[s][:, k, :], c.vcol("ln_g", k), c.vcol("ln_b", k),
                                                 ALU.mult, ALU.add)
                    last.then_inc(y_affine, 1)

                def add(s):
                    dve.wait_ge(wo_mm, n[s])
                    hv = c.h[:, :, at[s]]
                    dve.tensor_tensor(hv, c.ps[s][:, :, 0:CH], hv, ALU.add).then_inc(h_added, 1)

                def residual_of(s):
                    dve.wait_ge(h_added, n[s])
                    return c.h[:, :, at[s]]

                if rwkv_out:
                    in_turn(norm_stages_dve(dve, c, ny, 0, y_of, affine))
                    mixing = []
                else:
                    dve.wait_ge(rms_done, 1)
                    dve.tensor_scalar(c.o_ms[:, :, :], c.o_ms[:, :, :], 1e-8, None, ALU.add).then_inc(rms_steps, 1)
                    dve.wait_ge(rms_steps, 1)
                    dve.reciprocal(c.o_ms[:, :, :], c.o_ms[:, :, :]).then_inc(rms_steps, 1)
                    dve.wait_ge(rms_steps, 2)
                    for s in S2[:-1]:
                        over_rms(dve, s, o_normed)
                    mixing = []
                staggered(mixing + [(NX_LAG - 1, add)] +
                          norm_stages_dve(dve, c, nx, NX_LAG, residual_of,
                                          lambda s: norm_scale_dve(dve, c, nx, s, n[s], xn[s][:, :, :])))
                dve.wait_ge(logits_ready, STREAMS)
                gate_weights_dve(dve, (exp_in, exp_out), c, r, E, top,
                                 c.ps[0][0:GT, 1, 0:TILES * E].rearrange("p (t e) -> p t e", e=E))

            @block.scalar
            def _(act):
                n = [s + 1 for s in S2]
                def copy_turned(half, s):
                    act.wait_ge(oT_out if half == 0 else oT2_out, n[s])
                    act.activation(oT[s][:, 2 * half:2 * half + 2, :], c.ps[s][:, :, 0:CH],
                                   ACT.Copy).then_inc(oT_done if half == 0 else oT2_done, 1)

                if rwkv_out:
                    in_turn(norm_stages_act(act, c, ny, 0))
                    mixing = []
                else:
                    act.activation(c.o_ms[:, :, :], c.o_ms[:, :, :], ACT.Sqrt, scale=1.0 / 64).then_inc(rms_done, 1)
                    mixing = [(0, lambda s: copy_turned(0, s)), (1, lambda s: copy_turned(1, s))]
                staggered(mixing + norm_stages_act(act, c, nx, NX_LAG))
                for i in range(exps):
                    act.wait_ge(exp_in, i + 1)
                    act.activation(r.e[:, :, 0:E], r.a[:, :, 0:E], ACT.Exp).then_inc(exp_out, 1)
                for half in range(2):
                    act.wait_ge(turned, (half + 1) * HT)
                    act.activation(c.gates[:, half * HT * GT:(half + 1) * HT * GT], turned_rows[half], ACT.Copy).then_inc(rows_done, 1)
                act.wait_ge(rows_done, 2)

            @block.gpsimd
            def _(pool):
                n = [s + 1 for s in S2]
                at = [slice(s * CH, (s + 1) * CH) for s in S2]
                if not rwkv_out:
                    pool.wait_ge(rms_steps, 2)
                    over_rms(pool, S2[-1], o_normed_pool)
                for s in S2:
                    pool.wait_ge(nx.normed, n[s])
                    pool.tensor_copy(c.hi[:, :, at[s]], xn[s][:, :, :]).then_inc(hi_done, 1)
                    pool.wait_ge(hi_done, n[s])
                    pool.tensor_tensor(c.lo[:, :, at[s]], xn[s][:, :, :],
                                       c.hi[:, :, at[s]].bitcast(F32), ALU.subtract).then_inc(lo_done, 1)



def load_first_units_sp(sp, c, weights):
    width = weights.shape[2]
    for b in range(2):
        sp.dma_start(c.raw[b][:, 0:width], weights[b]).then_inc(c.first_loaded, 16)


def phase_experts(nc, c, tag, units, gated, weights, first_count, after=None, projections=False, store=False):
    UP, DOWN = 4, 2 if gated else 4
    WIDTH = KH * UP * P + DOWN * C
    EXP = 2 if gated else 1
    with ExitStack() as ctx:
        sb = lambda name, shape, dt=F32: ctx.enter_context(nc.sbuf_tensor(f"{tag}_{name}", shape, dt))
        sem = lambda name: c.sem(f"{tag}_{name}")
        raw, pick = c.raw, c.pick
        whi = [sb(f"whi{b}", [P, WIDTH], F32R) for b in range(2)]
        wlo = [sb(f"wlo{b}", [P, WIDTH], F32R) for b in range(2)]
        act_out = [sb(f"act_out{b}", [P, DOWN, E_MAX]) for b in range(2)]
        hid = [sb(f"hid{b}", [P, DOWN, E_MAX]) for b in range(2)]
        hhi = [sb(f"hhi{b}", [P, DOWN, E_MAX], F32R) for b in range(2)]
        hlo = [sb(f"hlo{b}", [P, DOWN, E_MAX], F32R) for b in range(2)]
        pu = [ctx.enter_context(nc.psum_tensor(f"{tag}_pu{j}", [P, 512], F32)) for j in range(UP)]
        pg = [ctx.enter_context(nc.psum_tensor(f"{tag}_pg{j}", [P, 512], F32)) for j in range(2)]
        pd = ctx.enter_context(nc.psum_tensor(f"{tag}_pd", [P, 2, 512], F32))
        loaded = [sem(f"w_loaded{b}") for b in range(2)]
        hi_done, split_done = sem("w_hi"), sem("w_split")
        gate_out, up_out, act_done, weighted, hi_ready, hid_split, down_out, added = (
            sem("gate_out"), sem("up_out"), sem("act_done"), sem("weighted"), sem("hid_hi"), sem("hid_split"),
            sem("down_out"), sem("added"))
        multiplied = sem("multiplied")
        first_hi, first_split = sem("first_hi"), sem("first_split")
        UP_PART, DOWN_PART = slice(0, KH * UP * P), slice(KH * UP * P, WIDTH)
        LOOPS = units // 2 if units % 2 else units // 2 - 1
        acts = UP // 2 if gated else UP

        def whole(eng, body):
            with eng.Fori(0, LOOPS) as it:
                for slot in range(2):
                    body(it * 2 + slot, slot, it, True)
            for i in range(LOOPS * 2, units):
                body(i, i % 2, i // 2, i + 1 < units)

        def chunk_of(b, ch):
            return slice(E_AT[ch], E_AT[ch + 1]), E_AT[ch + 1] - E_AT[ch], (b * E_CHUNKS + ch) % 2

        up_at = lambda t, k, j: t[:, (k * UP + j) * P:(k * UP + j + 1) * P]
        down_at = lambda t, j, m: t[:, KH * UP * P + j * C + m * P:KH * UP * P + j * C + (m + 1) * P]

        with nc.Block() as block:
            @block.sync
            def _(sp):
                if after:
                    after(sp)
                with sp.Fori(0, (units - 2) // 2) as it:
                    for b in range(2):
                        sp.wait_ge(split_done, it * 2 + b + 1)
                        sp.dma_start(raw[b][:, 0:WIDTH], weights[it * 2 + b + 2]).then_inc(loaded[b], 16)
                if units % 2:
                    sp.wait_ge(split_done, units - 2)
                    sp.dma_start(raw[0][:, 0:WIDTH], weights[units - 1]).then_inc(loaded[0], 16)
                if projections:
                    load_projections_sp(sp, c, split_done, units)
                if store:
                    for ch in range(E_CHUNKS):
                        at, w, q = chunk_of(0, ch)
                        sp.wait_ge(added, (units - 1) * E_CHUNKS + ch + 2)
                        sp.dma_start(c.dram["out"][:, :, at].rearrange("k p n -> p k n"), c.h[:, :, at]).then_inc(c.stored, 16)
                    sp.wait_ge(c.stored, 16 * E_CHUNKS)

            @block.gpsimd
            def _(pool):
                def split(i, b):
                    pool.tensor_copy(whi[b][:, :], raw[b][:, 0:WIDTH]).then_inc(hi_done, 1)
                    pool.wait_ge(hi_done, i)
                    pool.tensor_tensor(wlo[b][:, :], raw[b][:, 0:WIDTH], whi[b][:, :].bitcast(F32), ALU.subtract).then_inc(split_done, 1)

                pool.wait_ge(first_split, 2)
                pool.sem_inc(split_done, 1)
                split(1, 1)
                with pool.Fori(0, (units - 2) // 2) as it:
                    for b in range(2):
                        pool.wait_ge(down_out, (it * 2 + b + 1) * E_CHUNKS)
                        wait_alone(c, pool, loaded[b], (it + 1) * 16)
                        split(it * 2 + b + 2, b)
                if units % 2:
                    pool.wait_ge(down_out, (units - 2) * E_CHUNKS)
                    pool.wait_ge(loaded[0], units // 2 * 16)
                    split(units - 1, 0)
                if projections:
                    split_projections_pool(pool, c)

            @block.tensor
            def _(pe):
                def go_up(i, b, pair, ch):
                    v = i * E_CHUNKS + ch
                    at, w, q = chunk_of(b, ch)
                    for j in range(UP):
                        if gated and j % 2:
                            pe.wait_ge(multiplied, v * 2 + j // 2 + 1)
                        else:
                            pe.wait_ge(act_done, v * acts + (j // 2 if gated else j) + 1)
                        n = 0
                        for wt, xt in ((whi, c.hi), (wlo, c.hi), (whi, c.lo)):
                            for k in range(KH):
                                last = pe.matmul(pu[j][:, 0:w], up_at(wt[b], k, j), xt[:, k, at], start=(n == 0), stop=(n == 5))
                                n += 1
                        last.then_inc(up_out, 1)
                    for a in range(EXP):
                        g = a if gated else q
                        pe.wait_ge(weighted, v + (2 if gated else 1))
                        row = pair * 4 + 2 * b + a if gated else pair
                        last = pe.matmul(pg[g][:, 0:w], pick[:, row, :] if isinstance(row, int) else pick[:, bass.ds(row, 1), :].rearrange("r o p -> r (o p)"),
                                         c.gates[:, at], start=True, stop=True)
                    last.then_inc(gate_out, 1)

                def go_down(i, b, ch):
                    at, w, q = chunk_of(b, ch)
                    v = i * E_CHUNKS + ch
                    pe.wait_ge(hid_split, v + 1)
                    pe.wait_ge(added, v + 1)
                    for m in range(KH):
                        n = 0
                        for wt, xt in ((whi, hhi), (wlo, hhi), (whi, hlo)):
                            for j in range(DOWN):
                                last = pe.matmul(pd[:, m, 0:w], down_at(wt[b], j, m), xt[q][:, j, 0:w],
                                                 start=(n == 0), stop=(n == 3 * DOWN - 1))
                                n += 1
                    last.then_inc(down_out, 1)

                pe.wait_ge(first_split, 1)
                go_up(0, 0, 0, 0)
                pe.wait_ge(first_split, 2)

                def body(i, b, pair, more):
                    for ch in range(E_CHUNKS):
                        if ch + 1 < E_CHUNKS:
                            go_up(i, b, pair, ch + 1)
                        elif more:
                            pe.wait_ge(split_done, i + 2)
                            go_up(i + 1, 1 - b, pair + b, 0)
                        go_down(i, b, ch)

                whole(pe, body)

            @block.scalar
            def _(act):
                act.wait_ge(c.first_loaded, first_count)
                for part in (UP_PART, DOWN_PART):
                    act.activation(whi[0][:, part], raw[0][:, part], ACT.Copy).then_inc(first_hi, 1)

                def body(i, b, pair, more):
                    for ch in range(E_CHUNKS):
                        v = i * E_CHUNKS + ch
                        at, w, q = chunk_of(b, ch)
                        o = act_out[q]
                        act.wait_ge(weighted, v + 1)
                        for j in range(acts):
                            bank = 2 * j if gated else j
                            act.wait_ge(up_out, v * UP + bank + 1)
                            act.activation(o[:, j, 0:w], pu[bank][:, 0:w], ACT.Silu).then_inc(act_done, 1)
                        act.wait_ge(weighted, v + 1 + 2)
                        act.activation(hhi[q][:, :, 0:w], hid[q][:, :, 0:w], ACT.Copy).then_inc(hi_ready, 1)

                whole(act, body)

            @block.vector
            def _(dve):
                for i, part in enumerate((UP_PART, DOWN_PART)):
                    dve.wait_ge(first_hi, i + 1)
                    dve.tensor_tensor(wlo[0][:, part], raw[0][:, part], whi[0][:, part].bitcast(F32),
                                      ALU.subtract).then_inc(first_split, 1)
                dve.sem_inc(weighted, 2)
                dve.sem_inc(act_done, acts)
                dve.sem_inc(added, 1)
                if gated:
                    dve.sem_inc(multiplied, 2)

                def weigh(i, b, ch):
                    v = i * E_CHUNKS + ch
                    at, w, q = chunk_of(b, ch)
                    if gated:
                        for a in range(2):
                            dve.wait_ge(act_done, v * acts + a + 1 + acts)
                            dve.wait_ge(up_out, v * UP + 2 * a + 2)
                            dve.tensor_tensor(act_out[q][:, a, 0:w], pu[2 * a + 1][:, 0:w], act_out[q][:, a, 0:w],
                                              ALU.mult).then_inc(multiplied, 1)
                        dve.wait_ge(gate_out, v + 1)
                        for a in range(2):
                            dve.wait_ge(multiplied, v * 2 + a + 1 + 2)
                            last = dve.tensor_tensor(hid[q][:, a, 0:w], pg[a][:, 0:w], act_out[q][:, a, 0:w], ALU.mult)
                        last.then_inc(weighted, 1)
                    else:
                        dve.wait_ge(act_done, v * acts + acts + acts)
                        dve.wait_ge(gate_out, v + 1)
                        dve.tensor_tensor(hid[q][:, :, 0:w], act_out[q][:, :, 0:w], over_halves(pg[q][:, 0:w], DOWN),
                                          ALU.mult).then_inc(weighted, 1)
                    dve.wait_ge(hi_ready, v + 1)
                    dve.tensor_tensor(hlo[q][:, :, 0:w], hid[q][:, :, 0:w], hhi[q][:, :, 0:w].bitcast(F32), ALU.subtract).then_inc(hid_split, 1)

                def add(i, b, ch):
                    at, w, q = chunk_of(b, ch)
                    dve.wait_ge(down_out, i * E_CHUNKS + ch + 1)
                    hv = c.h[:, :, at]
                    dve.tensor_tensor(hv, pd[:, :, 0:w], hv, ALU.add).then_inc(added, 1)

                weigh(0, 0, 0)

                def body(i, b, pair, more):
                    for ch in range(E_CHUNKS):
                        if ch + 1 < E_CHUNKS:
                            weigh(i, b, ch + 1)
                        elif more:
                            weigh(i + 1, 1 - b, 0)
                        add(i, b, ch)

                whole(dve, body)



def load_attention_sp(sp, c):
    d = c.dram
    for dst, src in ((c.w_out[:, :, :], d["w_out"]),
                     (c.pair_ident[:, :], d["pair_ident"]), (c.ident_f[:, :], d["ident_f"]),
                     (c.lam4[:, :, :].rearrange("p a d -> p (a d)"), d["lambdas"].partition_broadcast(P)),
                     (c.gam[0:64, :], d["gamma1"]), (c.gam[64:P, :], d["gamma1"])):
        sp.dma_start(dst, src).then_inc(c.attn_loaded, 16)
    sp.dma_start(c.router1[:, :, :], d["router1"]).then_inc(c.late_loaded, 16)
    sp.dma_start(c.score_bias[:, :], d["score_bias"].partition_broadcast(GT)).then_inc(c.late_loaded, 16)


ATTN_LOADS = 6
QKV_PARTS = (slice(0, 2), slice(2, 3))


def load_projections_sp(sp, c, split_done, units):
    for b, part in enumerate(QKV_PARTS):
        sp.wait_ge(split_done, units - 1 + b)
        width = (part.stop - part.start) * KH * 512
        sp.dma_start(c.raw[b][:, 0:width], c.dram["wqkv"][:, part].rearrange("p a k n -> p (a k n)")).then_inc(c.wqkv_loaded[b], 16)


def split_projections_pool(pool, c):
    for b, part in enumerate(QKV_PARTS):
        hi, lo = (t[:, part].rearrange("p a k n -> p (a k n)") for t in (c.wqkv_hi, c.wqkv_lo))
        raw = c.raw[b][:, 0:(part.stop - part.start) * KH * 512]
        pool.wait_ge(c.wqkv_loaded[b], 16)
        pool.tensor_copy(hi, raw).then_inc(c.wqkv_split, 1)
        pool.wait_ge(c.wqkv_split, 2 * b + 1)
        pool.tensor_tensor(lo, raw, hi.bitcast(F32), ALU.subtract).then_inc(c.wqkv_split, 1)


def phase_qkv(nc, c):
    S2 = range(STREAMS)
    with ExitStack() as ctx:
        sb = lambda name, shape, dt=F32: ctx.enter_context(nc.sbuf_tensor(f"qkv_{name}", shape, dt))
        sem = lambda name: c.sem(f"qkv_{name}")
        setup_stream_buffers(ctx, nc, c, "qkv", c.pair_area)
        xn = c.xn
        lam_t, lam_s = sb("lam_t", [P, 2, HD]), sb("lam_s", [P, 2])
        nm = c.norm("attn_norm")
        GROUPS = 6
        proj_out, evacuated = ([sem(f"{name}{g}") for g in range(GROUPS)] for name in ("proj_out", "evacuated"))
        hi_done, lo_done = sem("hi_done"), sem("lo_done")
        link_sem, lam_ready, lam_exp, zeroed = sem("link"), sem("lam_ready"), sem("lam_exp"), sem("zeroed")
        n = [s + 1 for s in S2]
        at = [slice(s * CH, (s + 1) * CH) for s in S2]

        with nc.Block() as block:
            @block.tensor
            def _(pe):
                pe.wait_ge(c.wqkv_split, 2 * len(QKV_PARTS))
                def project(g, s):
                    if g == 0:
                        pe.wait_ge(lo_done, n[s])
                    else:
                        pe.wait_ge(evacuated[g - 1], n[s])
                    passes = [(wt, xt, k) for wt, xt in ((c.wqkv_hi, c.hi), (c.wqkv_lo, c.hi), (c.wqkv_hi, c.lo)) for k in range(KH)]
                    for half in range(2):
                        for i, (wt, xt, k) in enumerate(passes):
                            start, stop = i == 0, i == len(passes) - 1
                            if g < 4:
                                m = (g % 2) * 2 + half
                                last = pe.matmul(c.ps[s][:, half, 0:CH], wt[:, g // 2, k, m * P:(m + 1) * P],
                                                 xt[:, k, at[s]], start=start, stop=stop)
                            else:
                                first = s * CH + ((g - 4) * 2 + half) * GT
                                last = pe.matmul(c.ps[s][0:GT, half, :], xt[:, k, first:first + GT],
                                                 wt[:, 2, k, :], start=start, stop=stop)
                    last.then_inc(proj_out[g], 1)

                def residual_of(s):
                    return [c.h[:, k, at[s]] for k in range(KH)]

                def stage(g):
                    return lambda s: project(g, s)

                in_turn(norm_stages_pe(pe, c, nm, 0, residual_of) + [(3 + g, stage(g)) for g in range(GROUPS)])

            @block.scalar
            def _(act):
                def round_x(s):
                    act.wait_ge(nm.normed, n[s])
                    act.activation(c.hi[:, :, at[s]], xn[s][:, :, :], ACT.Copy).then_inc(hi_done, 1)

                def take(g, s):
                    act.wait_ge(proj_out[g], n[s])
                    if g < 4:
                        dst, src = (c.q, c.k)[g // 2][:, (g % 2) * 2:(g % 2) * 2 + 2, at[s]], c.ps[s][:, :, 0:CH]
                    else:
                        first = s * CHUNK_PAIRS + (g - 4) * 2
                        dst, src = c.v[:, first:first + 2, :], c.ps[s][0:GT, :, :]
                    act.activation(dst, src, ACT.Copy).then_inc(evacuated[g], 1)

                def stage(g):
                    return lambda s: take(g, s)

                in_turn(norm_stages_act(act, c, nm, 0) + [(2, round_x)] + [(3 + g, stage(g)) for g in range(GROUPS)])
                act.wait_ge(lam_ready, 1)
                act.activation(lam_s[:, :], lam_s[:, :], ACT.Exp).then_inc(lam_exp, 1)

            @block.vector
            def _(dve):
                def left_of_x(s):
                    dve.wait_ge(hi_done, n[s])
                    dve.tensor_tensor(c.lo[:, :, at[s]], xn[s][:, :, :], c.hi[:, :, at[s]].bitcast(F32),
                                      ALU.subtract).then_inc(lo_done, 1)

                in_turn(norm_stages_dve(dve, c, nm, 0, lambda s: c.h[:, :, at[s]],
                                        lambda s: norm_scale_dve(dve, c, nm, s, n[s], xn[s][:, :, :])) + [(2, left_of_x)])
                dve.wait_ge(c.attn_loaded, ATTN_LOADS * 16)
                link = Link(dve, link_sem)
                link(dve.tensor_tensor(lam_t[:, :, :], c.lam4[:, 0::2, :], c.lam4[:, 1::2, :], ALU.mult))
                dve.tensor_reduce(lam_s[:, :], lam_t[:, :, :], AX.X, ALU.add).then_inc(lam_ready, 1)
                link(dve.tensor_scalar(c.gam[:, :], c.gam[:, :], 1.0 - LAMBDA_INIT, None, ALU.mult))
                link(dve.tensor_scalar(c.w_out[:, :, :], c.w_out[:, :, :], c.gam[:, 0:1], None, ALU.mult))
                dve.wait_ge(lam_exp, 1)
                link(dve.tensor_tensor(c.neg_lam[:, :], lam_s[:, 1:2], lam_s[:, 0:1], ALU.subtract))
                link(dve.tensor_scalar(c.neg_lam[:, :], c.neg_lam[:, :], -LAMBDA_INIT, None, ALU.add))

            @block.gpsimd
            def _(pool):
                for t in c.k_diag + c.q_pad + c.wts:
                    pool.memset(t[:], 0.0).then_inc(zeroed, 1)
                pool.wait_ge(zeroed, 6)


def sweep(eng, stages):
    lags = [lag for lag, stage in stages]
    first = max(lags) + max(lags) % 2
    loops = (PAIRS - first) // 2

    def peeled(steps):
        for t in steps:
            for lag, stage in stages:
                if 0 <= t - lag < PAIRS:
                    stage(t - lag, (t - lag) % 2)

    peeled(range(first))
    with eng.Fori(0, loops) as it:
        for u in range(2):
            for lag, stage in stages:
                stage(it * 2 + (first + u - lag), (u - lag) % 2)
    peeled(range(first + 2 * loops, PAIRS + max(lags)))


def phase_pairs(nc, c):
    COMPS, G = 2 * HEADS, 4
    with ExitStack() as ctx:
        sb = lambda name, shape, dt=F32: ctx.enter_context(nc.sbuf_tensor(f"pr_{name}", shape, dt))
        pb = lambda name, shape: ctx.enter_context(nc.psum_tensor(f"pr_{name}", shape, F32))
        sem = lambda name: c.sem(f"pr_{name}")
        dif, ex = ([sb(f"{name}{b}", [P, COMPS, SEQ]) for b in range(2)] for name in ("dif", "ex"))
        top, den = [sb(f"top{b}", [P, COMPS]) for b in range(2)], [sb(f"den{b}", [P, COMPS]) for b in range(2)]
        wT = [sb(f"wT{b}", [GT, HEADS, GT]) for b in range(2)]
        o_sq = [c.w_o[0:GT, :, :].rearrange("p k n -> p (k n)"), c.gates[0:GT, 0:2 * 512].bitcast(F32)]
        score = [pb(f"score{b}", [P, 2, 512]) for b in range(2)]
        turned_w = pb("turned_w", [GT, 2, 512])
        o_ps = [pb(f"o{b}", [GT, 512]) for b in range(2)]
        k_placed, q_placed, scored, maxed, topped, exp_done = sem("k_placed"), sem("q_placed"), sem("scored"), sem("maxed"), sem("topped"), sem("exp_done")
        den_steps, den_done, scaled, combined = sem("den_steps"), sem("den_done"), sem("scaled"), sem("combined")
        turned, wT_done, o_out, squared, ms_done = sem("turned"), sem("wT_done"), sem("o_out"), sem("squared"), sem("ms_done")
        by_bank = lambda ap: ap.rearrange("p (a c) t -> p a c t", a=2)
        of_pair = lambda x, rows, t: x[rows, :, bass.ds(t * 2 * SEQ, 2 * SEQ)].rearrange("p m (b t) -> p m b t", b=2)

        with nc.Block() as block:
            @block.tensor
            def _(pe):
                def scores(t, b):
                    pe.wait_ge(k_placed, t + 1)
                    pe.wait_ge(q_placed, t + 1)
                    pe.wait_ge(topped, t + 1)
                    for img in range(2):
                        for m in range(G):
                            last = pe.matmul(score[b][QP * img:QP * img + QP, m // 2, (m % 2) * G * SEQ:(m % 2 + 1) * G * SEQ],
                                             c.q_pad[b][:, m, img, :],
                                             c.k_diag[b][:, m, img, :, :].rearrange("p g t -> p (g t)"),
                                             start=True, stop=True, tile_position=(0, QP * img))
                    last.then_inc(scored, 1)

                def turn(t, b):
                    pe.wait_ge(combined, t + 3)
                    pe.wait_ge(wT_done, t + 1)
                    for h in range(HEADS):
                        last = pe.matmul(turned_w[:, h // 4, (h % 4) * GT:(h % 4 + 1) * GT], c.wts[b][:, h, :],
                                         c.pair_ident[:, :], start=True, stop=True)
                    last.then_inc(turned, 1)

                def weigh_v(t, b):
                    pe.wait_ge(wT_done, t + 2)
                    pe.wait_ge(squared, t + 1)
                    for h in range(HEADS):
                        last = pe.matmul(o_ps[b][:, h * 64:(h + 1) * 64], wT[b][:, h, :],
                                         c.v[:, t, h * 64:(h + 1) * 64] if isinstance(t, int) else
                                         c.v[:, bass.ds(t, 1), h * 64:(h + 1) * 64].rearrange("p o d -> p (o d)"),
                                         start=True, stop=True)
                    last.then_inc(o_out, 1)

                sweep(pe, [(1, scores), (4, turn), (5, weigh_v)])

            @block.scalar
            def _(act):
                act.sem_inc(exp_done, 2)
                act.sem_inc(wT_done, 1)
                act.sem_inc(squared, 2)

                def place_q(t, b):
                    wait_alone(c, act, scored, t + 1)
                    act.activation(c.q_pad[b][:, :, :, 0:SEQ], of_pair(c.q, slice(0, P), t), ACT.Copy)
                    rows = slice(P - HD, P)
                    act.activation(c.k_diag[b][rows, :, :, G - 1, :], of_pair(c.k, rows, t), ACT.Copy).then_inc(q_placed, 1)

                def exponentials(t, b):
                    act.wait_ge(topped, t + 3)
                    act.wait_ge(combined, t + 1)
                    act.activation(ex[b][:, :, :], dif[b][:, :, :], ACT.Exp, scale=HD ** -0.5).then_inc(exp_done, 1)

                def copy_turned(t, b):
                    act.wait_ge(turned, t + 3)
                    act.wait_ge(o_out, t + 1)
                    act.activation(wT[b][:, :, :].rearrange("p (a h) t -> p a (h t)", a=2),
                                   turned_w[:, :, 0:4 * GT], ACT.Copy).then_inc(wT_done, 1)

                def copy_o(t, b):
                    act.wait_ge(o_out, t + 3)
                    act.activation(c.o_tok[:, t, :] if isinstance(t, int) else
                                   c.o_tok[:, bass.ds(t, 1), :].rearrange("p o d -> p (o d)"), o_ps[b][:, :], ACT.Copy)
                    act.wait_ge(ms_done, t + 1)
                    act.activation(o_sq[b][:, :], o_ps[b][:, :], ACT.Square).then_inc(squared, 1)

                sweep(act, [(0, place_q), (2, exponentials), (4, copy_turned), (5, copy_o)])

            @block.vector
            def _(dve):
                dve.sem_inc(topped, 2)
                dve.sem_inc(ms_done, 2)

                def place_k(t, b):
                    wait_alone(c, dve, scored, t + 1)
                    for g in range(G - 1):
                        rows = slice(HD * g, HD * g + HD)
                        last = dve.tensor_copy(c.k_diag[b][rows, :, :, g, :], of_pair(c.k, rows, t))
                    last.then_inc(k_placed, 1)

                def less_top(t, b):
                    dve.wait_ge(scored, t + 3)
                    sc = score[b][:, :, 0:2 * G * SEQ].rearrange("p a (c t) -> p a c t", t=SEQ)
                    dve.tensor_reduce(top[b][:, :].rearrange("p (a c) -> p a c", a=2), sc, AX.X, ALU.max).then_inc(maxed, 1)
                    dve.wait_ge(maxed, t + 1)
                    dve.wait_ge(exp_done, t + 1)
                    dve.tensor_tensor(by_bank(dif[b][:, :, :]), sc,
                                      by_bank(top[b][:, :].unsqueeze(2).to_broadcast([P, COMPS, SEQ])), ALU.subtract).then_inc(topped, 1)

                def denominators(t, b):
                    dve.wait_ge(exp_done, t + 3)
                    dve.tensor_reduce(den[b][:, :], ex[b][:, :, :], AX.X, ALU.add).then_inc(den_steps, 1)
                    dve.wait_ge(den_steps, t * 2 + 1)
                    dve.reciprocal(den[b][:, :], den[b][:, :]).then_inc(den_steps, 1)
                    dve.wait_ge(den_steps, t * 2 + 2)
                    dve.tensor_scalar(den[b][:, 1::2], den[b][:, 1::2], c.neg_lam[:, 0:1], None, ALU.mult).then_inc(den_done, 1)

                def mean_squares(t, b):
                    dve.wait_ge(squared, t + 3)
                    dve.tensor_reduce(c.o_ms[:, t, :] if isinstance(t, int) else
                                      c.o_ms[:, bass.ds(t, 1), :].rearrange("p o h -> p (o h)"),
                                      o_sq[b][:, :].rearrange("p (h d) -> p h d", d=64), AX.X, ALU.add).then_inc(ms_done, 1)

                sweep(dve, [(0, place_k), (2, less_top), (3, denominators), (6, mean_squares)])

            @block.gpsimd
            def _(pool):
                pool.sem_inc(scored, 2)
                pool.sem_inc(combined, 2)
                pool.sem_inc(turned, 2)
                pool.sem_inc(o_out, 2)

                def combine(t, b):
                    pool.wait_ge(combined, t + 2)
                    pool.wait_ge(den_done, t + 1)
                    e = ex[b]
                    pool.tensor_tensor(e[:, :, :], e[:, :, :], den[b][:, :].unsqueeze(2).to_broadcast([P, COMPS, SEQ]),
                                       ALU.mult).then_inc(scaled, 1)
                    pool.wait_ge(scaled, t + 1)
                    pool.wait_ge(turned, t + 1)
                    for img in range(2):
                        rows = slice(QP * img, QP * img + QP)
                        last = pool.tensor_tensor(c.wts[b][rows, :, SEQ * img:SEQ * img + SEQ],
                                                  e[rows, 0::2, :], e[rows, 1::2, :], ALU.add)
                    last.then_inc(combined, 1)

                sweep(pool, [(3, combine)])


def tower(nc, dram):
    with ExitStack() as ctx:
        sb = lambda name, shape, dt=F32: ctx.enter_context(nc.sbuf_tensor(name, shape, dt))
        c = Shared()
        c.dram = dram
        c.taken = []

        def sem(name):
            s = nc.alloc_semaphore(name)
            c.taken.append(s)
            return s

        c.sem = sem
        c.norm = lambda name: Norm(c.sem, name)
        c.h = sb("h", [P, KH, TOK])
        c.vec = sb("vec", [P, len(VEC) * KH])
        c.vcol = lambda name, k: c.vec[:, VEC[name] * KH + k:VEC[name] * KH + k + 1]
        c.mean_w = sb("mean_w", [P, P])
        c.eps = sb("eps", [P, 1])
        c.ident_c = sb("ident_c", [GT, GT])
        c.raw = [sb(f"raw{b}", [P, RAW]) for b in range(2)]
        c.pick = sb("pick", [3 * EROWS, EROWS, P], BF16)
        c.hi, c.lo = sb("hi", [P, KH, TOK], F32R), sb("lo", [P, KH, TOK], F32R)
        c.w_o = sb("w_o", [P, KH, C])
        c.router0, c.router1 = sb("router0", [P, KH, 8]), sb("router1", [P, KH, 32])
        c.escale, c.score_bias = sb("escale", [GT, 8]), sb("score_bias", [GT, 32])
        c.gates = sb("gates", [3 * EROWS, TOK], BF16)
        c.late_loaded, c.scan_tables_loaded = c.sem("late_loaded"), c.sem("scan_tables_loaded")
        c.passed = c.sem("passed")
        c.first_loaded = c.sem("first_loaded")
        c.wqkv_loaded, c.wqkv_split = [c.sem(f"wqkv_loaded{b}") for b in range(2)], c.sem("wqkv_split")
        c.ident_loaded, c.stored, c.attn_loaded = c.sem("ident_loaded"), c.sem("stored"), c.sem("attn_loaded")
        c.late_count = {"route0": 3, "route1": 5}
        c.taken = []

        def phase(build, *args, **named):
            build(nc, c, *args, **named)
            nc.clear_and_free_semaphores(c.taken)
            nc.all_engine_barrier()
            c.taken = []

        with ExitStack() as rwkv:
            rb = lambda name, shape, dt=F32: rwkv.enter_context(nc.sbuf_tensor(name, shape, dt))
            c.r, c.k, c.w, c.y = (rb(name, [P, KH, TOK]) for name in ("r", "k", "w", "y"))
            c.red = rb("red", [P, HS, P])
            phase(phase_tokens)
            phase(phase_scan)
            phase(phase_route, "route0", 8, 2, True)
        with ExitStack() as attention:
            ab = lambda name, shape, dt=F32: attention.enter_context(nc.sbuf_tensor(name, shape, dt))
            c.w_out, c.pair_ident, c.ident_f = ab("w_out", [P, 4, C]), ab("pair_ident", [P, GT]), ab("ident_f", [GT, GT])
            c.lam4, c.gam, c.neg_lam = ab("lam4", [P, 4, HD]), ab("gam", [P, 1]), ab("neg_lam", [P, 1])
            c.wqkv_hi, c.wqkv_lo = ab("wqkv_hi", [P, 3, KH, 512], F32R), ab("wqkv_lo", [P, 3, KH, 512], F32R)
            phase(phase_experts, "moe0", 16, False, dram["moe0"], 32, lambda sp: load_attention_sp(sp, c), projections=True)
            c.pair_area, c.o_ms = ab("pair_area", [P, PAIRS * 512]), ab("o_ms", [GT, PAIRS, HEADS])
            c.o_tok = c.pair_area[0:GT, :].rearrange("p (a n) -> p a n", n=512)
            with ExitStack() as heads:
                hb = lambda name, shape: heads.enter_context(nc.sbuf_tensor(f"at_{name}", shape, F32))
                c.q, c.k, c.v = hb("q", [P, 4, TOK]), hb("k", [P, 4, TOK]), hb("v", [GT, PAIRS, 512])
                diag, pad = 4 * 2 * 4 * SEQ, 4 * 2 * QP
                c.k_diag = [c.raw[b][:, 0:diag].rearrange("p (m b g t) -> p m b g t", m=4, b=2, g=4) for b in range(2)]
                c.q_pad = [c.raw[b][:, diag:diag + pad].rearrange("p (m b t) -> p m b t", m=4, b=2) for b in range(2)]
                c.wts = [hb(f"wts{b}", [P, HEADS, GT]) for b in range(2)]
                phase(phase_qkv)
                phase(phase_pairs)
            phase(phase_route, "route1", 32, 6, False, dram["moe1"])
        phase(phase_experts, "moe1", 17, True, dram["moe1"], 64, store=True)


def kernel(**inputs):
    import numpy as np
    import concourse.bacc as bacc
    from concourse.bass_utils import run_bass_kernel_spmd

    nc = bacc.Bacc("TRN2", target_bir_lowering=False, num_devices=1)
    a = {name: np.asarray(x) for name, x in inputs.items()}
    f = np.float32

    def rows(w):
        return w.reshape(-1, P, w.shape[1]).transpose(1, 0, 2)

    put = {}
    x = a["x"].reshape(CHUNKS, CH_IMAGES, 3, 6, 16, 6, 16).transpose(0, 2, 4, 6, 1, 3, 5)
    put["patches"] = x.reshape(CHUNKS, PB, P, CH_IMAGES * PATCHES).transpose(0, 2, 1, 3)
    put["wtok"] = rows(a["L0_tok_W"])
    A0 = "L0_attn_time_"
    vectors = [a["L0_tok_b"], a["L0_tok_cls_token"], a["L0_tok_gamma"], a["L0_tok_beta"], a[A0 + "maa_x"], a[A0 + "maa_w"],
               a[A0 + "maa_k"], a[A0 + "maa_v"], a[A0 + "maa_r"], a[A0 + "decay"], a[A0 + "faaaa"],
               a["L0_attn_ln_g"], a["L0_attn_ln_b"]]
    put["vec"] = np.stack([v.reshape(KH, P) for v in vectors]).transpose(2, 0, 1).reshape(P, -1)
    put["pos"] = rows(a["L0_tok_pos_embedding"][0].T)
    put["mean_w"] = np.full((P, P), 1.0 / C, f)
    put["w_lora"] = rows(a[A0 + "maa_w1"])
    put["w_lora2"] = a[A0 + "maa_w2"].reshape(P, C)
    put["w_rkv"] = np.stack([rows(a["L0_attn_W_" + n]) for n in "rkv"], axis=1)
    put["w_decay"] = rows(a[A0 + "decay_w1"])
    put["w_decay2"] = a[A0 + "decay_w2"]
    put["w_o"] = rows(a["L0_attn_W_o"])
    row = np.arange(P)
    put["head_ones"] = (row[:, None] // HS == row[None, :] // HS).astype(f)
    same = row[:, None, None] // HS == row[None, None, :] // HS
    j = np.arange(HS)[None, :, None]
    put["sel"] = (same & (row[:, None, None] % HS == j)).astype(f)
    put["red"] = (same & (row[None, None, :] % HS == j)).astype(f)
    put["router0"] = rows(a["L0_ffn_router_w"].T)
    put["router1"] = rows(a["L1_ffn_router_weight"].T)
    put["escale"] = a["L0_ffn_expert_scale"].reshape(1, 8)
    put["score_bias"] = a["L1_ffn_e_score_bias"].reshape(1, 32)
    put["ident"] = np.eye(P, dtype=mybir.dt.np(BF16))
    put["ident_c"] = np.eye(GT, dtype=f) * C
    put["ident_f"] = np.eye(GT, dtype=f)
    put["pair_ident"] = np.concatenate([np.eye(QP, SEQ, dtype=f), np.zeros((QP, SEQ), f), np.zeros((QP, SEQ), f),
                                        np.eye(QP, SEQ, dtype=f)]).reshape(2, 2, QP, SEQ).transpose(0, 2, 1, 3).reshape(P, GT)
    part_row = np.arange(3 * EROWS)[:, None] % EROWS
    put["pick_id"] = (part_row == np.arange(EROWS)[None, :]).astype(mybir.dt.np(BF16))
    w1 = a["L0_ffn_w1"].reshape(8, 2, 512, KH, P).transpose(0, 1, 4, 3, 2)
    w2 = a["L0_ffn_w2"].reshape(8, C, 2, 4, P).transpose(0, 2, 4, 3, 1)
    put["moe0"] = np.concatenate([w1.reshape(16, P, -1), w2.reshape(16, P, -1)], axis=2)
    shared = np.stack([a["L1_ffn_shared_gate_w"].reshape(2, P, C), a["L1_ffn_shared_up_w"].reshape(2, P, C)], axis=1)
    up = np.concatenate([a["L1_ffn_gate_up_proj"], shared.reshape(2, 2 * P, C)])
    up = up.reshape(17, 512, KH, P).transpose(0, 3, 2, 1)
    down = np.concatenate([a["L1_ffn_down_proj"], a["L1_ffn_shared_down_w"].reshape(C, 2, P).transpose(1, 0, 2)])
    down = down.reshape(17, 2, C, P).transpose(0, 3, 1, 2)
    put["moe1"] = np.concatenate([up.reshape(17, P, -1), down.reshape(17, P, -1)], axis=2)
    wq, wkv = a["L1_attn_Wq"], a["L1_attn_Wkv"]
    put["wqkv"] = np.stack([rows(wq), rows(wkv[:, :512]), rows(wkv[:, 512:])], axis=1)
    put["w_out"] = rows(a["L1_attn_Wout"])
    put["lambdas"] = np.concatenate([a["L1_attn_lambda_" + n] for n in ("q1", "k1", "q2", "k2")]).reshape(1, 4 * HD)
    put["gamma1"] = a["L1_attn_gamma"].reshape(64, 1)

    arrays = {f"in_{name}": np.ascontiguousarray(v) for name, v in put.items()}
    dram = {name: nc.dram_tensor(f"in_{name}", v.shape, mybir.dt.from_np(v.dtype), kind="ExternalInput").ap()
            for name, v in ((n[3:], v) for n, v in arrays.items())}
    dram["out"] = nc.dram_tensor("out", (KH, P, TOK), F32, kind="ExternalOutput").ap()
    tower(nc, dram)
    out = run_bass_kernel_spmd(nc, [arrays], core_ids=[0]).results[0]["out"]
    return np.ascontiguousarray(out.reshape(C, IMAGES, SEQ).transpose(1, 2, 0))
```
